# Optimizing a Trainium2 kernel written in Bass

```python
import numpy as np
import jax
import jax.numpy as jnp

def _softmax(x, axis=-1):
    return jax.nn.softmax(x, axis=axis)
def _gelu(x):
    return jax.nn.gelu(x, approximate=True)
def _silu(x):
    return jax.nn.silu(x)
def _sigmoid(x):
    return jax.nn.sigmoid(x)
def _layernorm(x, axis=-1, eps=1e-5):
    m = jnp.mean(x, axis=axis, keepdims=True)
    v = jnp.var(x, axis=axis, keepdims=True)
    return (x - m) / jnp.sqrt(v + eps)
def _scatter_add(tgt, idx, src, axis=0):
    return tgt.at[idx].add(src)
def _segment_sum(src, seg, n):
    return jax.ops.segment_sum(src, seg, n)

kernel_name = 'mk_conv_seq_d4_conv_nchw128_9c7b6e'

def setup_inputs(seed: int = 0):
    np.random.seed(seed)
    _w = jnp.asarray
    def _rec_inputs():
        import jax
        import jax.numpy as jnp
        _gk = jax.random.key(seed)
        x = -0.0005207 + 1.001 * jax.random.normal(jax.random.fold_in(_gk, 1), (4, 128, 64, 64), jnp.float32)
        return x
    x = _rec_inputs()
    def _L0_conv_setup():
        import jax, jax.numpy as jnp
        import numpy as np
        B, C, IC, H, W = (4, 128, 64, 64, 64)
        key = jax.random.key(seed)
        ks = jax.random.split(key, 9)
        return {'x': jax.random.normal(ks[0], (B, C, H, W), jnp.float32), 'Wg': jax.random.normal(ks[1], (IC, C), jnp.float32) * 0.05, 'bg': jax.random.normal(ks[2], (IC,), jnp.float32) * 0.05, 'Wt': jax.random.normal(ks[3], (IC, C), jnp.float32) * 0.05, 'bt': jax.random.normal(ks[4], (IC,), jnp.float32) * 0.05, 'Wp': jax.random.normal(ks[5], (IC, C), jnp.float32) * 0.05, 'bp': jax.random.normal(ks[6], (IC,), jnp.float32) * 0.05, 'Ww': jax.random.normal(ks[7], (C, IC), jnp.float32) * 0.05, 'bw': jax.random.normal(ks[8], (C,), jnp.float32) * 0.05}
    _L0_conv_all = _L0_conv_setup()
    _L0_conv_in = {k: v for k, v in _L0_conv_all.items() if k in ('Wg', 'bg', 'Wt', 'bt', 'Wp', 'bp', 'Ww', 'bw', )}
    del _L0_conv_all

    def _L1_conv_setup():
        import jax, jax.numpy as jnp
        import numpy as np
        B, C, H, W = (4, 128, 64, 64)
        HEADS = 4
        HD = C // HEADS
        HIDDEN = 2 * C
        EPS = 1e-05

        def layernorm(x, w, b):
            mu = jnp.mean(x, axis=-1, keepdims=True)
            var = jnp.mean(jnp.square(x - mu), axis=-1, keepdims=True)
            return (x - mu) * jax.lax.rsqrt(var + EPS) * w + b
        key = jax.random.key(seed)
        ks = jax.random.split(key, 8)
        s = 0.02
        return {'x': jax.random.normal(ks[0], (B, C, H, W), dtype=jnp.float32), 'ln1_w': jnp.ones((C,), jnp.float32), 'ln1_b': jnp.zeros((C,), jnp.float32), 'qkv_w': jax.random.normal(ks[1], (3 * C, C), jnp.float32) * s, 'proj_w': jax.random.normal(ks[2], (C, C), jnp.float32) * s, 'proj_b': jnp.zeros((C,), jnp.float32), 'ln2_w': jnp.ones((C,), jnp.float32), 'ln2_b': jnp.zeros((C,), jnp.float32), 'fc1_w': jax.random.normal(ks[3], (HIDDEN, C), jnp.float32) * s, 'fc1_b': jnp.zeros((HIDDEN,), jnp.float32), 'fc2_w': jax.random.normal(ks[4], (C, HIDDEN), jnp.float32) * s, 'fc2_b': jnp.zeros((C,), jnp.float32)}
    _L1_conv_all = _L1_conv_setup()
    _L1_conv_in = {k: v for k, v in _L1_conv_all.items() if k in ('ln1_w', 'ln1_b', 'qkv_w', 'proj_w', 'proj_b', 'ln2_w', 'ln2_b', 'fc1_w', 'fc1_b', 'fc2_w', 'fc2_b', )}
    del _L1_conv_all

    def _L2_conv_setup():
        import jax, jax.numpy as jnp
        import numpy as np
        DIM = 128
        HEADS = 8
        K_RATIO = 0.5
        LAYER_SCALE = 0.1
        EPS = 1e-06

        def _group_norm(x, g, b, groups):
            B, C, H, W = x.shape
            xg = x.reshape(B, groups, -1)
            mu = xg.mean(-1, keepdims=True)
            var = xg.var(-1, keepdims=True)
            xn = ((xg - mu) * jax.lax.rsqrt(var + EPS)).reshape(B, C, H, W)
            return xn * g[:, None, None] + b[:, None, None]

        def _conv1x1(x, w):
            return jnp.einsum('oc,bchw->bohw', w, x)

        def _l2norm(t):
            return t / jnp.maximum(jnp.linalg.norm(t, axis=-1, keepdims=True), 1e-12)

        def _sparse_attn(ll, qkv_w, proj_w, g, b):
            B, C, H, W = ll.shape
            N = H * W
            nh = HEADS
            hd = C // nh
            scale = hd ** (-0.5)
            qkv = _conv1x1(ll, qkv_w).reshape(B, 3, nh, hd, N)
            q = jnp.swapaxes(qkv[:, 0], -1, -2)
            k = jnp.swapaxes(qkv[:, 1], -1, -2)
            v = jnp.swapaxes(qkv[:, 2], -1, -2)
            q = _l2norm(q)
            k = _l2norm(k)
            attn = jnp.einsum('bhnd,bhmd->bhnm', q, k) * scale
            attn = jnp.clip(attn, -32.0, 32.0)
            k_num = max(int(N * K_RATIO), 1)
            if k_num < N:
                _, idx = jax.lax.top_k(attn, k_num)
                flat_attn = attn.reshape(-1, N)
                rows = jnp.arange(flat_attn.shape[0])[:, None]
                mask = jnp.zeros(flat_attn.shape, dtype=bool).at[rows, idx.reshape(-1, k_num)].set(True)
                attn = jnp.where(mask.reshape(attn.shape), attn, jnp.float32(-1000000000.0))
            attn = jax.nn.softmax(attn, axis=-1)
            out = jnp.einsum('bhnm,bhmd->bhnd', attn, v)
            out = jnp.swapaxes(out, 2, 3).reshape(B, C, H, W)
            out = _conv1x1(out, proj_w)
            return _group_norm(out, g, b, min(32, C // 4))

        def _high_enhance(h, dw_w, g1, b1, pw_w, g2, b2, alpha):
            C = h.shape[1]
            groups = min(32, C // 8)
            y = jax.lax.conv_general_dilated(h, dw_w, window_strides=(1, 1), padding='SAME', feature_group_count=C, dimension_numbers=('NCHW', 'OIHW', 'NCHW'))
            y = jax.nn.silu(_group_norm(y, g1, b1, groups))
            y = _group_norm(_conv1x1(y, pw_w), g2, b2, groups)
            return h + alpha[0] * y

        def _iwt(ll, lh, hl, hh):
            a = ll - lh - hl + hh
            bq = ll - lh + hl - hh
            c = ll + lh - hl - hh
            d = ll + lh + hl + hh
            B, C, H, W = ll.shape
            row_even = jnp.stack([a, c], axis=-1)
            row_odd = jnp.stack([bq, d], axis=-1)
            h = jnp.stack([row_even, row_odd], axis=3)
            return h.reshape(B, C, 2 * H, 2 * W)

        def _ffn(x, w1, g1, b1, w2, g2, b2):
            d = x.shape[1]
            groups = min(32, d // 4)
            y = _group_norm(_conv1x1(x, w1), g1, b1, groups)
            y = jax.nn.gelu(y, approximate=False)
            return _group_norm(_conv1x1(y, w2), g2, b2, groups)
        key = jax.random.key(seed)
        ks = jax.random.split(key, 18)
        d = DIM
        hd3 = d * 3
        f = lambda k, shape, s=0.05: jax.random.normal(k, shape, dtype=jnp.float32) * s
        return {'x': jax.random.normal(ks[0], (8, d, 64, 64), dtype=jnp.float32), 'qkv_w': f(ks[1], (3 * d, d)), 'proj_w': f(ks[2], (d, d)), 'attn_gn_g': 1.0 + f(ks[3], (d,)), 'attn_gn_b': f(ks[4], (d,)), 'he_dw_w': f(ks[5], (hd3, 1, 3, 3)), 'he_gn1_g': 1.0 + f(ks[6], (hd3,)), 'he_gn1_b': f(ks[7], (hd3,)), 'he_pw_w': f(ks[8], (hd3, hd3)), 'he_gn2_g': 1.0 + f(ks[9], (hd3,)), 'he_gn2_b': f(ks[10], (hd3,)), 'alpha': jnp.array([0.1], dtype=jnp.float32), 'ffn_w1': f(ks[11], (2 * d, d)), 'ffn_gn1_g': 1.0 + f(ks[12], (2 * d,)), 'ffn_gn1_b': f(ks[13], (2 * d,)), 'ffn_w2': f(ks[14], (d, 2 * d)), 'ffn_gn2_g': 1.0 + f(ks[15], (d,)), 'ffn_gn2_b': f(ks[16], (d,))}
    _L2_conv_all = _L2_conv_setup()
    _L2_conv_in = {k: v for k, v in _L2_conv_all.items() if k in ('qkv_w', 'proj_w', 'attn_gn_g', 'attn_gn_b', 'he_dw_w', 'he_gn1_g', 'he_gn1_b', 'he_pw_w', 'he_gn2_g', 'he_gn2_b', 'alpha', 'ffn_w1', 'ffn_gn1_g', 'ffn_gn1_b', 'ffn_w2', 'ffn_gn2_g', 'ffn_gn2_b', )}
    del _L2_conv_all

    def _L3_conv_setup():
        import jax, jax.numpy as jnp
        from jax import lax
        import numpy as np
        DIM = 128
        HID = 64
        C2 = 2 * HID
        P = 8
        key = jax.random.key(seed)
        ks = jax.random.split(key, 8)
        x = jax.random.normal(ks[0], (4, DIM, 256, 256), dtype=jnp.float32)
        w_in = jax.random.normal(ks[1], (C2, DIM), dtype=jnp.float32) * 0.02
        b_in = jax.random.normal(ks[2], (C2,), dtype=jnp.float32) * 0.02
        w_dw = jax.random.normal(ks[3], (C2, 1, 3, 3), dtype=jnp.float32) * 0.02
        b_dw = jax.random.normal(ks[4], (C2,), dtype=jnp.float32) * 0.02
        fft_filter = jnp.ones((C2, 1, 1, P, P // 2 + 1), dtype=jnp.float32)
        w_out = jax.random.normal(ks[5], (DIM, HID), dtype=jnp.float32) * 0.02
        b_out = jax.random.normal(ks[6], (DIM,), dtype=jnp.float32) * 0.02
        return {'x': x, 'w_in': w_in, 'b_in': b_in, 'w_dw': w_dw, 'b_dw': b_dw, 'fft_filter': fft_filter, 'w_out': w_out, 'b_out': b_out}
    _L3_conv_all = _L3_conv_setup()
    _L3_conv_in = {k: v for k, v in _L3_conv_all.items() if k in ('w_in', 'b_in', 'w_dw', 'b_dw', 'fft_filter', 'w_out', 'b_out', )}
    del _L3_conv_all

    return {
        "x": x,
        "L0_conv_Wg": _L0_conv_in["Wg"],
        "L0_conv_bg": _L0_conv_in["bg"],
        "L0_conv_Wt": _L0_conv_in["Wt"],
        "L0_conv_bt": _L0_conv_in["bt"],
        "L0_conv_Wp": _L0_conv_in["Wp"],
        "L0_conv_bp": _L0_conv_in["bp"],
        "L0_conv_Ww": _L0_conv_in["Ww"],
        "L0_conv_bw": _L0_conv_in["bw"],
        "L1_conv_ln1_w": _L1_conv_in["ln1_w"],
        "L1_conv_ln1_b": _L1_conv_in["ln1_b"],
        "L1_conv_qkv_w": _L1_conv_in["qkv_w"],
        "L1_conv_proj_w": _L1_conv_in["proj_w"],
        "L1_conv_proj_b": _L1_conv_in["proj_b"],
        "L1_conv_ln2_w": _L1_conv_in["ln2_w"],
        "L1_conv_ln2_b": _L1_conv_in["ln2_b"],
        "L1_conv_fc1_w": _L1_conv_in["fc1_w"],
        "L1_conv_fc1_b": _L1_conv_in["fc1_b"],
        "L1_conv_fc2_w": _L1_conv_in["fc2_w"],
        "L1_conv_fc2_b": _L1_conv_in["fc2_b"],
        "L2_conv_qkv_w": _L2_conv_in["qkv_w"],
        "L2_conv_proj_w": _L2_conv_in["proj_w"],
        "L2_conv_attn_gn_g": _L2_conv_in["attn_gn_g"],
        "L2_conv_attn_gn_b": _L2_conv_in["attn_gn_b"],
        "L2_conv_he_dw_w": _L2_conv_in["he_dw_w"],
        "L2_conv_he_gn1_g": _L2_conv_in["he_gn1_g"],
        "L2_conv_he_gn1_b": _L2_conv_in["he_gn1_b"],
        "L2_conv_he_pw_w": _L2_conv_in["he_pw_w"],
        "L2_conv_he_gn2_g": _L2_conv_in["he_gn2_g"],
        "L2_conv_he_gn2_b": _L2_conv_in["he_gn2_b"],
        "L2_conv_alpha": _L2_conv_in["alpha"],
        "L2_conv_ffn_w1": _L2_conv_in["ffn_w1"],
        "L2_conv_ffn_gn1_g": _L2_conv_in["ffn_gn1_g"],
        "L2_conv_ffn_gn1_b": _L2_conv_in["ffn_gn1_b"],
        "L2_conv_ffn_w2": _L2_conv_in["ffn_w2"],
        "L2_conv_ffn_gn2_g": _L2_conv_in["ffn_gn2_g"],
        "L2_conv_ffn_gn2_b": _L2_conv_in["ffn_gn2_b"],
        "L3_conv_w_in": _L3_conv_in["w_in"],
        "L3_conv_b_in": _L3_conv_in["b_in"],
        "L3_conv_w_dw": _L3_conv_in["w_dw"],
        "L3_conv_b_dw": _L3_conv_in["b_dw"],
        "L3_conv_fft_filter": _L3_conv_in["fft_filter"],
        "L3_conv_w_out": _L3_conv_in["w_out"],
        "L3_conv_b_out": _L3_conv_in["b_out"],
    }

def reference(x, L0_conv_Wg, L0_conv_bg, L0_conv_Wt, L0_conv_bt, L0_conv_Wp, L0_conv_bp, L0_conv_Ww, L0_conv_bw, L1_conv_ln1_w, L1_conv_ln1_b, L1_conv_qkv_w, L1_conv_proj_w, L1_conv_proj_b, L1_conv_ln2_w, L1_conv_ln2_b, L1_conv_fc1_w, L1_conv_fc1_b, L1_conv_fc2_w, L1_conv_fc2_b, L2_conv_qkv_w, L2_conv_proj_w, L2_conv_attn_gn_g, L2_conv_attn_gn_b, L2_conv_he_dw_w, L2_conv_he_gn1_g, L2_conv_he_gn1_b, L2_conv_he_pw_w, L2_conv_he_gn2_g, L2_conv_he_gn2_b, L2_conv_alpha, L2_conv_ffn_w1, L2_conv_ffn_gn1_g, L2_conv_ffn_gn1_b, L2_conv_ffn_w2, L2_conv_ffn_gn2_g, L2_conv_ffn_gn2_b, L3_conv_w_in, L3_conv_b_in, L3_conv_w_dw, L3_conv_b_dw, L3_conv_fft_filter, L3_conv_w_out, L3_conv_b_out):
    import jax
    import jax.numpy as jnp
    def _L0_conv_ref(x, Wg, bg, Wt, bt, Wp, bp, Ww, bw):
        import jax, jax.numpy as jnp
        import numpy as np
        B, C, IC, H, W = (4, 128, 64, 64, 64)
        b, c, h, w = x.shape
        n = h * w
        xf = x.reshape(b, c, n)
        g = jnp.einsum('oc,bcn->bon', Wg, xf) + bg[:, None]
        theta = jnp.einsum('oc,bcn->bon', Wt, xf) + bt[:, None]
        phi = jnp.einsum('oc,bcn->bon', Wp, xf) + bp[:, None]
        f = jnp.einsum('bcn,bcm->bnm', theta, phi)
        a = jax.nn.softmax(f, axis=-1)
        y = jnp.einsum('bnm,bom->bon', a, g)
        out = jnp.einsum('co,bon->bcn', Ww, y) + bw[:, None]
        return x + out.reshape(b, c, h, w)

    def _L1_conv_ref(x, ln1_w, ln1_b, qkv_w, proj_w, proj_b, ln2_w, ln2_b, fc1_w, fc1_b, fc2_w, fc2_b):
        import jax, jax.numpy as jnp
        import numpy as np
        B, C, H, W = (4, 128, 64, 64)
        HEADS = 4
        HD = C // HEADS
        HIDDEN = 2 * C
        EPS = 1e-05

        def layernorm(x, w, b):
            mu = jnp.mean(x, axis=-1, keepdims=True)
            var = jnp.mean(jnp.square(x - mu), axis=-1, keepdims=True)
            return (x - mu) * jax.lax.rsqrt(var + EPS) * w + b
        b, c, h, w = x.shape
        n = h * w
        x_ln = layernorm(jnp.transpose(x, (0, 2, 3, 1)), ln1_w, ln1_b)
        qkv = jnp.einsum('bhwc,oc->bohw', x_ln, qkv_w)
        q, k, v = jnp.split(qkv, 3, axis=1)
        q = q.reshape(b, HEADS, HD, n)
        k = k.reshape(b, HEADS, HD, n)
        v = v.reshape(b, HEADS, HD, n)
        scale = 1.0 / jnp.sqrt(jnp.float32(HD))
        scores = jnp.einsum('bhdn,bhdm->bhnm', q, k) * scale
        attn = jax.nn.softmax(scores, axis=-1)
        out = jnp.einsum('bhnm,bhdm->bhdn', attn, v)
        out = out.reshape(b, c, h, w)
        out = jnp.einsum('bchw,oc->bohw', out, proj_w) + proj_b[None, :, None, None]
        x = x + out
        x_ln2 = layernorm(jnp.transpose(x, (0, 2, 3, 1)), ln2_w, ln2_b)
        x_flat = x_ln2.reshape(b, n, c)
        hdn = jax.nn.gelu(jnp.einsum('bnc,oc->bno', x_flat, fc1_w) + fc1_b, approximate=False)
        x_mlp = jnp.einsum('bno,co->bnc', hdn, fc2_w) + fc2_b
        x_mlp = jnp.transpose(x_mlp.reshape(b, h, w, c), (0, 3, 1, 2))
        return x + x_mlp

    def _L2_conv_ref(x, qkv_w, proj_w, attn_gn_g, attn_gn_b, he_dw_w, he_gn1_g, he_gn1_b, he_pw_w, he_gn2_g, he_gn2_b, alpha, ffn_w1, ffn_gn1_g, ffn_gn1_b, ffn_w2, ffn_gn2_g, ffn_gn2_b):
        import jax, jax.numpy as jnp
        import numpy as np
        DIM = 128
        HEADS = 8
        K_RATIO = 0.5
        LAYER_SCALE = 0.1
        EPS = 1e-06

        def _group_norm(x, g, b, groups):
            B, C, H, W = x.shape
            xg = x.reshape(B, groups, -1)
            mu = xg.mean(-1, keepdims=True)
            var = xg.var(-1, keepdims=True)
            xn = ((xg - mu) * jax.lax.rsqrt(var + EPS)).reshape(B, C, H, W)
            return xn * g[:, None, None] + b[:, None, None]

        def _conv1x1(x, w):
            return jnp.einsum('oc,bchw->bohw', w, x)

        def _l2norm(t):
            return t / jnp.maximum(jnp.linalg.norm(t, axis=-1, keepdims=True), 1e-12)

        def _sparse_attn(ll, qkv_w, proj_w, g, b):
            B, C, H, W = ll.shape
            N = H * W
            nh = HEADS
            hd = C // nh
            scale = hd ** (-0.5)
            qkv = _conv1x1(ll, qkv_w).reshape(B, 3, nh, hd, N)
            q = jnp.swapaxes(qkv[:, 0], -1, -2)
            k = jnp.swapaxes(qkv[:, 1], -1, -2)
            v = jnp.swapaxes(qkv[:, 2], -1, -2)
            q = _l2norm(q)
            k = _l2norm(k)
            attn = jnp.einsum('bhnd,bhmd->bhnm', q, k) * scale
            attn = jnp.clip(attn, -32.0, 32.0)
            k_num = max(int(N * K_RATIO), 1)
            if k_num < N:
                _, idx = jax.lax.top_k(attn, k_num)
                flat_attn = attn.reshape(-1, N)
                rows = jnp.arange(flat_attn.shape[0])[:, None]
                mask = jnp.zeros(flat_attn.shape, dtype=bool).at[rows, idx.reshape(-1, k_num)].set(True)
                attn = jnp.where(mask.reshape(attn.shape), attn, jnp.float32(-1000000000.0))
            attn = jax.nn.softmax(attn, axis=-1)
            out = jnp.einsum('bhnm,bhmd->bhnd', attn, v)
            out = jnp.swapaxes(out, 2, 3).reshape(B, C, H, W)
            out = _conv1x1(out, proj_w)
            return _group_norm(out, g, b, min(32, C // 4))

        def _high_enhance(h, dw_w, g1, b1, pw_w, g2, b2, alpha):
            C = h.shape[1]
            groups = min(32, C // 8)
            y = jax.lax.conv_general_dilated(h, dw_w, window_strides=(1, 1), padding='SAME', feature_group_count=C, dimension_numbers=('NCHW', 'OIHW', 'NCHW'))
            y = jax.nn.silu(_group_norm(y, g1, b1, groups))
            y = _group_norm(_conv1x1(y, pw_w), g2, b2, groups)
            return h + alpha[0] * y

        def _iwt(ll, lh, hl, hh):
            a = ll - lh - hl + hh
            bq = ll - lh + hl - hh
            c = ll + lh - hl - hh
            d = ll + lh + hl + hh
            B, C, H, W = ll.shape
            row_even = jnp.stack([a, c], axis=-1)
            row_odd = jnp.stack([bq, d], axis=-1)
            h = jnp.stack([row_even, row_odd], axis=3)
            return h.reshape(B, C, 2 * H, 2 * W)

        def _ffn(x, w1, g1, b1, w2, g2, b2):
            d = x.shape[1]
            groups = min(32, d // 4)
            y = _group_norm(_conv1x1(x, w1), g1, b1, groups)
            y = jax.nn.gelu(y, approximate=False)
            return _group_norm(_conv1x1(y, w2), g2, b2, groups)
        x1 = x[:, :, 0::2, 0::2]
        x2 = x[:, :, 1::2, 0::2]
        x3 = x[:, :, 0::2, 1::2]
        x4 = x[:, :, 1::2, 1::2]
        ll = (x1 + x2 + x3 + x4) * 0.5
        lh = (-x1 - x2 + x3 + x4) * 0.5
        hl = (-x1 + x2 - x3 + x4) * 0.5
        hh = (x1 - x2 - x3 + x4) * 0.5
        high = jnp.concatenate([lh, hl, hh], axis=1)
        ll_out = _sparse_attn(ll, qkv_w, proj_w, attn_gn_g, attn_gn_b)
        high_out = _high_enhance(high, he_dw_w, he_gn1_g, he_gn1_b, he_pw_w, he_gn2_g, he_gn2_b, alpha)
        C = ll.shape[1]
        x_rec = _iwt(ll + ll_out, high_out[:, :C], high_out[:, C:2 * C], high_out[:, 2 * C:])
        out = x + LAYER_SCALE * x_rec
        out = out + LAYER_SCALE * _ffn(out, ffn_w1, ffn_gn1_g, ffn_gn1_b, ffn_w2, ffn_gn2_g, ffn_gn2_b)
        return out

    def _L3_conv_ref(x, w_in, b_in, w_dw, b_dw, fft_filter, w_out, b_out):
        import jax, jax.numpy as jnp
        from jax import lax
        import numpy as np
        DIM = 128
        HID = 64
        C2 = 2 * HID
        P = 8
        b, c, H, W = x.shape
        h = jnp.einsum('bchw,oc->bohw', x, w_in) + b_in[None, :, None, None]
        hp = h.reshape(b, C2, H // P, P, W // P, P).transpose(0, 1, 2, 4, 3, 5)
        f = jnp.fft.rfft2(hp)
        f = f * fft_filter
        hp = jnp.fft.irfft2(f, s=(P, P))
        h = hp.transpose(0, 1, 2, 4, 3, 5).reshape(b, C2, H, W)
        hd = lax.conv_general_dilated(h, w_dw, window_strides=(1, 1), padding='SAME', feature_group_count=C2, dimension_numbers=('NCHW', 'OIHW', 'NCHW'))
        hd = hd + b_dw[None, :, None, None]
        x1, x2 = jnp.split(hd, 2, axis=1)
        g = jax.nn.gelu(x1, approximate=False) * x2
        out = jnp.einsum('bchw,oc->bohw', g, w_out) + b_out[None, :, None, None]
        return out + x

    def _gn(v, G=32, eps=1e-5):
        B_, C_, H_, W_ = v.shape
        g = v.reshape(B_, G, C_ // G, H_, W_)
        m = jnp.mean(g, axis=(2, 3, 4), keepdims=True)
        s = jnp.var(g, axis=(2, 3, 4), keepdims=True)
        return ((g - m) / jnp.sqrt(s + eps)).reshape(v.shape)

    def _ln_c(v, eps=1e-6):
        m = jnp.mean(v, axis=1, keepdims=True)
        s = jnp.var(v, axis=1, keepdims=True)
        return (v - m) / jnp.sqrt(s + eps)

    def _ln_t(v, eps=1e-5):
        m = jnp.mean(v, axis=-1, keepdims=True)
        s = jnp.var(v, axis=-1, keepdims=True)
        return (v - m) / jnp.sqrt(s + eps)

    def _to_tokens(v):
        B_, C_, H_, W_ = v.shape
        return v.reshape(B_, C_, H_ * W_).transpose(0, 2, 1)
    def _from_tokens(t, like):
        B_, C_, H_, W_ = like.shape
        return t.transpose(0, 2, 1).reshape(B_, C_, H_, W_)

    x = _L0_conv_ref(x, L0_conv_Wg, L0_conv_bg, L0_conv_Wt, L0_conv_bt, L0_conv_Wp, L0_conv_bp, L0_conv_Ww, L0_conv_bw)
    x = _L1_conv_ref(x, L1_conv_ln1_w, L1_conv_ln1_b, L1_conv_qkv_w, L1_conv_proj_w, L1_conv_proj_b, L1_conv_ln2_w, L1_conv_ln2_b, L1_conv_fc1_w, L1_conv_fc1_b, L1_conv_fc2_w, L1_conv_fc2_b)
    x = _L2_conv_ref(x, L2_conv_qkv_w, L2_conv_proj_w, L2_conv_attn_gn_g, L2_conv_attn_gn_b, L2_conv_he_dw_w, L2_conv_he_gn1_g, L2_conv_he_gn1_b, L2_conv_he_pw_w, L2_conv_he_gn2_g, L2_conv_he_gn2_b, L2_conv_alpha, L2_conv_ffn_w1, L2_conv_ffn_gn1_g, L2_conv_ffn_gn1_b, L2_conv_ffn_w2, L2_conv_ffn_gn2_g, L2_conv_ffn_gn2_b)
    x = _L3_conv_ref(x, L3_conv_w_in, L3_conv_b_in, L3_conv_w_dw, L3_conv_b_dw, L3_conv_fft_filter, L3_conv_w_out, L3_conv_b_out)
    return x


_drawn_inputs = setup_inputs


def setup_inputs(seed=0):
    import zlib

    import numpy as np

    out = dict(_drawn_inputs(seed))
    spreads = {'L1_conv_ln1_w': (1.0, 0.6),
     'L1_conv_ln1_b': (0.0, 0.8),
     'L1_conv_proj_b': (0.0, 0.365),
     'L1_conv_ln2_w': (1.0, 0.6),
     'L1_conv_ln2_b': (0.0, 2.0),
     'L1_conv_fc1_b': (0.0, 2.0),
     'L1_conv_fc2_b': (0.0, 0.357),
     'L3_conv_fft_filter': (1.0, 0.6)}
    factors = {'L0_conv_bt': 5.945,
     'L0_conv_bp': 200.0,
     'L1_conv_qkv_w': 8.0,
     'L1_conv_proj_w': 7.125,
     'L2_conv_attn_gn_g': 34.91,
     'L2_conv_attn_gn_b': 40.993,
     'L2_conv_he_dw_w': 4.308,
     'L2_conv_he_gn1_g': 200.0,
     'L2_conv_he_gn1_b': 200.0,
     'L2_conv_he_pw_w': 3.973,
     'L2_conv_he_gn2_g': 200.0,
     'L2_conv_he_gn2_b': 200.0,
     'L2_conv_ffn_gn1_g': 37.861,
     'L2_conv_ffn_gn1_b': 41.077,
     'L2_conv_ffn_gn2_g': 36.692,
     'L2_conv_ffn_gn2_b': 64.0,
     'L3_conv_w_in': 8.0,
     'L3_conv_b_in': 27.514,
     'L3_conv_w_dw': 8.0,
     'L3_conv_b_dw': 8.0,
     'L3_conv_w_out': 8.0,
     'L3_conv_b_out': 133.116,
     'L1_conv_fc1_w': 3.025}
    for name, (base, spread) in spreads.items():
        noise = np.random.default_rng([zlib.crc32(name.encode()), seed]).standard_normal(out[name].shape)
        drawn = base * np.exp(spread * noise) if base else spread * noise
        out[name] = jnp.asarray(drawn.astype(out[name].dtype))
    for name, factor in factors.items():
        out[name] = (out[name] * factor).astype(out[name].dtype)
    return out
```

```python
import concourse.bass as bass
from concourse import mybir
from contextlib import ExitStack
import numpy as np

FP32 = mybir.dt.float32
FP16 = mybir.dt.float16
ALU = mybir.AluOpType
ACT = mybir.ActivationFunctionType
AX = mybir.AxisListType

B, C, SIDE = 4, 128, 64
N = SIDE * SIDE
CH = 512
NCH = N // CH
BLK = 128
NBLK = N // BLK
IC = 64
H1, D1 = 4, 32
H2, D2 = 8, 16
N2 = 1024
S2 = 32
KEEP = N2 // 2
SLOT = 32

WCOLS, CCOLS = {}, {}


def _columns(table, spec):
    at = 0
    for name, n in spec:
        table[name] = (at, n)
        at += n
    return at


W_TOTAL = _columns(WCOLS, [
    ("wt2", 128), ("wp2", 128), ("wg", IC), ("ww", C), ("bt2", 1), ("bp2", 1), ("bg", IC), ("bw", 1),
    ("ln1w", 1), ("ln1b", 1), ("wq", H1 * 96), ("wk", H1 * 96), ("wv", C), ("proj", C), ("projb", 1),
    ("ln2w", 1), ("ln2b", 1), ("fc1", 256), ("fc1b", 2), ("fc2", 256), ("fc2b", 1),
    ("q2", 3 * C), ("proj2", 256), ("agn_g", 1), ("agn_b", 1), ("he_dw", 27), ("he1_g", 3), ("he1_b", 3),
    ("he_pw", 3 * 384), ("he2_g", 3), ("he2_b", 3), ("alpha", 1), ("f1", 256), ("f1_g", 2), ("f1_b", 2),
    ("f2", 256), ("f2_g", 1), ("f2_b", 1),
    ("w_in", C), ("b_in", C), ("w_dw", 9), ("b_dw", 1), ("b_dw2", 1), ("filt", C), ("w_out", C), ("b_out", 1),
])
C_TOTAL = _columns(CCOLS, [
    ("ident", 128), ("mean", 128), ("g12", 9 * 128), ("g8", 128), ("g4", 128), ("bd16", 128),
    ("sel", H2 * 96), ("dft", 128), ("idft", 128), ("msel", 128),
])


class Layer:

    def __init__(self, sem, name, units, o_buffers):
        self.units, self.o_buffers = units, o_buffers
        self.tile_scored = sem(name + "_tile_scored")
        self.tile_free = sem(name + "_tile_free")
        self.shift_split = sem(name + "_shift_split")
        self.shift_step = sem(name + "_shift_step")
        self.scored = sem(name + "_scored")
        self.p_ready = sem(name + "_p_ready")
        self.p_used = sem(name + "_p_used")
        self.o_free = sem(name + "_o_free")
        self.o_step = sem(name + "_o_step")


TILES = 66
STEPS = NBLK
TILE_PLAN = [3] * 10 + [2] * 17 + [0] * 5
assert sum(TILE_PLAN) == 64 and len(TILE_PLAN) == STEPS


def build(nc, x, weights, consts, out, nb=B):
    nc.disable_value_cache = True
    ctx = ExitStack()
    with ctx:
        def sb(name, shape, dt=FP32):
            return ctx.enter_context(nc.sbuf_tensor(name, shape, dt))

        def sem(name):
            return ctx.enter_context(nc.semaphore(name))

        W = sb("W", [128, W_TOTAL])
        K = sb("K", [128, C_TOTAL])
        DG = sb("DG", [128, 36 * 128])
        XIN = sb("XIN", [128, N])
        X = sb("X", [128, N])
        SM = sb("SM", [128, 512])
        ARENA = sb("ARENA", [128, 31 * 1024])
        PS = ctx.enter_context(nc.psum_tensor("PS", [128, 8, CH], FP32))

        def w(name, p=128):
            a, n = WCOLS[name]
            return W[0:p, a:a + n]

        def k(name, p=128):
            a, n = CCOLS[name]
            return K[0:p, a:a + n]

        def area(kb, n_kb, dt=FP32):
            v = ARENA[:, kb * 256:(kb + n_kb) * 256]
            return v if dt == FP32 else v.bitcast(dt)

        def chunk(t):
            return slice(t * CH, (t + 1) * CH)

        QA, QB, KA, KB = (area(8 * i, 8, FP16) for i in range(4))
        GT = area(32, 16).rearrange("p (j o) -> p j o", j=NBLK)
        Y0 = area(48, 16)
        QS = [area(8 * h, 8, FP16) for h in range(H1)]
        KS = [area(32 + 8 * h, 8, FP16) for h in range(H1)]
        VT = area(64, 32).rearrange("p (j h o) -> p j h o", j=NBLK, h=H1)
        XLN = area(96, 16)
        O1 = XLN
        XC, SQ, SD, RS, XH = (area(4 * i, 4).rearrange("p (s n) -> p s n", s=2) for i in range(5))
        HID = area(0, 8).rearrange("p (s h n) -> p s h n", s=2, h=2)
        P = area(112, 8).rearrange("p (s n) -> p s n", s=2)
        RCP = area(120, 4).rearrange("p (i n) -> p i n", i=2)
        MX = SM[:, 0:64].rearrange("p (r m) -> p r m", r=8)
        NEG, N16 = SM[:, 64:72], SM[:, 72:76].bitcast(FP16)
        NHL = SM[:, 80:96].rearrange("p (r two) -> p r two", two=2)
        EPS5, EPS6 = SM[:, 96:97], SM[:, 97:98]
        ONE = SM[0:1, 128:256]

        XH2 = area(0, 16)
        SROW = area(0, 64).rearrange("p (t n) -> p t n", t=16)
        QS2 = [area(64 + 2 * i, 2, FP16) for i in range(2)]
        KS2 = [area(68 + 2 * i, 2, FP16) for i in range(2)]
        QKN = area(72, 8)
        VT2 = area(80, 16).rearrange("p (j h o) -> p j h o", j=8, h=H2)
        LL = area(96, 4)
        O2 = area(100, 8).rearrange("p (g n) -> p g n", g=2)
        E2 = area(108, 8).rearrange("p (s n) -> p s n", s=2)
        PT2 = area(116, 8).rearrange("p (s n) -> p s n", s=2)
        SQ2, SD2 = area(100, 8), area(108, 8)
        JUNK = [area(108 + 2 * i, 2, FP16) for i in range(4)]
        RC2 = area(116, 8).rearrange("p (s n) -> p s n", s=4)
        PADN = (S2 + 2) * (S2 + 2)
        PAD = [ARENA[:, g * PADN:(g + 1) * PADN] for g in range(3)]
        Y1 = [area(16 + 4 * g, 4) for g in range(3)]
        HO = [area(28 + 4 * g, 4) for g in range(3)]
        TMP = [area(40 + 4 * g, 4) for g in range(4)]
        XHB = area(56, 16)
        TMPB = [area(72 + 4 * g, 4) for g in range(4)]
        F1 = area(0, 32).rearrange("p (h n) -> p h n", h=2)
        F2 = area(32, 16)
        AO = area(40, 4)
        BST = SM[:, 256:352]
        MV, EX, GM = (SM[:, 352 + 6 * i:358 + 6 * i].rearrange("p (t two) -> p t two", two=2) for i in range(3))
        MSQ, VAR, SDG, RG = (SM[:, 370 + 3 * i:373 + 3 * i] for i in range(4))

        def SC(g):
            return SM[:, 384 + 6 * g:387 + 6 * g]

        def SH(g):
            return SM[:, 387 + 6 * g:390 + 6 * g]
        LO, MID, NMID, CNT, FL = (SM[:, 416 + 16 * i:432 + 16 * i] for i in range(5))
        STEP = SM[:, 496:497]
        HP = ARENA[:, 0:66 * 66].rearrange("p (r c) -> p r c", c=66)
        FILT = ARENA[:, 19 * 256:19 * 256 + 128]
        HT, GC, G1, G2, XP = (area(20 + 4 * i, 4).rearrange("p (s n) -> p s n", s=2) for i in range(5))

        def quarter(v, r, c):
            return v.rearrange("p (y a x b) -> p y a x b", y=S2, a=2, b=2)[:, :, r, :, c]

        def half(v):
            return v.rearrange("p (y x) -> p y x", x=S2)

        def inner(g):
            return PAD[g].rearrange("p (y x) -> p y x", x=S2 + 2)[:, 1:S2 + 1, 1:S2 + 1]

        loaded = sem("loaded")
        x_loaded = sem("x_loaded")
        xin_free = sem("xin_free")
        out_stored = sem("out_stored")
        setup_done = sem("setup_done")
        stage_done = sem("stage_done")
        wait_passed = sem("wait_passed")
        dve_link = sem("dve_link")
        L0 = Layer(sem, "L0", NCH // 2, 1)
        L1 = Layer(sem, "L1", 2 * NCH, 2)

        def events(*names):
            return [sem(n) for n in names]

        p0_made, p0_head, p0_free, g0_made, g0_free = events("p0_made", "p0_head", "p0_free", "g0_made", "g0_free")
        y0_made, y0_free = events("y0_made", "y0_free")
        ln_mean, ln_xc, ln_sq, ln_var, ln_sd, ln_rs, ln_xh, ln_out = events(
            "ln_mean", "ln_xc", "ln_sq", "ln_var", "ln_sd", "ln_rs", "ln_xh", "ln_out")
        p1_made, p1_head, p1_free, v1_made, v1_free = events("p1_made", "p1_head", "p1_free", "v1_made", "v1_free")
        pr_made, pr_free = events("pr_made", "pr_free")
        f1_made, f1_done, f2_made, f2_free = events("f1_made", "f1_done", "f2_made", "f2_free")
        xh_made, xh2_made = events("xh_made", "xh2_made")
        n2_made, n2_sq, n2_sum, n2_sd, n2_done, v2_made = events("n2_made", "n2_sq", "n2_sum", "n2_sd", "n2_done", "v2_made")
        s2_made, s2_head, s2_free = events("s2_made", "s2_head", "s2_free")
        t2_made, t2_free_act, t2_free_dve = events("t2_made", "t2_free_act", "t2_free_dve")
        mid_ready, act_counted, dve_counted, found = events("mid_ready", "act_counted", "dve_counted", "found")
        e2_ready, m2_ready, x2_made, x2_free_act, x2_free_dve, pv2_done = events(
            "e2_ready", "m2_ready", "x2_made", "x2_free_act", "x2_free_dve", "pv2_done")
        gn_stats, gn_sums, gn_var, gn_sd, gn_ready = events("gn_stats", "gn_sums", "gn_var", "gn_sd", "gn_ready")
        o2_made, ao_done = events("o2_made", "ao_done")
        dw2_made, pw2_made, ho_made = events("dw2_made", "pw2_made", "ho_made")
        u1_made, u1_copied, u2_ready, u2_made, u2_copied, u3_ready = events(
            "u1_made", "u1_copied", "u2_ready", "u2_made", "u2_copied", "u3_ready")
        (xp_made,) = events("xp_made")
        fl_made, h3_made, h3_copied, c3_made, c3_scaled, i3_made, i3_placed = events(
            "fl_made", "h3_made", "h3_copied", "c3_made", "c3_scaled", "i3_made", "i3_placed")
        d3_made, d3_gelu, d3_gated, o3_made, o3_free = events("d3_made", "d3_gelu", "d3_gated", "o3_made", "o3_free")
        BISECTIONS = 26
        LOWEST, RANGE = -0.25 - 2.0 ** -12, 0.5 + 2.0 ** -11

        block = ctx.enter_context(nc.Block())
        STAGES = 33

        def stage_end(eng, b, at):
            at[0] += 1
            eng.drain().then_inc(stage_done, 1)
            eng.wait_ge(stage_done, b * (4 * STAGES) + 4 * at[0])
            eng.sem_inc(wait_passed, 1)

        @block.sync
        def _(sp):
            sp.sem_inc(out_stored, 16)
            sp.dma_start(W[:, :], weights).then_inc(loaded, 16)
            sp.dma_start(K[:, :], consts).then_inc(loaded, 16)
            with sp.Fori(0, nb) as b:
                sp.wait_ge(xin_free, b + 1)
                sp.dma_start(XIN[:, :], x[bass.ds(b, 1), :, :].rearrange("a p n -> (a p) n")).then_inc(x_loaded, 16)
                sp.wait_ge(stage_done, b * (4 * STAGES) + 4 * STAGES)
                sp.dma_start(out[bass.ds(b, 1), :, :].rearrange("a p n -> (a p) n"), X[:, :]).then_inc(out_stored, 16)
            sp.wait_ge(out_stored, 16 * nb + 16)

        @block.tensor
        def _(pe):
            mm = nc.tensor.matmul
            pe.sem_inc(L0.p_used, 2)
            pe.sem_inc(L1.p_used, 2)
            pe.wait_ge(loaded, 32)
            pe.wait_ge(setup_done, 2)

            def l0_tile(t, col):
                r, m = t // NCH, t % NCH
                rows = bass.ds(col + r * BLK, BLK)
                mm(PS[:, t % 2, :], QA[:, rows], KA[:, chunk(m)], start=True, stop=False)
                return mm(PS[:, t % 2, :], QB[0:66, rows], KB[0:66, chunk(m)], start=False, stop=True)

            def l0_scores(s, col):
                for i in range(2):
                    cols = bass.ds(col + i * CH, CH)
                    o = PS[:, 2 + 2 * (s % 2) + i, :]
                    mm(o, KA[:, s * BLK:(s + 1) * BLK], QA[:, cols], start=True, stop=False)
                    last = mm(o, KB[0:66, s * BLK:(s + 1) * BLK], QB[0:66, cols], start=False, stop=True)
                return last

            def l0_sums(s):
                for i in range(2):
                    last = mm(PS[:, 6 + i, :], GT[:, s, :], P[:, s % 2, chunk(i)],
                              start=(s == 0), stop=(s == STEPS - 1))
                return last

            def l1_tile(pair):
                def tile(t, col):
                    h, r, m = 2 * pair + t // 32, t // NCH % 4, t % NCH
                    return mm(PS[:, t % 2, :], QS[h][0:96, bass.ds(col + r * BLK, BLK)], KS[h][0:96, chunk(m)],
                              start=True, stop=True)
                return tile

            def l1_scores(pair):
                def scores(s, col):
                    for i in range(2):
                        h = 2 * pair + i
                        last = mm(PS[:, 2 + 2 * (s % 2) + i, :], KS[h][0:98, s * BLK:(s + 1) * BLK],
                                  QS[h][0:98, bass.ds(col, CH)], start=True, stop=True)
                    return last
                return scores

            def l1_sums(pair):
                def sums(s):
                    for i in range(2):
                        last = mm(PS[64 * i:64 * i + 64, 6 + pair, :], VT[:, s, 2 * pair + i, :],
                                  P[:, s % 2, chunk(i)], start=(s == 0), stop=(s == STEPS - 1))
                    return last
                return sums

            def unit(L, at, ua=None, a_tile=None, a_col=None, a_scores=None, ub=None, b_scores=None, b_col=None,
                     b_sums=None):
                t = 0
                for s in range(STEPS):
                    if ua is not None:
                        for _ in range(TILE_PLAN[s]):
                            pe.wait_ge(L.tile_free, ua * TILES + (t + 1))
                            a_tile(t, a_col).then_inc(L.tile_scored, 1)
                            t += 1
                        if s == STEPS - 2:
                            pe.wait_ge(L.shift_split, ua + 1)
                            for i in range(2):
                                pe.wait_ge(L.tile_free, ua * TILES + (65 + i))
                                for r in range(4):
                                    last = mm(PS[at:at + 2, i, r * BLK:(r + 1) * BLK], NHL[:, 4 * i + r, :], k("ident"),
                                              start=True, stop=True)
                                last.then_inc(L.tile_scored, 1)
                        if s == STEPS - 1:
                            pe.wait_ge(L.tile_free, ua * TILES + (TILES + 2))
                            pe.wait_ge(L.p_ready, ua * STEPS + 1)
                            a_scores(0, a_col).then_inc(L.scored, 1)
                    if ub is not None:
                        if s + 1 < STEPS:
                            pe.wait_ge(L.p_ready, ub * STEPS + (s + 2))
                            b_scores(s + 1, b_col).then_inc(L.scored, 1)
                        pe.wait_ge(L.p_ready, ub * STEPS + (s + 3))
                        if s == 0:
                            pe.wait_ge(L.o_free, ub + 1)
                        b_sums(s).then_inc(L.p_used, 1)

            pe_at = [0]
            with pe.Fori(0, nb) as b:
                pe.wait_ge(x_loaded, b * 16 + 16)
                for j in range(2 * NCH):
                    if j >= 4:
                        pe.wait_ge(p0_free, b * (2 * NCH) + (j - 3))
                    mm(PS[:, j % 4, :], w("wt2") if j % 2 == 0 else w("wp2"), XIN[:, chunk(j // 2)],
                       start=True, stop=True).then_inc(p0_made, 1)
                for j in range(NBLK):
                    o = PS[:, 4 + j // 8, (j % 8) * IC:(j % 8 + 1) * IC]
                    mm(o, XIN[:, j * BLK:(j + 1) * BLK], w("wg"), start=True, stop=False)
                    last = mm(o, ONE[:, 0:BLK], w("bg", 1), start=False, stop=True)
                    if j % 8 == 7:
                        last.then_inc(g0_made, 1)
                stage_end(pe, b, pe_at)
                a = dict(a_tile=l0_tile, a_scores=l0_scores)
                bb = dict(b_scores=l0_scores, b_sums=l0_sums)
                u0 = b * (NCH // 2)
                unit(L0, 64, ua=u0, a_col=0, **a)
                with pe.Fori(0, NCH // 2 - 1) as q:
                    unit(L0, 64, ua=u0 + q + 1, a_col=q * (2 * CH) + 2 * CH, ub=u0 + q, b_col=q * (2 * CH), **a, **bb)
                unit(L0, 64, ub=u0 + (NCH // 2 - 1), b_col=N - 2 * CH, **bb)
                stage_end(pe, b, pe_at)
                for t in range(NCH):
                    if t >= 2:
                        pe.wait_ge(y0_free, b * NCH + (t - 1))
                    mm(PS[:, t % 2, :], w("ww", IC), Y0[0:IC, chunk(t)], start=True, stop=True).then_inc(y0_made, 1)
                stage_end(pe, b, pe_at)

                def layernorm(n):
                    base = b * (2 * NCH) + n * NCH
                    for t in range(NCH + 1):
                        if t < NCH:
                            if t >= 2:
                                pe.wait_ge(ln_xc, base + (t - 1))
                            mm(PS[:, t % 2, :], k("mean"), X[:, chunk(t)], start=True, stop=True).then_inc(ln_mean, 1)
                        if t >= 1:
                            pe.wait_ge(ln_sq, base + t)
                            if t >= 3:
                                pe.wait_ge(ln_sd, base + (t - 2))
                            mm(PS[:, 2 + (t - 1) % 2, :], k("mean"), SQ[:, (t - 1) % 2, :],
                               start=True, stop=True).then_inc(ln_var, 1)

                layernorm(0)
                stage_end(pe, b, pe_at)
                for j in range(2 * H1 * NCH):
                    h, t = j // 2 % H1, j // (2 * H1)
                    if j >= 4:
                        pe.wait_ge(p1_free, b * (2 * H1 * NCH) + (j - 3))
                    mm(PS[0:96, j % 4, :], w("wq" if j % 2 == 0 else "wk")[:, h * 96:(h + 1) * 96],
                       XLN[:, chunk(t)], start=True, stop=True).then_inc(p1_made, 1)
                for j in range(NBLK):
                    if j % 4 == 0 and j >= 16:
                        pe.wait_ge(v1_free, b * (NBLK // 4) + (j // 4 - 3))
                    last = mm(PS[:, 4 + j // 4 % 4, (j % 4) * C:(j % 4 + 1) * C], XLN[:, j * BLK:(j + 1) * BLK],
                              w("wv"), start=True, stop=True)
                    if j % 4 == 3:
                        last.then_inc(v1_made, 1)
                stage_end(pe, b, pe_at)
                u1 = b * (2 * NCH)

                def a1(p):
                    return dict(a_tile=l1_tile(p), a_scores=l1_scores(p))

                def b1(p):
                    return dict(b_scores=l1_scores(p), b_sums=l1_sums(p))

                unit(L1, 96, ua=u1, a_col=0, **a1(0))
                with pe.Fori(0, NCH - 1) as q:
                    unit(L1, 96, ua=u1 + q * 2 + 1, a_col=q * CH, **a1(1), ub=u1 + q * 2, b_col=q * CH, **b1(0))
                    unit(L1, 96, ua=u1 + q * 2 + 2, a_col=q * CH + CH, **a1(0), ub=u1 + q * 2 + 1, b_col=q * CH, **b1(1))
                unit(L1, 96, ua=u1 + (2 * NCH - 1), a_col=N - CH, **a1(1), ub=u1 + (2 * NCH - 2), b_col=N - CH, **b1(0))
                unit(L1, 96, ub=u1 + (2 * NCH - 1), b_col=N - CH, **b1(1))
                stage_end(pe, b, pe_at)
                for t in range(NCH):
                    if t >= 2:
                        pe.wait_ge(pr_free, b * NCH + (t - 1))
                    mm(PS[:, t % 2, :], w("proj"), O1[:, chunk(t)], start=True, stop=True).then_inc(pr_made, 1)
                stage_end(pe, b, pe_at)
                layernorm(1)
                stage_end(pe, b, pe_at)
                for t in range(NCH + 1):
                    if t < NCH:
                        for i in range(2):
                            if t >= 2:
                                pe.wait_ge(f1_done, b * (2 * NCH) + (2 * (t - 2) + i + 1))
                            mm(PS[:, 2 * (t % 2) + i, :], w("fc1")[:, i * 128:(i + 1) * 128], XLN[:, chunk(t)],
                               start=True, stop=True).then_inc(f1_made, 1)
                    if t >= 1:
                        pe.wait_ge(f1_done, b * (2 * NCH) + 2 * t)
                        if t >= 3:
                            pe.wait_ge(f2_free, b * NCH + (t - 2))
                        for i in range(2):
                            last = mm(PS[:, 4 + (t - 1) % 2, :], w("fc2")[:, i * 128:(i + 1) * 128],
                                      HID[:, (t - 1) % 2, i, :], start=(i == 0), stop=(i == 1))
                        last.then_inc(f2_made, 1)
                stage_end(pe, b, pe_at)
                stage_end(pe, b, pe_at)
                for j in range(4):
                    mm(PS[:, j, :], w("q2")[:, j // 2 * C:(j // 2 + 1) * C], LL[:, chunk(j % 2)],
                       start=True, stop=True).then_inc(n2_made, 1)
                for j in range(8):
                    last = mm(PS[:, 6 + j // 4, (j % 4) * C:(j % 4 + 1) * C], LL[:, j * BLK:(j + 1) * BLK],
                              w("q2")[:, 2 * C:3 * C], start=True, stop=True)
                last.then_inc(v2_made, 1)
                for j in range(4):
                    pe.wait_ge(n2_sq, b * 4 + (j + 1))
                    if j >= 2:
                        pe.wait_ge(n2_sd, b * 4 + (j - 1))
                    mm(PS[:, 4 + j % 2, :], k("bd16"), SQ2[:, chunk(j)], start=True, stop=True).then_inc(n2_sum, 1)
                stage_end(pe, b, pe_at)
                for pr in range(H2 // 2):
                    for j in range(8):
                        i, z, t = j // 4, j // 2 % 2, j % 2
                        if j >= 4:
                            pe.wait_ge(s2_free, b * (8 * 4) + (8 * pr + j - 3))
                        mm(PS[0:96, j % 4, :], k("sel")[:, (2 * pr + i) * 96:(2 * pr + i + 1) * 96],
                           QKN[:, z * N2 + t * CH:z * N2 + (t + 1) * CH], start=True, stop=True).then_inc(s2_made, 1)
                    stage_end(pe, b, pe_at)
                    for t in range(16):
                        if t >= 2:
                            pe.wait_ge(t2_free_act if t % 2 == 0 else t2_free_dve, b * (8 * 4) + (8 * pr + (t - 2) // 2 + 1))
                        for m in range(2):
                            last = mm(PS[:, 4 + 2 * (t % 2) + m, :], QS2[t // 8][0:96, t % 8 * BLK:(t % 8 + 1) * BLK],
                                      KS2[t // 8][0:96, chunk(m)], start=True, stop=True)
                        last.then_inc(t2_made, 1)
                    stage_end(pe, b, pe_at)
                    for t in range(17):
                        if t < 16:
                            pe.wait_ge(m2_ready, b * (16 * 4) + (16 * pr + t + 1))
                            if t >= 2:
                                pe.wait_ge(x2_free_act, b * (16 * 4) + (16 * pr + t - 1))
                                pe.wait_ge(x2_free_dve, b * (16 * 4) + (16 * pr + t - 1))
                            for j in range(8):
                                last = nc.tensor.transpose(PS[:, 2 * (t % 2) + j // 4, (j % 4) * BLK:(j % 4 + 1) * BLK],
                                                           SROW[:, t, j * BLK:(j + 1) * BLK], k("ident"))
                            last.then_inc(x2_made, 1)
                        if t >= 1:
                            u = t - 1
                            i, r = u // 8, u % 8
                            pe.wait_ge(x2_free_act, b * (16 * 4) + (16 * pr + u + 1))
                            pe.wait_ge(x2_free_dve, b * (16 * 4) + (16 * pr + u + 1))
                            for j in range(8):
                                last = mm(PS[0:64, 4 + 2 * i + r // 4, (r % 4) * BLK:(r % 4 + 1) * BLK],
                                          VT2[:, j, 2 * pr + i, :], PT2[:, u % 2, j * BLK:(j + 1) * BLK],
                                          start=(j == 0), stop=(j == 7))
                            last.then_inc(pv2_done, 1)
                    stage_end(pe, b, pe_at)
                    stage_end(pe, b, pe_at)

                def group_sums(g, tiles, name):
                    pe.wait_ge(gn_stats, b * 5 + (g + 1))
                    for o in range(tiles):
                        n = tiles if name == "g12" else 1
                        for i in range(n):
                            gi = i if n > 1 else o
                            m = k(name)[:, gi * 384 + o * 128:gi * 384 + (o + 1) * 128] if n > 1 else k(name)
                            last = mm(PS[:, 7, 2 * o:2 * o + 2], m, EX[:, gi, :], start=(i == 0), stop=(i == n - 1))
                    last.then_inc(gn_sums, 1)

                for t in range(2):
                    for g in range(2):
                        last = mm(PS[:, t, :], w("proj2")[:, g * C:(g + 1) * C], O2[:, g, chunk(t)],
                                  start=(g == 0), stop=(g == 1))
                    last.then_inc(o2_made, 1)
                group_sums(0, 1, "g4")
                stage_end(pe, b, pe_at)
                for g in range(3):
                    for t in range(2):
                        for tap in range(9):
                            src = PAD[g].rearrange("p (y x) -> p y x", x=S2 + 2)[:, 16 * t + tap // 3:16 * t + tap // 3 + 16,
                                                                              tap % 3:tap % 3 + S2]
                            last = mm(PS[:, 2 * g + t, :].rearrange("p (y x) -> p y x", x=S2),
                                      DG[:, (9 * g + tap) * 128:(9 * g + tap + 1) * 128], src,
                                      start=(tap == 0), stop=(tap == 8))
                        last.then_inc(dw2_made, 1)
                group_sums(1, 3, "g12")
                stage_end(pe, b, pe_at)
                for o in range(3):
                    for t in range(2):
                        for g in range(3):
                            last = mm(PS[:, 2 * o + t, :], w("he_pw")[:, g * 384 + o * 128:g * 384 + (o + 1) * 128],
                                      Y1[g][:, chunk(t)], start=(g == 0), stop=(g == 2))
                        last.then_inc(pw2_made, 1)
                group_sums(2, 3, "g12")
                stage_end(pe, b, pe_at)
                for j in range(2 * NCH):
                    if j >= 4:
                        pe.wait_ge(u1_copied, b * (2 * NCH) + (j - 3))
                    mm(PS[:, j % 4, :], w("f1")[:, j // NCH * 128:(j // NCH + 1) * 128], X[:, chunk(j % NCH)],
                       start=True, stop=True).then_inc(u1_made, 1)
                group_sums(3, 2, "g8")
                for t in range(NCH):
                    pe.wait_ge(u2_ready, b * (2 * NCH) + (2 * t + 2))
                    if t >= 2:
                        pe.wait_ge(u2_copied, b * NCH + (t - 1))
                    for i in range(2):
                        last = mm(PS[:, 4 + t % 2, :], w("f2")[:, i * 128:(i + 1) * 128], F1[:, i, chunk(t)],
                                  start=(i == 0), stop=(i == 1))
                    last.then_inc(u2_made, 1)
                group_sums(4, 1, "g4")
                stage_end(pe, b, pe_at)
                mm(PS[:, 6, 0:128], k("msel", 40), w("filt", 40), start=True, stop=True).then_inc(fl_made, 1)
                for g in range(NCH + 2):
                    if g < NCH:
                        if g >= 2:
                            pe.wait_ge(h3_copied, b * NCH + (g - 1))
                        pe.wait_ge(xp_made, b * NCH + (g + 1))
                        for q in range(4):
                            o = PS[:, g % 2, q * 128:(q + 1) * 128]
                            mm(o, XP[:, g % 2, q * 128:(q + 1) * 128], w("w_in"), start=True, stop=False)
                            last = mm(o, ONE[:, 0:128], w("b_in", 1), start=False, stop=True)
                        last.then_inc(h3_made, 1)
                    if 1 <= g <= NCH:
                        i = g - 1
                        pe.wait_ge(h3_copied, b * NCH + (i + 1))
                        if i >= 2:
                            pe.wait_ge(c3_scaled, b * NCH + (i - 1))
                        mm(PS[:, 2 + i % 2, :], k("dft"), HT[:, i % 2, :], start=True, stop=True).then_inc(c3_made, 1)
                    if g >= 2:
                        i = g - 2
                        pe.wait_ge(c3_scaled, b * NCH + (i + 1))
                        if i >= 2:
                            pe.wait_ge(i3_placed, b * NCH + (i - 1))
                        for q in range(4):
                            last = mm(PS[:, 4 + i % 2, q * 128:(q + 1) * 128], GC[:, i % 2, q * 128:(q + 1) * 128],
                                      k("idft"), start=True, stop=True)
                        last.then_inc(i3_made, 1)
                stage_end(pe, b, pe_at)
                for g in range(NCH + 1):
                    if g < NCH:
                        if g >= 2:
                            pe.wait_ge(d3_gated, b * NCH + (g - 1))
                        for tap in range(9):
                            last = mm(PS[:, 6 + g % 2, :].rearrange("p (y x) -> p y x", x=SIDE),
                                      DG[:, (27 + tap) * 128:(28 + tap) * 128],
                                      HP[:, 8 * g + tap // 3:8 * g + tap // 3 + 8, tap % 3:tap % 3 + SIDE],
                                      start=(tap == 0), stop=(tap == 8))
                        last.then_inc(d3_made, 1)
                    if g >= 1:
                        i = g - 1
                        pe.wait_ge(d3_gated, b * NCH + (i + 1))
                        if i >= 2:
                            pe.wait_ge(o3_free, b * NCH + (i - 1))
                        mm(PS[:, i % 2, :], w("w_out", 64), G2[0:64, i % 2, :], start=True, stop=True).then_inc(o3_made, 1)
                stage_end(pe, b, pe_at)
            assert pe_at[0] == STAGES

        @block.scalar
        def _(act):
            go = nc.scalar.activation
            act.sem_inc(L0.p_ready, 2)
            act.sem_inc(L1.p_ready, 2)
            act.sem_inc(act_counted, 2)
            act.wait_ge(loaded, 32)
            act.wait_ge(setup_done, 2)

            def exps(L, u, scale):
                for s in range(STEPS):
                    act.wait_ge(L.scored, u * STEPS + (s + 1))
                    act.wait_ge(L.p_used, u * STEPS + (s + 1))
                    go(P[:, s % 2, :].rearrange("p (i n) -> p i n", i=2), PS[:, 2 + 2 * (s % 2):4 + 2 * (s % 2), :],
                       ACT.Exp, scale=scale).then_inc(L.p_ready, 1)

            act_at = [0]
            with act.Fori(0, nb) as b:
                for t in range(NCH):
                    act.wait_ge(p0_made, b * (2 * NCH) + (2 * t + 1))
                    go(QA[:, chunk(t)], PS[:, 2 * t % 4, :], ACT.Identity, bias=w("bt2")).then_inc(p0_head, 1)
                    act.wait_ge(p0_made, b * (2 * NCH) + (2 * t + 2))
                    go(KB[0:64, chunk(t)], PS[0:64, (2 * t + 1) % 4, :], ACT.Identity, bias=w("bp2", 64))
                    go(KA[:, chunk(t)], PS[:, (2 * t + 1) % 4, :], ACT.Identity, bias=w("bp2")).then_inc(p0_head, 1)
                stage_end(act, b, act_at)
                with act.Fori(0, NCH // 2) as q:
                    exps(L0, b * (NCH // 2) + q, 1.0)
                stage_end(act, b, act_at)
                stage_end(act, b, act_at)

                def layernorm(n):
                    base = b * (2 * NCH) + n * NCH
                    for t in range(NCH + 1):
                        if t < NCH:
                            act.wait_ge(ln_xc, base + (t + 1))
                            if t >= 2:
                                act.wait_ge(ln_var, base + (t - 1))
                            go(SQ[:, t % 2, :], XC[:, t % 2, :], ACT.Square).then_inc(ln_sq, 1)
                        if t >= 1:
                            act.wait_ge(ln_var, base + t)
                            if t >= 3:
                                act.wait_ge(ln_rs, base + (t - 2))
                            go(SD[:, (t - 1) % 2, :], PS[:, 2 + (t - 1) % 2, :], ACT.Sqrt, bias=EPS5).then_inc(ln_sd, 1)

                layernorm(0)
                stage_end(act, b, act_at)
                for j in range(2 * H1 * NCH):
                    h, t = j // 2 % H1, j // (2 * H1)
                    act.wait_ge(p1_made, b * (2 * H1 * NCH) + (j + 1))
                    go((QS if j % 2 == 0 else KS)[h][0:96, chunk(t)], PS[0:96, j % 4, :], ACT.Copy).then_inc(p1_head, 1)
                stage_end(act, b, act_at)
                with act.Fori(0, 2 * NCH) as q:
                    exps(L1, b * (2 * NCH) + q, float(D1) ** -0.5)
                stage_end(act, b, act_at)
                stage_end(act, b, act_at)
                layernorm(1)
                stage_end(act, b, act_at)
                for t in range(NCH):
                    for i in range(2):
                        act.wait_ge(f1_made, b * (2 * NCH) + (2 * t + i + 1))
                        if t >= 2:
                            act.wait_ge(f2_made, b * NCH + (t - 1))
                        go(HID[:, t % 2, i, :], PS[:, 2 * (t % 2) + i, :], ACT.Gelu,
                           bias=w("fc1b")[:, i:i + 1]).then_inc(f1_done, 1)
                stage_end(act, b, act_at)
                go(XH2, X[:, :], ACT.Copy, scale=0.5).then_inc(xh_made, 1)
                stage_end(act, b, act_at)
                for j in range(4):
                    act.wait_ge(n2_made, b * 4 + (j + 1))
                    go(SQ2[:, chunk(j)], PS[:, j, :], ACT.Square).then_inc(n2_sq, 1)
                for j in range(4):
                    act.wait_ge(n2_sum, b * 4 + (j + 1))
                    go(SD2[:, chunk(j)], PS[:, 4 + j % 2, :], ACT.Sqrt).then_inc(n2_sd, 1)
                stage_end(act, b, act_at)
                for pr in range(H2 // 2):
                    for j in range(8):
                        i, z, t = j // 4, j // 2 % 2, j % 2
                        act.wait_ge(s2_made, b * (8 * 4) + (8 * pr + j + 1))
                        go((QS2, KS2)[z][i][0:96, chunk(t)], PS[0:96, j % 4, :], ACT.Copy).then_inc(s2_head, 1)
                    stage_end(act, b, act_at)
                    for t in range(0, 16, 2):
                        act.wait_ge(t2_made, b * (16 * 4) + (16 * pr + t + 1))
                        go(SROW[:, t, :].rearrange("p (m n) -> p m n", m=2), PS[:, 4:6, :], ACT.Copy,
                           scale=float(D2) ** -0.5).then_inc(t2_free_act, 1)
                    stage_end(act, b, act_at)
                    base = b * (4 * BISECTIONS + 4) + pr * (BISECTIONS + 1)
                    cbase = b * (4 * BISECTIONS) + pr * BISECTIONS
                    with act.Fori(0, BISECTIONS) as n:
                        act.wait_ge(mid_ready, base + n + 1)
                        for t in range(8):
                            act.wait_ge(act_counted, cbase * 8 + n * 8 + (t + 1))
                            go(JUNK[2 + t % 2], SROW[:, 8 + t, :], ACT.Sign, bias=NMID[:, 8 + t:9 + t],
                               accum_out=CNT[:, 8 + t:9 + t]).then_inc(act_counted, 1)
                    act.wait_ge(found, b * 4 + (pr + 1))
                    for t in range(17):
                        if t < 16:
                            if t >= 2:
                                act.wait_ge(m2_ready, b * (16 * 4) + (16 * pr + t - 1))
                            go(E2[:, t % 2, :], SROW[:, t, :], ACT.Exp).then_inc(e2_ready, 1)
                        if t >= 1:
                            u = t - 1
                            act.wait_ge(x2_made, b * (16 * 4) + (16 * pr + u + 1))
                            if u >= 2:
                                act.wait_ge(pv2_done, b * (16 * 4) + (16 * pr + u - 1))
                            go(PT2[:, u % 2, 0:CH], PS[:, 2 * (u % 2), :], ACT.Copy).then_inc(x2_free_act, 1)
                    stage_end(act, b, act_at)
                    stage_end(act, b, act_at)

                def group_sd(g, tiles):
                    act.wait_ge(gn_var, b * 5 + (g + 1))
                    go(SDG[:, 0:tiles], VAR[:, 0:tiles], ACT.Sqrt, bias=EPS6).then_inc(gn_sd, 1)

                group_sd(0, 1)
                act.wait_ge(gn_ready, b * 5 + 1)
                go(AO.rearrange("p (t n) -> p t n", t=2), PS[:, 0:2, :], ACT.Identity,
                   bias=SH(0)[:, 0:1], scale=SC(0)[:, 0:1]).then_inc(ao_done, 1)
                go(XHB, X[:, :], ACT.Copy, scale=0.5).then_inc(xh2_made, 1)
                stage_end(act, b, act_at)
                group_sd(1, 3)
                act.wait_ge(gn_ready, b * 5 + 2)
                for g in range(3):
                    go(Y1[g].rearrange("p (t n) -> p t n", t=2), PS[:, 2 * g:2 * g + 2, :], ACT.Silu,
                       bias=SH(1)[:, g:g + 1], scale=SC(1)[:, g:g + 1])
                stage_end(act, b, act_at)
                group_sd(2, 3)
                act.wait_ge(gn_ready, b * 5 + 3)
                for g in range(3):
                    go(HO[g].rearrange("p (t n) -> p t n", t=2), PS[:, 2 * g:2 * g + 2, :], ACT.Identity,
                       bias=SH(2)[:, g:g + 1], scale=SC(2)[:, g:g + 1]).then_inc(ho_made, 1)
                stage_end(act, b, act_at)
                for j in range(2 * NCH):
                    act.wait_ge(u1_made, b * (2 * NCH) + (j + 1))
                    go(F1[:, j // NCH, chunk(j % NCH)], PS[:, j % 4, :], ACT.Copy).then_inc(u1_copied, 1)
                group_sd(3, 2)
                act.wait_ge(gn_ready, b * 5 + 4)
                for t in range(NCH):
                    for i in range(2):
                        go(F1[:, i, chunk(t)], F1[:, i, chunk(t)], ACT.Gelu, bias=SH(3)[:, i:i + 1],
                           scale=SC(3)[:, i:i + 1]).then_inc(u2_ready, 1)
                for t in range(NCH):
                    act.wait_ge(u2_made, b * NCH + (t + 1))
                    go(F2[:, chunk(t)], PS[:, 4 + t % 2, :], ACT.Copy).then_inc(u2_copied, 1)
                group_sd(4, 1)
                act.wait_ge(gn_ready, b * 5 + 5)
                for t in range(NCH):
                    go(F2[:, chunk(t)], F2[:, chunk(t)], ACT.Identity, bias=SH(4)[:, 0:1],
                       scale=SC(4)[:, 0:1]).then_inc(u3_ready, 1)
                stage_end(act, b, act_at)
                for g in range(NCH + 1):
                    if g < NCH:
                        act.wait_ge(h3_made, b * NCH + (g + 1))
                        if g >= 2:
                            act.wait_ge(c3_made, b * NCH + (g - 1))
                        go(HT[:, g % 2, :], PS[:, g % 2, :], ACT.Copy).then_inc(h3_copied, 1)
                    if g >= 1:
                        i = g - 1
                        act.wait_ge(i3_made, b * NCH + (i + 1))
                        go(HP[:, 8 * i + 1:8 * i + 9, 1:SIDE + 1].rearrange("p r (q c) -> p r q c", q=4),
                           PS[:, 4 + i % 2, :].rearrange("p (q r c) -> p r q c", q=4, r=8), ACT.Copy).then_inc(i3_placed, 1)
                stage_end(act, b, act_at)
                for g in range(NCH):
                    act.wait_ge(d3_made, b * NCH + (g + 1))
                    if g >= 2:
                        act.wait_ge(d3_gated, b * NCH + (g - 1))
                    go(G1[0:64, g % 2, :], PS[0:64, 6 + g % 2, :], ACT.Gelu, bias=w("b_dw", 64)).then_inc(d3_gelu, 1)
                stage_end(act, b, act_at)
            assert act_at[0] == STAGES

        @block.gpsimd
        def _(pool):
            pool.sem_inc(xin_free, 1)
            pool.wait_ge(loaded, 32)
            for i in range(36):
                col = w("he_dw")[:, i:i + 1] if i < 27 else w("w_dw")[:, i - 27:i - 26]
                nc.gpsimd.tensor_scalar(DG[:, i * 128:(i + 1) * 128], k("ident"), col, None, ALU.mult)
            pool.drain().then_inc(setup_done, 1)
            pool_at = [0]
            with pool.Fori(0, nb) as b:
                stage_end(pool, b, pool_at)
                stage_end(pool, b, pool_at)
                stage_end(pool, b, pool_at)
                for n in range(4, 10):
                    if n in (4, 8):
                        base = b * (2 * NCH) + (n == 8) * NCH
                        for t in range(NCH):
                            pool.wait_ge(ln_xh, base + (t + 1))
                            pool.sem_inc(wait_passed, 1)
                            nc.gpsimd.tensor_scalar(XLN[:, chunk(t)], XH[:, t % 2, :], w("ln1w" if n == 4 else "ln2w"),
                                                    w("ln1b" if n == 4 else "ln2b"), ALU.mult, ALU.add).then_inc(ln_out, 1)
                    stage_end(pool, b, pool_at)
                for n in range(10, STAGES + 1):
                    if n == STAGES - 1:
                        for g in range(NCH):
                            if g >= 2:
                                pool.wait_ge(h3_made, b * NCH + (g - 1))
                                pool.sem_inc(wait_passed, 1)
                            nc.gpsimd.tensor_copy(
                                XP[:, g % 2, :].rearrange("p (q r c) -> p r q c", q=4, r=8),
                                X[:, chunk(g)].rearrange("p (r q c) -> p r q c", r=8, q=4)).then_inc(xp_made, 1)
                    stage_end(pool, b, pool_at)
            assert pool_at[0] == STAGES

        @block.vector
        def _(dve):
            v = nc.vector
            dve.sem_inc(L0.tile_free, 2)
            dve.sem_inc(L1.tile_free, 2)
            dve.sem_inc(L0.o_free, 1)
            dve.sem_inc(L1.o_free, 2)
            dve.sem_inc(dve_counted, 2)
            v.memset(EPS5, 1e-5)
            v.memset(EPS6, 1e-6)
            v.memset(ONE, 1.0)
            dve.drain().then_inc(setup_done, 1)
            dve.wait_ge(loaded, 32)

            def maxima(L, u, at, rows_to):
                for t in range(64):
                    dve.wait_ge(L.tile_scored, u * TILES + (t + 1))
                    v.tensor_reduce(MX[:, t // 8, t % 8:t % 8 + 1], PS[:, t % 2, :], AX.X, ALU.max).then_inc(L.tile_free, 1)
                dve.wait_ge(L.tile_free, u * TILES + 66)
                v.tensor_reduce(NEG, MX, AX.X, ALU.max, negate=True).then_inc(L.shift_step, 1)
                dve.wait_ge(L.shift_step, u * 3 + 1)
                v.tensor_copy(N16, NEG).then_inc(L.shift_step, 1)
                dve.wait_ge(L.shift_step, u * 3 + 2)
                v.tensor_copy(NHL[:, :, 0], N16).then_inc(L.shift_step, 1)
                dve.wait_ge(L.shift_step, u * 3 + 3)
                v.tensor_tensor(NHL[:, :, 1], NEG, NHL[:, :, 0], ALU.subtract).then_inc(L.shift_split, 1)
                for i in range(2):
                    dve.wait_ge(L.tile_scored, u * TILES + (65 + i))
                    v.tensor_copy(rows_to(i), PS[at:at + 2, i, :]).then_inc(L.tile_free, 1)

            def l0_maxima(u, col):
                maxima(L0, u, 64, lambda i: QB[64:66, bass.ds(col + i * CH, CH)])

            def l1_maxima(u, pair, col):
                maxima(L1, u, 96, lambda i: QS[2 * pair + i][96:98, bass.ds(col, CH)])

            def l0_take(u, col):
                dve.wait_ge(L0.o_free, u + L0.o_buffers)
                dve.wait_ge(L0.p_used, u * STEPS + (STEPS + 2))
                for i in range(2):
                    r = RCP[0:64, i, :]
                    v.reciprocal(r, PS[64:128, 6 + i, :]).then_inc(L0.o_step, 1)
                    dve.wait_ge(L0.o_step, u * 2 + (i + 1))
                    last = v.tensor_tensor(Y0[0:64, bass.ds(col + i * CH, CH)], PS[0:64, 6 + i, :], r, ALU.mult)
                last.then_inc(L0.o_free, 1)

            def l1_take(u, pair, col):
                dve.wait_ge(L1.o_free, u + L1.o_buffers)
                dve.wait_ge(L1.p_used, u * STEPS + (STEPS + 2))
                for i in range(2):
                    h = 2 * pair + i
                    r = RCP[0:32, i, :]
                    v.reciprocal(r, PS[64 * i + 32:64 * i + 64, 6 + pair, :]).then_inc(L1.o_step, 1)
                    dve.wait_ge(L1.o_step, u * 2 + (i + 1))
                    last = v.tensor_tensor(O1[32 * h:32 * h + 32, bass.ds(col, CH)], PS[64 * i:64 * i + 32, 6 + pair, :],
                                           r, ALU.mult)
                last.then_inc(L1.o_free, 1)

            dve_at = [0]
            with dve.Fori(0, nb) as b:
                for t in range(NCH):
                    for i in range(2):
                        j = 2 * t + i
                        dve.wait_ge(p0_head, b * (2 * NCH) + (j + 1))
                        if i == 0:
                            v.scalar_tensor_tensor(QB[0:64, chunk(t)], PS[0:64, j % 4, :], w("bt2", 64), QA[0:64, chunk(t)],
                                                   ALU.add, ALU.subtract).then_inc(p0_free, 1)
                        else:
                            v.scalar_tensor_tensor(KA[64:128, chunk(t)], PS[64:128, j % 4, :], w("bp2")[64:128, :],
                                                   KA[64:128, chunk(t)], ALU.add, ALU.subtract).then_inc(p0_free, 1)
                v.memset(GT[:, :, IC:128], 1.0)
                v.memset(QB[64:66, :], 0.0)
                v.memset(KB[64:66, :], 1.0)
                for j in range(4):
                    dve.wait_ge(g0_made, b * 4 + (j + 1))
                    v.tensor_copy(GT[:, 8 * j:8 * j + 8, 0:IC], PS[:, 4 + j, :].rearrange("p (j o) -> p j o", o=IC))
                stage_end(dve, b, dve_at)
                u0 = b * (NCH // 2)
                l0_maxima(u0, 0)
                with dve.Fori(0, NCH // 2 - 1) as q:
                    l0_maxima(u0 + q + 1, q * (2 * CH) + 2 * CH)
                    l0_take(u0 + q, q * (2 * CH))
                l0_take(u0 + (NCH // 2 - 1), N - 2 * CH)
                stage_end(dve, b, dve_at)
                dve.wait_ge(out_stored, b * 16 + 16)
                for t in range(NCH):
                    dve.wait_ge(y0_made, b * NCH + (t + 1))
                    v.scalar_tensor_tensor(X[:, chunk(t)], PS[:, t % 2, :], w("bw"), XIN[:, chunk(t)],
                                           ALU.add, ALU.add).then_inc(y0_free, 1)
                dve.drain().then_inc(xin_free, 1)
                stage_end(dve, b, dve_at)

                def layernorm(n):
                    base = b * (2 * NCH) + n * NCH
                    for t in range(NCH + 1):
                        if t < NCH:
                            dve.wait_ge(ln_mean, base + (t + 1))
                            if t >= 2:
                                dve.wait_ge(ln_xh, base + (t - 1))
                            v.tensor_tensor(XC[:, t % 2, :], X[:, chunk(t)], PS[:, t % 2, :], ALU.subtract).then_inc(ln_xc, 1)
                        if t >= 1:
                            i = (t - 1) % 2
                            dve.wait_ge(ln_sd, base + t)
                            v.reciprocal(RS[:, i, :], SD[:, i, :]).then_inc(ln_rs, 1)
                            dve.wait_ge(ln_rs, base + t)
                            if t >= 3:
                                dve.wait_ge(ln_out, base + (t - 2))
                            v.tensor_tensor(XH[:, i, :], XC[:, i, :], RS[:, i, :], ALU.mult).then_inc(ln_xh, 1)

                layernorm(0)
                stage_end(dve, b, dve_at)
                for j in range(2 * H1 * NCH):
                    h, t = j // 2 % H1, j // (2 * H1)
                    at, to = (64, QS) if j % 2 == 0 else (32, KS)
                    dve.wait_ge(p1_head, b * (2 * H1 * NCH) + (j + 1))
                    low = to[h][at:at + 32, chunk(t)]
                    v.tensor_tensor(low, PS[at:at + 32, j % 4, :], low, ALU.subtract).then_inc(p1_free, 1)
                for h in range(H1):
                    v.memset(QS[h][96:98, :], 0.0)
                    v.memset(KS[h][96:98, :], 1.0)
                v.memset(VT[:, :, :, 32:64], 1.0)
                for j in range(NBLK // 4):
                    dve.wait_ge(v1_made, b * (NBLK // 4) + (j + 1))
                    for i in range(4):
                        last = v.tensor_copy(VT[:, 4 * j + i, :, 0:32],
                                             PS[:, 4 + j % 4, i * C:(i + 1) * C].rearrange("p (h o) -> p h o", h=H1))
                    last.then_inc(v1_free, 1)
                stage_end(dve, b, dve_at)
                u1 = b * (2 * NCH)
                l1_maxima(u1, 0, 0)
                with dve.Fori(0, NCH - 1) as q:
                    l1_maxima(u1 + q * 2 + 1, 1, q * CH)
                    l1_take(u1 + q * 2, 0, q * CH)
                    l1_maxima(u1 + q * 2 + 2, 0, q * CH + CH)
                    l1_take(u1 + q * 2 + 1, 1, q * CH)
                l1_maxima(u1 + (2 * NCH - 1), 1, N - CH)
                l1_take(u1 + (2 * NCH - 2), 0, N - CH)
                l1_take(u1 + (2 * NCH - 1), 1, N - CH)
                stage_end(dve, b, dve_at)
                for t in range(NCH):
                    dve.wait_ge(pr_made, b * NCH + (t + 1))
                    v.scalar_tensor_tensor(X[:, chunk(t)], PS[:, t % 2, :], w("projb"), X[:, chunk(t)],
                                           ALU.add, ALU.add).then_inc(pr_free, 1)
                stage_end(dve, b, dve_at)
                layernorm(1)
                stage_end(dve, b, dve_at)
                for t in range(NCH):
                    dve.wait_ge(f2_made, b * NCH + (t + 1))
                    v.scalar_tensor_tensor(X[:, chunk(t)], PS[:, 4 + t % 2, :], w("fc2b"), X[:, chunk(t)],
                                           ALU.add, ALU.add).then_inc(f2_free, 1)
                stage_end(dve, b, dve_at)
                dve.wait_ge(xh_made, b + 1)
                tt = v.tensor_tensor
                tt(half(E2[:, 0, :]), quarter(XH2, 0, 0), quarter(XH2, 1, 0), ALU.add)
                tt(half(E2[:, 1, :]), quarter(XH2, 0, 1), quarter(XH2, 1, 1), ALU.add)
                dve.drain()
                tt(LL, E2[:, 0, :], E2[:, 1, :], ALU.add)
                stage_end(dve, b, dve_at)
                v.memset(VT2[:, :, :, D2:SLOT], 0.0)
                v.memset(VT2[:, :, :, SLOT:64], 1.0)
                dve.wait_ge(v2_made, b + 1)
                for j in range(8):
                    v.tensor_copy(VT2[:, j, :, 0:D2],
                                  PS[:, 6 + j // 4, (j % 4) * C:(j % 4 + 1) * C].rearrange("p (h o) -> p h o", h=H2))
                for j in range(4):
                    dve.wait_ge(n2_sd, b * 4 + (j + 1))
                    v.tensor_scalar_max(SD2[:, chunk(j)], SD2[:, chunk(j)], 1e-12)
                    dve.drain()
                    v.reciprocal(SQ2[:, chunk(j)], SD2[:, chunk(j)])
                    dve.drain()
                    tt(QKN[:, chunk(j)], PS[:, j, :], SQ2[:, chunk(j)], ALU.mult)
                stage_end(dve, b, dve_at)
                for pr in range(H2 // 2):
                    for j in range(8):
                        i, z, t = j // 4, j // 2 % 2, j % 2
                        at = (64, 32)[z]
                        dve.wait_ge(s2_head, b * (8 * 4) + (8 * pr + j + 1))
                        low = (QS2, KS2)[z][i][at:at + 32, chunk(t)]
                        tt(low, PS[at:at + 32, j % 4, :], low, ALU.subtract).then_inc(s2_free, 1)
                    stage_end(dve, b, dve_at)
                    for t in range(1, 16, 2):
                        dve.wait_ge(t2_made, b * (16 * 4) + (16 * pr + t + 1))
                        v.tensor_scalar(SROW[:, t, :].rearrange("p (m n) -> p m n", m=2), PS[:, 6:8, :],
                                        float(D2) ** -0.5, None, ALU.mult).then_inc(t2_free_dve, 1)
                    v.memset(LO, LOWEST)
                    v.memset(STEP, RANGE / 2)
                    v.memset(MID, LOWEST + RANGE / 2)
                    v.memset(NMID, -(LOWEST + RANGE / 2)).then_inc(mid_ready, 1)
                    stage_end(dve, b, dve_at)
                    base = b * (4 * BISECTIONS) + pr * BISECTIONS
                    with dve.Fori(0, BISECTIONS) as n:
                        for t in range(8):
                            dve.wait_ge(dve_counted, base * 8 + n * 8 + (t + 1))
                            v.tensor_scalar(JUNK[t % 2], SROW[:, t, :], MID[:, t:t + 1], None, ALU.is_ge, ALU.add,
                                            accum_out=CNT[:, t:t + 1]).then_inc(dve_counted, 1)
                        dve.drain()
                        dve.wait_ge(act_counted, base * 8 + n * 8 + 10)
                        v.tensor_scalar(FL[:, 0:8], CNT[:, 0:8], KEEP - 0.5, STEP, ALU.is_ge, ALU.mult)
                        v.tensor_scalar(FL[:, 8:16], CNT[:, 8:16], 2.0 * KEEP - N2 - 0.5, STEP, ALU.is_ge, ALU.mult)
                        dve.drain()
                        tt(LO, LO, FL, ALU.add)
                        v.tensor_scalar(STEP, STEP, 0.5, None, ALU.mult)
                        dve.drain()
                        v.tensor_scalar(MID, LO, STEP, None, ALU.add)
                        dve.drain()
                        v.tensor_scalar(NMID, MID, -1.0, None, ALU.mult).then_inc(mid_ready, 1)
                    dve.drain().then_inc(found, 1)
                    for t in range(17):
                        if t < 16:
                            dve.wait_ge(e2_ready, b * (16 * 4) + (16 * pr + t + 1))
                            v.scalar_tensor_tensor(SROW[:, t, :], SROW[:, t, :], LO[:, t:t + 1], E2[:, t % 2, :],
                                                   ALU.is_ge, ALU.mult).then_inc(m2_ready, 1)
                        if t >= 1:
                            u = t - 1
                            dve.wait_ge(x2_made, b * (16 * 4) + (16 * pr + u + 1))
                            if u >= 2:
                                dve.wait_ge(pv2_done, b * (16 * 4) + (16 * pr + u - 1))
                            v.tensor_copy(PT2[:, u % 2, CH:2 * CH], PS[:, 2 * (u % 2) + 1, :]).then_inc(x2_free_dve, 1)
                    stage_end(dve, b, dve_at)
                    for i in range(2):
                        for t in range(2):
                            v.reciprocal(RC2[0:32, 2 * i + t, :], PS[32:64, 4 + 2 * i + t, :])
                    dve.drain()
                    for i in range(2):
                        h = 2 * pr + i
                        for t in range(2):
                            tt(O2[32 * (h % 4):32 * (h % 4) + 32, h // 4, chunk(t)], PS[0:32, 4 + 2 * i + t, :],
                               RC2[0:32, 2 * i + t, :], ALU.mult)
                    stage_end(dve, b, dve_at)

                def group_norm(g, tiles, stats, gamma, beta, factor=None):
                    dve.drain()
                    for i in range(tiles):
                        v.bn_aggr(MV[:, i, :], stats(i))
                    dve.drain()
                    v.tensor_copy(EX[:, 0:tiles, 0], MV[:, 0:tiles, 0])
                    tt(MSQ[:, 0:tiles], MV[:, 0:tiles, 0], MV[:, 0:tiles, 0], ALU.mult)
                    dve.drain()
                    tt(EX[:, 0:tiles, 1], MSQ[:, 0:tiles], MV[:, 0:tiles, 1], ALU.add).then_inc(gn_stats, 1)
                    dve.wait_ge(gn_sums, b * 5 + (g + 1))
                    v.tensor_copy(GM[:, 0:tiles, :], PS[:, 7, 0:2 * tiles].rearrange("p (t two) -> p t two", two=2))
                    dve.drain()
                    tt(MSQ[:, 0:tiles], GM[:, 0:tiles, 0], GM[:, 0:tiles, 0], ALU.mult)
                    dve.drain()
                    tt(VAR[:, 0:tiles], GM[:, 0:tiles, 1], MSQ[:, 0:tiles], ALU.subtract).then_inc(gn_var, 1)
                    dve.wait_ge(gn_sd, b * 5 + (g + 1))
                    v.reciprocal(RG[:, 0:tiles], SDG[:, 0:tiles])
                    dve.drain()
                    tt(SC(g)[:, 0:tiles], RG[:, 0:tiles], gamma, ALU.mult)
                    dve.drain()
                    tt(MSQ[:, 0:tiles], GM[:, 0:tiles, 0], SC(g)[:, 0:tiles], ALU.mult)
                    dve.drain()
                    tt(SH(g)[:, 0:tiles], beta, MSQ[:, 0:tiles], ALU.subtract)
                    dve.drain()
                    if factor is not None:
                        v.tensor_scalar(SC(g)[:, 0:tiles], SC(g)[:, 0:tiles], factor, None, ALU.mult)
                        v.tensor_scalar(SH(g)[:, 0:tiles], SH(g)[:, 0:tiles], factor, None, ALU.mult)
                    dve.drain().then_inc(gn_ready, 1)

                def stat(i, n):
                    return BST[:, i * 6 * n:(i + 1) * 6 * n].rearrange("p (c six) -> p c six", six=6)

                for t in range(2):
                    dve.wait_ge(o2_made, b * 2 + (t + 1))
                    v.bn_stats(BST[:, 6 * t:6 * t + 6], PS[:, t, :])
                group_norm(0, 1, lambda i: stat(i, 2), w("agn_g"), w("agn_b"))
                dve.wait_ge(ao_done, b + 1)
                tt(LL, LL, AO, ALU.add)
                for g in range(3):
                    v.memset(PAD[g], 0.0)
                dve.drain()
                dve.wait_ge(xh2_made, b + 1)
                q00, q10, q01, q11 = quarter(XHB, 0, 0), quarter(XHB, 1, 0), quarter(XHB, 0, 1), quarter(XHB, 1, 1)
                tt(half(TMPB[0]), q00, q10, ALU.add)
                tt(half(TMPB[1]), q01, q11, ALU.add)
                tt(half(TMPB[2]), q10, q00, ALU.subtract)
                tt(half(TMPB[3]), q11, q01, ALU.subtract)
                dve.drain()
                tt(inner(0), half(TMPB[1]), half(TMPB[0]), ALU.subtract)
                tt(inner(1), half(TMPB[2]), half(TMPB[3]), ALU.add)
                tt(inner(2), half(TMPB[3]), half(TMPB[2]), ALU.subtract)
                stage_end(dve, b, dve_at)
                for j in range(6):
                    dve.wait_ge(dw2_made, b * 6 + (j + 1))
                    v.bn_stats(BST[:, 6 * j:6 * j + 6], PS[:, j, :])
                group_norm(1, 3, lambda i: stat(i, 2), w("he1_g"), w("he1_b"))
                stage_end(dve, b, dve_at)
                for j in range(6):
                    dve.wait_ge(pw2_made, b * 6 + (j + 1))
                    v.bn_stats(BST[:, 6 * j:6 * j + 6], PS[:, j, :])
                group_norm(2, 3, lambda i: stat(i, 2), w("he2_g"), w("he2_b"), w("alpha"))
                for g in range(3):
                    dve.wait_ge(ho_made, b * 3 + (g + 1))
                    tt(half(HO[g]), half(HO[g]), inner(g), ALU.add)
                dve.drain()
                tt(TMP[0], LL, HO[2], ALU.add)
                tt(TMP[1], LL, HO[2], ALU.subtract)
                tt(TMP[2], HO[0], HO[1], ALU.add)
                tt(TMP[3], HO[0], HO[1], ALU.subtract)
                dve.drain()
                q = [area(56 + 4 * i, 4) for i in range(4)]
                tt(q[0], TMP[0], TMP[2], ALU.subtract)
                tt(q[1], TMP[1], TMP[3], ALU.subtract)
                tt(q[2], TMP[1], TMP[3], ALU.add)
                tt(q[3], TMP[0], TMP[2], ALU.add)
                dve.drain()
                for i, (r, c) in enumerate(((0, 0), (1, 0), (0, 1), (1, 1))):
                    v.scalar_tensor_tensor(quarter(X, r, c), half(q[i]), 0.1, quarter(X, r, c), ALU.mult, ALU.add)
                stage_end(dve, b, dve_at)
                for j in range(2 * NCH):
                    dve.wait_ge(u1_copied, b * (2 * NCH) + (j + 1))
                    v.bn_stats(BST[:, 6 * j:6 * j + 6], F1[:, j // NCH, chunk(j % NCH)])
                group_norm(3, 2, lambda i: stat(i, 8), w("f1_g"), w("f1_b"))
                for t in range(NCH):
                    dve.wait_ge(u2_copied, b * NCH + (t + 1))
                    v.bn_stats(BST[:, 6 * t:6 * t + 6], F2[:, chunk(t)])
                group_norm(4, 1, lambda i: stat(i, 8), w("f2_g"), w("f2_b"), 0.1)
                for t in range(NCH):
                    dve.wait_ge(u3_ready, b * NCH + (t + 1))
                    tt(X[:, chunk(t)], X[:, chunk(t)], F2[:, chunk(t)], ALU.add)
                stage_end(dve, b, dve_at)
                v.memset(HP, 0.0)
                dve.wait_ge(fl_made, b + 1)
                v.tensor_copy(FILT, PS[:, 6, 0:128]).then_inc(dve_link, 1)
                dve.wait_ge(dve_link, b + 1)
                for g in range(NCH):
                    dve.wait_ge(c3_made, b * NCH + (g + 1))
                    if g >= 2:
                        dve.wait_ge(i3_made, b * NCH + (g - 1))
                    tt(GC[:, g % 2, :].rearrange("p (q c) -> p q c", q=4), PS[:, 2 + g % 2, :].rearrange("p (q c) -> p q c", q=4),
                       FILT.rearrange("p (one c) -> p one c", one=1).to_broadcast([128, 4, 128]), ALU.mult).then_inc(c3_scaled, 1)
                stage_end(dve, b, dve_at)
                for g in range(NCH + 1):
                    if g < NCH:
                        dve.wait_ge(d3_gelu, b * NCH + (g + 1))
                        if g >= 2:
                            dve.wait_ge(o3_made, b * NCH + (g - 1))
                        v.scalar_tensor_tensor(G2[0:64, g % 2, :], PS[64:128, 6 + g % 2, :], w("b_dw2", 64),
                                               G1[0:64, g % 2, :], ALU.add, ALU.mult).then_inc(d3_gated, 1)
                    if g >= 1:
                        i = g - 1
                        dve.wait_ge(o3_made, b * NCH + (i + 1))
                        v.scalar_tensor_tensor(X[:, chunk(i)], PS[:, i % 2, :], w("b_out"), X[:, chunk(i)],
                                               ALU.add, ALU.add).then_inc(o3_free, 1)
                stage_end(dve, b, dve_at)
            assert dve_at[0] == STAGES


def _packed_constants():
    K = np.zeros((128, C_TOTAL), np.float32)

    def put(name, a):
        at, n = CCOLS[name]
        K[0:a.shape[0], at:at + n] = a
    i = np.arange(128)
    put("ident", np.eye(128))
    put("mean", np.full((128, 128), 1 / 128))
    ch = np.arange(384)
    g12 = (ch[:, None] // 12 == ch[None, :] // 12) / 12.0
    put("g12", g12.reshape(3, 128, 384).transpose(1, 0, 2).reshape(128, 9 * 128))
    put("g8", (i[:, None] // 8 == i[None, :] // 8) / 8.0)
    put("g4", (i[:, None] // 4 == i[None, :] // 4) / 4.0)
    put("bd16", (i[:, None] // D2 == i[None, :] // D2) * 1.0)
    sel = np.zeros((128, H2, 96))
    for h in range(H2):
        for d in range(D2):
            for s in range(3):
                sel[h * D2 + d, h, s * SLOT + d] = 1
    put("sel", sel.reshape(128, H2 * 96))
    r, c = np.meshgrid(np.arange(8), np.arange(8), indexing="ij")
    basis, scales = [], []
    for v in range(5):
        for u in range(8):
            if v in (0, 4) and u > 4:
                continue
            a = 2 * np.pi * (u * r + v * c) / 8
            f = np.zeros((8, 5))
            if v in (0, 4):
                f[u, v] += 0.5
                f[(8 - u) % 8, v] += 0.5
            else:
                f[u, v] = 1
            if v in (0, 4) and u in (0, 4):
                basis.append(np.cos(a) / 8)
                scales.append(f)
            else:
                basis += [np.cos(a) * np.sqrt(2) / 8, np.sin(a) * np.sqrt(2) / 8]
                scales += [f, f]
    dft = np.zeros((8, 2, 8, 2, 64))
    for p in range(2):
        dft[:, p, :, p, :] = np.stack(basis, -1)
    dft = dft.reshape(128, 128)
    put("dft", dft)
    put("idft", dft.T)
    put("msel", np.tile(np.stack(scales).reshape(64, 40).T, (1, 2)))
    return K


def kernel(**inputs):
    import concourse.bacc as bacc
    from concourse.bass_utils import run_bass_kernel_spmd

    a = {n: np.ascontiguousarray(v) for n, v in inputs.items()}
    Wp = np.zeros((128, W_TOTAL), np.float32)

    def put(name, v):
        at, n = WCOLS[name]
        v = v.reshape(-1, n)
        Wp[0:v.shape[0], at:at + n] = v

    def tiles(v):
        return v.reshape(-1, 128, v.shape[1]).transpose(1, 0, 2).reshape(128, -1)

    def cols(v):
        return v.reshape(-1, 128).T

    put("wt2", np.tile(a["L0_conv_Wt"].T, (1, 2)))
    put("wp2", np.tile(a["L0_conv_Wp"].T, (1, 2)))
    put("wg", a["L0_conv_Wg"].T)
    put("ww", a["L0_conv_Ww"].T)
    put("bt2", np.tile(a["L0_conv_bt"], 2)[:, None])
    put("bp2", np.tile(a["L0_conv_bp"], 2)[:, None])
    put("bg", a["L0_conv_bg"][None])
    put("bw", a["L0_conv_bw"][:, None])
    put("ln1w", a["L1_conv_ln1_w"][:, None])
    put("ln1b", a["L1_conv_ln1_b"][:, None])
    qkv = a["L1_conv_qkv_w"].reshape(3, H1, D1, C)
    for name, m in (("wq", 0), ("wk", 1)):
        put(name, np.tile(qkv[m].transpose(2, 0, 1)[:, :, None, :], (1, 1, 3, 1)).reshape(C, H1 * 96))
    put("wv", qkv[2].reshape(C, C).T)
    put("proj", a["L1_conv_proj_w"].T)
    put("projb", a["L1_conv_proj_b"][:, None])
    put("ln2w", a["L1_conv_ln2_w"][:, None])
    put("ln2b", a["L1_conv_ln2_b"][:, None])
    put("fc1", a["L1_conv_fc1_w"].T)
    put("fc1b", cols(a["L1_conv_fc1_b"]))
    put("fc2", tiles(a["L1_conv_fc2_w"].T))
    put("fc2b", a["L1_conv_fc2_b"][:, None])
    put("q2", a["L2_conv_qkv_w"].T)
    p2 = np.zeros((2, 4, SLOT, C), np.float32)
    p2[:, :, 0:D2, :] = a["L2_conv_proj_w"].T.reshape(2, 4, D2, C)
    put("proj2", tiles(p2.reshape(256, C)))
    put("agn_g", a["L2_conv_attn_gn_g"][:, None])
    put("agn_b", a["L2_conv_attn_gn_b"][:, None])
    put("he_dw", a["L2_conv_he_dw_w"].reshape(3, 128, 9).transpose(1, 0, 2).reshape(128, 27))
    for n, v in (("he1", "he_gn1"), ("he2", "he_gn2"), ("f1", "ffn_gn1"), ("f2", "ffn_gn2")):
        put(n + "_g", cols(a[f"L2_conv_{v}_g"]))
        put(n + "_b", cols(a[f"L2_conv_{v}_b"]))
    put("he_pw", tiles(a["L2_conv_he_pw_w"].T))
    put("alpha", np.broadcast_to(a["L2_conv_alpha"], (128, 1)))
    put("f1", a["L2_conv_ffn_w1"].T)
    put("f2", tiles(a["L2_conv_ffn_w2"].T))
    put("w_in", a["L3_conv_w_in"].T)
    put("b_in", a["L3_conv_b_in"][None])
    put("w_dw", a["L3_conv_w_dw"].reshape(128, 9))
    put("b_dw", a["L3_conv_b_dw"][:, None])
    put("b_dw2", a["L3_conv_b_dw"][64:, None])
    put("filt", a["L3_conv_fft_filter"].reshape(128, 40).T)
    put("w_out", a["L3_conv_w_out"].T)
    put("b_out", a["L3_conv_b_out"][:, None])

    nc = bacc.Bacc("TRN2", target_bir_lowering=False, num_devices=1)
    arrays = {"x_dram": a["x"].reshape(B, C, N), "weights_dram": Wp, "consts_dram": _packed_constants()}
    aps = [nc.dram_tensor(n, v.shape, FP32, kind="ExternalInput").ap() for n, v in arrays.items()]
    out = nc.dram_tensor("out_dram", (B, C, N), FP32, kind="ExternalOutput").ap()
    build(nc, *aps, out)
    r = run_bass_kernel_spmd(nc, [arrays], core_ids=[0])
    return r.results[0]["out_dram"].reshape(B, C, SIDE, SIDE)
```

```python
import concourse.bass as bass
from concourse import mybir
from contextlib import ExitStack
import numpy as np

FP32 = mybir.dt.float32
FP16 = mybir.dt.float16
ALU = mybir.AluOpType
ACT = mybir.ActivationFunctionType
AX = mybir.AxisListType

B, C, SIDE = 4, 128, 64
N = SIDE * SIDE
CH = 512
NCH = N // CH
BLK = 128
NBLK = N // BLK
IC = 64
H1, D1 = 4, 32
H2, D2 = 8, 16
N2 = 1024
S2 = 32
KEEP = N2 // 2
SLOT = 32

WCOLS, CCOLS = {}, {}


def _columns(table, spec):
    at = 0
    for name, n in spec:
        table[name] = (at, n)
        at += n
    return at


W_TOTAL = _columns(WCOLS, [
    ("wt2", 128), ("wp2", 128), ("wg", IC), ("ww", C), ("bt2", 1), ("bp2", 1), ("bg", IC), ("bw", 1),
    ("ln1w", 1), ("ln1b", 1), ("wq", H1 * 96), ("wk", H1 * 96), ("wv", C), ("proj", C), ("projb", 1),
    ("ln2w", 1), ("ln2b", 1), ("fc1", 256), ("fc1b", 2), ("fc2", 256), ("fc2b", 1),
    ("q2", 3 * C), ("proj2", 256), ("agn_g", 1), ("agn_b", 1), ("he_dw", 27), ("he1_g", 3), ("he1_b", 3),
    ("he_pw", 3 * 384), ("he2_g", 3), ("he2_b", 3), ("alpha", 1), ("f1", 256), ("f1_g", 2), ("f1_b", 2),
    ("f2", 256), ("f2_g", 1), ("f2_b", 1),
    ("w_in", C), ("b_in", C), ("w_dw", 9), ("b_dw", 1), ("b_dw2", 1), ("filt", C), ("w_out", C), ("b_out", 1),
])
C_TOTAL = _columns(CCOLS, [
    ("ident", 128), ("mean", 128), ("g12", 9 * 128), ("g8", 128), ("g4", 128), ("bd16", 128),
    ("sel", H2 * 96), ("dft", 128), ("idft", 128), ("msel", 128),
])


class Layer:

    def __init__(self, sem, name, units, o_buffers):
        self.units, self.o_buffers = units, o_buffers
        self.tile_scored = sem(name + "_tile_scored")
        self.tile_free = sem(name + "_tile_free")
        self.shift_split = sem(name + "_shift_split")
        self.shift_step = sem(name + "_shift_step")
        self.scored = sem(name + "_scored")
        self.p_ready = sem(name + "_p_ready")
        self.p_used = sem(name + "_p_used")
        self.o_free = sem(name + "_o_free")
        self.inverted = sem(name + "_inverted")
        self.divided = sem(name + "_divided")


TILES = 66
STEPS = NBLK
TILE_PLAN = [3] * 10 + [2] * 17 + [0] * 5
assert sum(TILE_PLAN) == 64 and len(TILE_PLAN) == STEPS


def build(nc, x, weights, consts, out, nb=B):
    nc.disable_value_cache = True
    ctx = ExitStack()
    with ctx:
        def sb(name, shape, dt=FP32):
            return ctx.enter_context(nc.sbuf_tensor(name, shape, dt))

        def sem(name):
            return ctx.enter_context(nc.semaphore(name))

        W = sb("W", [128, W_TOTAL])
        K = sb("K", [128, C_TOTAL])
        DG = sb("DG", [128, 36 * 128])
        XIN = sb("XIN", [128, N])
        X = sb("X", [128, N])
        SM = sb("SM", [128, 512])
        ARENA = sb("ARENA", [128, 31 * 1024])
        PS = ctx.enter_context(nc.psum_tensor("PS", [128, 8, CH], FP32))

        def w(name, p=128):
            a, n = WCOLS[name]
            return W[0:p, a:a + n]

        def k(name, p=128):
            a, n = CCOLS[name]
            return K[0:p, a:a + n]

        def area(kb, n_kb, dt=FP32):
            v = ARENA[:, kb * 256:(kb + n_kb) * 256]
            return v if dt == FP32 else v.bitcast(dt)

        def chunk(t):
            return slice(t * CH, (t + 1) * CH)

        QA, QB, KA, KB = (area(8 * i, 8, FP16) for i in range(4))
        GT = area(32, 16).rearrange("p (j o) -> p j o", j=NBLK)
        Y0, Z0 = (area(48 + 8 * i, 8).rearrange("p (c n) -> p c n", c=NCH // 2) for i in range(2))
        QS = [area(8 * h, 8, FP16) for h in range(H1)]
        KS = [area(32 + 8 * h, 8, FP16) for h in range(H1)]
        VT = area(64, 32).rearrange("p (j h o) -> p j h o", j=NBLK, h=H1)
        XLN = area(96, 16)
        O1 = XLN
        XC, SQ, SD, RS, XH = (area(4 * i, 4).rearrange("p (s n) -> p s n", s=2) for i in range(5))
        HID = area(0, 8).rearrange("p (s h n) -> p s h n", s=2, h=2)
        P = area(112, 8).rearrange("p (s n) -> p s n", s=2)
        RCP = area(120, 4).rearrange("p (i n) -> p i n", i=2)
        Z1 = XIN
        MX = SM[:, 0:64].rearrange("p (r m) -> p r m", r=8)
        NEG, N16 = SM[:, 64:72], SM[:, 72:76].bitcast(FP16)
        NHL = SM[:, 80:96].rearrange("p (r two) -> p r two", two=2)
        EPS5, EPS6 = SM[:, 96:97], SM[:, 97:98]
        ONE = SM[0:1, 128:256]

        XH2 = area(0, 16)
        SROW = area(0, 64).rearrange("p (t n) -> p t n", t=16)
        QS2 = [area(64 + 2 * i, 2, FP16) for i in range(2)]
        KS2 = [area(68 + 2 * i, 2, FP16) for i in range(2)]
        QKN = area(72, 8)
        VT2 = area(80, 16).rearrange("p (j h o) -> p j h o", j=8, h=H2)
        LL = area(96, 4)
        O2 = area(100, 8).rearrange("p (g n) -> p g n", g=2)
        Z2 = XIN[:, 0:2 * N2].rearrange("p (g n) -> p g n", g=2)
        E2 = area(108, 8).rearrange("p (s n) -> p s n", s=2)
        PT2 = area(116, 8).rearrange("p (s n) -> p s n", s=2)
        SQ2, SD2 = area(100, 8), area(108, 8)
        JUNK = [area(108 + 2 * i, 2, FP16) for i in range(4)]
        RC2 = area(116, 8).rearrange("p (g n) -> p g n", g=2)
        PADN = (S2 + 2) * (S2 + 2)
        PAD = [ARENA[:, g * PADN:(g + 1) * PADN] for g in range(3)]
        Y1 = [area(16 + 4 * g, 4) for g in range(3)]
        HO = [area(28 + 4 * g, 4) for g in range(3)]
        TMP = [area(40 + 4 * g, 4) for g in range(4)]
        XHB = area(56, 16)
        TMPB = [area(72 + 4 * g, 4) for g in range(4)]
        F1 = area(0, 32).rearrange("p (h n) -> p h n", h=2)
        F2 = area(32, 16)
        AO = area(40, 4)
        BST = SM[:, 256:352]
        MV, EX, GM = (SM[:, 352 + 6 * i:358 + 6 * i].rearrange("p (t two) -> p t two", two=2) for i in range(3))
        MSQ, VAR, SDG, RG = (SM[:, 370 + 3 * i:373 + 3 * i] for i in range(4))

        def SC(g):
            return SM[:, 384 + 6 * g:387 + 6 * g]

        def SH(g):
            return SM[:, 387 + 6 * g:390 + 6 * g]
        THR = SM[:, 416:432]
        BAD, BADSUM, FLAG = SM[:, 432:448], SM[:, 448:449], SM[0:1, 449:450].bitcast(mybir.dt.int32)
        IOTA8 = SM[:, 456:464]
        (LOW, HIGH, DLOW, DHIGH, MID, CNT, DEV, POS, NEGA, OUTW, NEXT, SPAN, RDEV, SEEN, IDX, STEP) = (
            ARENA[:, 120 * 256 + 16 * i:120 * 256 + 16 * i + 16] for i in range(16))
        BEST = ARENA[:, 121 * 256:121 * 256 + 128].rearrange("p (t e) -> p t e", e=8)
        M8J = ARENA[:, 122 * 256:122 * 256 + 128].rearrange("p (t e) -> p t e", e=8)
        JUNKF = area(116, 2, FP16)
        MK = [area(116, 4), area(108, 4)]
        HP = ARENA[:, 0:66 * 66].rearrange("p (r c) -> p r c", c=66)
        FILT = ARENA[:, 19 * 256:19 * 256 + 128]
        HT, GC, G1, G2, XP = (area(20 + 4 * i, 4).rearrange("p (s n) -> p s n", s=2) for i in range(5))

        def quarter(v, r, c):
            return v.rearrange("p (y a x b) -> p y a x b", y=S2, a=2, b=2)[:, :, r, :, c]

        def half(v):
            return v.rearrange("p (y x) -> p y x", x=S2)

        def inner(g):
            return PAD[g].rearrange("p (y x) -> p y x", x=S2 + 2)[:, 1:S2 + 1, 1:S2 + 1]

        loaded = sem("loaded")
        x_loaded = sem("x_loaded")
        xin_free = sem("xin_free")
        out_stored = sem("out_stored")
        setup_done = sem("setup_done")
        stage_done = sem("stage_done")
        wait_passed = sem("wait_passed")
        dve_link = sem("dve_link")
        L0 = Layer(sem, "L0", NCH // 2, 1)
        L1 = Layer(sem, "L1", 2 * NCH, 2)

        def events(*names):
            return [sem(n) for n in names]

        p0_made, p0_head, p0_free, g0_made, g0_free = events("p0_made", "p0_head", "p0_free", "g0_made", "g0_free")
        y0_made, y0_free = events("y0_made", "y0_free")
        ln_mean, ln_xc, ln_sq, ln_var, ln_sd, ln_rs, ln_xh, ln_out = events(
            "ln_mean", "ln_xc", "ln_sq", "ln_var", "ln_sd", "ln_rs", "ln_xh", "ln_out")
        p1_made, p1_head, p1_free, v1_made, v1_free = events("p1_made", "p1_head", "p1_free", "v1_made", "v1_free")
        pr_made, pr_free = events("pr_made", "pr_free")
        f1_made, f1_done, f2_made, f2_free = events("f1_made", "f1_done", "f2_made", "f2_free")
        xh_made, xh2_made = events("xh_made", "xh2_made")
        n2_made, n2_sq, n2_sum, n2_sd, n2_done, v2_made = events("n2_made", "n2_sq", "n2_sum", "n2_sd", "n2_done", "v2_made")
        s2_made, s2_head, s2_free = events("s2_made", "s2_head", "s2_free")
        t2_made, t2_free_act, t2_free_dve = events("t2_made", "t2_free_act", "t2_free_dve")
        mid_ready, act_counted, dve_counted, found = events("mid_ready", "act_counted", "dve_counted", "found")
        masked, best_made, bad_summed, bad_total = events("masked", "best_made", "bad_summed", "bad_total")
        e2_ready, m2_ready, x2_made, x2_free_act, x2_free_dve, pv2_done = events(
            "e2_ready", "m2_ready", "x2_made", "x2_free_act", "x2_free_dve", "pv2_done")
        gn_stats, gn_sums, gn_var, gn_sd, gn_ready = events("gn_stats", "gn_sums", "gn_var", "gn_sd", "gn_ready")
        o2_divided, o2_made, ao_done = events("o2_divided", "o2_made", "ao_done")
        dw2_made, pw2_made, ho_made = events("dw2_made", "pw2_made", "ho_made")
        u1_made, u1_copied, u2_ready, u2_made, u2_copied, u3_ready = events(
            "u1_made", "u1_copied", "u2_ready", "u2_made", "u2_copied", "u3_ready")
        (xp_made,) = events("xp_made")
        fl_made, h3_made, h3_copied, c3_made, c3_scaled, i3_made, i3_placed = events(
            "fl_made", "h3_made", "h3_copied", "c3_made", "c3_scaled", "i3_made", "i3_placed")
        d3_made, d3_gelu, d3_gated, o3_made, o3_free = events("d3_made", "d3_gelu", "d3_gated", "o3_made", "o3_free")
        EVALS = 7
        AIM = 4.5
        SLOPE = 0.0625 * 2.5066 / N2
        BISECTIONS = 26
        LOWEST, RANGE = -0.25 - 2.0 ** -12, 0.5 + 2.0 ** -11

        block = ctx.enter_context(nc.Block())
        STAGES = 37

        def stage_end(eng, b, at):
            at[0] += 1
            eng.drain().then_inc(stage_done, 1)
            eng.wait_ge(stage_done, b * (4 * STAGES) + 4 * at[0])
            eng.sem_inc(wait_passed, 1)

        @block.sync
        def _(sp):
            sp.sem_inc(out_stored, 16)
            sp.dma_start(W[:, :], weights).then_inc(loaded, 16)
            sp.dma_start(K[:, :], consts).then_inc(loaded, 16)
            with sp.Fori(0, nb) as b:
                sp.wait_ge(xin_free, b + 1)
                sp.sem_inc(wait_passed, 1)
                sp.dma_start(XIN[:, :], x[bass.ds(b, 1), :, :].rearrange("a p n -> (a p) n")).then_inc(x_loaded, 16)
                sp.wait_ge(stage_done, b * (4 * STAGES) + 4 * STAGES)
                sp.dma_start(out[bass.ds(b, 1), :, :].rearrange("a p n -> (a p) n"), X[:, :]).then_inc(out_stored, 16)
            sp.wait_ge(out_stored, 16 * nb + 16)

        @block.tensor
        def _(pe):
            mm = nc.tensor.matmul
            pe.sem_inc(L0.p_used, 2)
            pe.sem_inc(L1.p_used, 2)
            pe.wait_ge(loaded, 32)
            pe.wait_ge(setup_done, 2)

            def l0_tile(t, col):
                r, m = t // NCH, t % NCH
                rows = bass.ds(col + r * BLK, BLK)
                mm(PS[:, t % 2, :], QA[:, rows], KA[:, chunk(m)], start=True, stop=False)
                return mm(PS[:, t % 2, :], QB[0:66, rows], KB[0:66, chunk(m)], start=False, stop=True)

            def l0_scores(s, col):
                for i in range(2):
                    cols = bass.ds(col + i * CH, CH)
                    o = PS[:, 2 + 2 * (s % 2) + i, :]
                    mm(o, KA[:, s * BLK:(s + 1) * BLK], QA[:, cols], start=True, stop=False)
                    last = mm(o, KB[0:66, s * BLK:(s + 1) * BLK], QB[0:66, cols], start=False, stop=True)
                return last

            def l0_sums(s):
                for i in range(2):
                    last = mm(PS[:, 6 + i, :], GT[:, s, :], P[:, s % 2, chunk(i)],
                              start=(s == 0), stop=(s == STEPS - 1))
                return last

            def l1_tile(pair):
                def tile(t, col):
                    h, r, m = 2 * pair + t // 32, t // NCH % 4, t % NCH
                    return mm(PS[:, t % 2, :], QS[h][0:96, bass.ds(col + r * BLK, BLK)], KS[h][0:96, chunk(m)],
                              start=True, stop=True)
                return tile

            def l1_scores(pair):
                def scores(s, col):
                    for i in range(2):
                        h = 2 * pair + i
                        last = mm(PS[:, 2 + 2 * (s % 2) + i, :], KS[h][0:98, s * BLK:(s + 1) * BLK],
                                  QS[h][0:98, bass.ds(col, CH)], start=True, stop=True)
                    return last
                return scores

            def l1_sums(pair):
                def sums(s):
                    for i in range(2):
                        last = mm(PS[64 * i:64 * i + 64, 6 + pair, :], VT[:, s, 2 * pair + i, :],
                                  P[:, s % 2, chunk(i)], start=(s == 0), stop=(s == STEPS - 1))
                    return last
                return sums

            def unit(L, at, ua=None, a_tile=None, a_col=None, a_scores=None, ub=None, b_scores=None, b_col=None,
                     b_sums=None):
                t = 0
                for s in range(STEPS):
                    if ua is not None:
                        for _ in range(TILE_PLAN[s]):
                            pe.wait_ge(L.tile_free, ua * TILES + (t + 1))
                            a_tile(t, a_col).then_inc(L.tile_scored, 1)
                            t += 1
                        if s == STEPS - 2:
                            pe.wait_ge(L.shift_split, ua + 1)
                            for i in range(2):
                                pe.wait_ge(L.tile_free, ua * TILES + (65 + i))
                                for r in range(4):
                                    last = mm(PS[at:at + 2, i, r * BLK:(r + 1) * BLK], NHL[:, 4 * i + r, :], k("ident"),
                                              start=True, stop=True)
                                last.then_inc(L.tile_scored, 1)
                        if s == STEPS - 1:
                            pe.wait_ge(L.tile_free, ua * TILES + (TILES + 2))
                            pe.wait_ge(L.p_ready, ua * STEPS + 1)
                            a_scores(0, a_col).then_inc(L.scored, 1)
                    if ub is not None:
                        if s + 1 < STEPS:
                            pe.wait_ge(L.p_ready, ub * STEPS + (s + 2))
                            b_scores(s + 1, b_col).then_inc(L.scored, 1)
                        pe.wait_ge(L.p_ready, ub * STEPS + (s + 3))
                        if s == 0:
                            pe.wait_ge(L.o_free, ub + 1)
                        b_sums(s).then_inc(L.p_used, 1)

            pe_at = [0]
            with pe.Fori(0, nb) as b:
                pe.wait_ge(x_loaded, b * 16 + 16)
                for j in range(2 * NCH):
                    if j >= 4:
                        pe.wait_ge(p0_free, b * (2 * NCH) + (j - 3))
                    mm(PS[:, j % 4, :], w("wt2") if j % 2 == 0 else w("wp2"), XIN[:, chunk(j // 2)],
                       start=True, stop=True).then_inc(p0_made, 1)
                for j in range(NBLK):
                    o = PS[:, 4 + j // 8, (j % 8) * IC:(j % 8 + 1) * IC]
                    mm(o, XIN[:, j * BLK:(j + 1) * BLK], w("wg"), start=True, stop=False)
                    last = mm(o, ONE[:, 0:BLK], w("bg", 1), start=False, stop=True)
                    if j % 8 == 7:
                        last.then_inc(g0_made, 1)
                stage_end(pe, b, pe_at)
                a = dict(a_tile=l0_tile, a_scores=l0_scores)
                bb = dict(b_scores=l0_scores, b_sums=l0_sums)
                u0 = b * (NCH // 2)
                unit(L0, 64, ua=u0, a_col=0, **a)
                with pe.Fori(0, NCH // 2 - 1) as q:
                    unit(L0, 64, ua=u0 + q + 1, a_col=q * (2 * CH) + 2 * CH, ub=u0 + q, b_col=q * (2 * CH), **a, **bb)
                unit(L0, 64, ub=u0 + (NCH // 2 - 1), b_col=N - 2 * CH, **bb)
                stage_end(pe, b, pe_at)
                for t in range(NCH):
                    if t >= 2:
                        pe.wait_ge(y0_free, b * NCH + (t - 1))
                    pe.wait_ge(L0.divided, b * (NCH // 2) + (t // 2 + 1))
                    at = IC * (t % 2)
                    mm(PS[:, t % 2, :], w("ww")[at:at + IC, :], Y0[at:at + IC, t // 2, :],
                       start=True, stop=True).then_inc(y0_made, 1)
                stage_end(pe, b, pe_at)

                def layernorm(n):
                    base = b * (2 * NCH) + n * NCH
                    for t in range(NCH + 1):
                        if t < NCH:
                            if t >= 2:
                                pe.wait_ge(ln_xc, base + (t - 1))
                            mm(PS[:, t % 2, :], k("mean"), X[:, chunk(t)], start=True, stop=True).then_inc(ln_mean, 1)
                        if t >= 1:
                            pe.wait_ge(ln_sq, base + t)
                            if t >= 3:
                                pe.wait_ge(ln_sd, base + (t - 2))
                            mm(PS[:, 2 + (t - 1) % 2, :], k("mean"), SQ[:, (t - 1) % 2, :],
                               start=True, stop=True).then_inc(ln_var, 1)

                layernorm(0)
                stage_end(pe, b, pe_at)
                for j in range(2 * H1 * NCH):
                    h, t = j // 2 % H1, j // (2 * H1)
                    if j >= 4:
                        pe.wait_ge(p1_free, b * (2 * H1 * NCH) + (j - 3))
                    mm(PS[0:96, j % 4, :], w("wq" if j % 2 == 0 else "wk")[:, h * 96:(h + 1) * 96],
                       XLN[:, chunk(t)], start=True, stop=True).then_inc(p1_made, 1)
                for j in range(NBLK):
                    if j % 4 == 0 and j >= 16:
                        pe.wait_ge(v1_free, b * (NBLK // 4) + (j // 4 - 3))
                    last = mm(PS[:, 4 + j // 4 % 4, (j % 4) * C:(j % 4 + 1) * C], XLN[:, j * BLK:(j + 1) * BLK],
                              w("wv"), start=True, stop=True)
                    if j % 4 == 3:
                        last.then_inc(v1_made, 1)
                stage_end(pe, b, pe_at)
                u1 = b * (2 * NCH)

                def a1(p):
                    return dict(a_tile=l1_tile(p), a_scores=l1_scores(p))

                def b1(p):
                    return dict(b_scores=l1_scores(p), b_sums=l1_sums(p))

                unit(L1, 96, ua=u1, a_col=0, **a1(0))
                with pe.Fori(0, NCH - 1) as q:
                    unit(L1, 96, ua=u1 + q * 2 + 1, a_col=q * CH, **a1(1), ub=u1 + q * 2, b_col=q * CH, **b1(0))
                    unit(L1, 96, ua=u1 + q * 2 + 2, a_col=q * CH + CH, **a1(0), ub=u1 + q * 2 + 1, b_col=q * CH, **b1(1))
                unit(L1, 96, ua=u1 + (2 * NCH - 1), a_col=N - CH, **a1(1), ub=u1 + (2 * NCH - 2), b_col=N - CH, **b1(0))
                unit(L1, 96, ub=u1 + (2 * NCH - 1), b_col=N - CH, **b1(1))
                stage_end(pe, b, pe_at)
                for t in range(NCH):
                    if t >= 2:
                        pe.wait_ge(pr_free, b * NCH + (t - 1))
                    pe.wait_ge(L1.divided, b * NCH + (t + 1))
                    mm(PS[:, t % 2, :], w("proj"), O1[:, chunk(t)], start=True, stop=True).then_inc(pr_made, 1)
                stage_end(pe, b, pe_at)
                layernorm(1)
                stage_end(pe, b, pe_at)
                for t in range(NCH + 1):
                    if t < NCH:
                        for i in range(2):
                            if t >= 2:
                                pe.wait_ge(f1_done, b * (2 * NCH) + (2 * (t - 2) + i + 1))
                            mm(PS[:, 2 * (t % 2) + i, :], w("fc1")[:, i * 128:(i + 1) * 128], XLN[:, chunk(t)],
                               start=True, stop=True).then_inc(f1_made, 1)
                    if t >= 1:
                        pe.wait_ge(f1_done, b * (2 * NCH) + 2 * t)
                        if t >= 3:
                            pe.wait_ge(f2_free, b * NCH + (t - 2))
                        for i in range(2):
                            last = mm(PS[:, 4 + (t - 1) % 2, :], w("fc2")[:, i * 128:(i + 1) * 128],
                                      HID[:, (t - 1) % 2, i, :], start=(i == 0), stop=(i == 1))
                        last.then_inc(f2_made, 1)
                stage_end(pe, b, pe_at)
                stage_end(pe, b, pe_at)
                for j in range(4):
                    mm(PS[:, j, :], w("q2")[:, j // 2 * C:(j // 2 + 1) * C], LL[:, chunk(j % 2)],
                       start=True, stop=True).then_inc(n2_made, 1)
                for j in range(8):
                    last = mm(PS[:, 6 + j // 4, (j % 4) * C:(j % 4 + 1) * C], LL[:, j * BLK:(j + 1) * BLK],
                              w("q2")[:, 2 * C:3 * C], start=True, stop=True)
                last.then_inc(v2_made, 1)
                for j in range(4):
                    pe.wait_ge(n2_sq, b * 4 + (j + 1))
                    if j >= 2:
                        pe.wait_ge(n2_sd, b * 4 + (j - 1))
                    mm(PS[:, 4 + j % 2, :], k("bd16"), SQ2[:, chunk(j)], start=True, stop=True).then_inc(n2_sum, 1)
                stage_end(pe, b, pe_at)
                for pr in range(H2 // 2):
                    for j in range(8):
                        i, z, t = j // 4, j // 2 % 2, j % 2
                        if j >= 4:
                            pe.wait_ge(s2_free, b * (8 * 4) + (8 * pr + j - 3))
                        mm(PS[0:96, j % 4, :], k("sel")[:, (2 * pr + i) * 96:(2 * pr + i + 1) * 96],
                           QKN[:, z * N2 + t * CH:z * N2 + (t + 1) * CH], start=True, stop=True).then_inc(s2_made, 1)
                    stage_end(pe, b, pe_at)
                    for t in range(16):
                        if t >= 2:
                            pe.wait_ge(t2_free_act if t % 2 == 0 else t2_free_dve, b * (8 * 4) + (8 * pr + (t - 2) // 2 + 1))
                        for m in range(2):
                            last = mm(PS[:, 4 + 2 * (t % 2) + m, :], QS2[t // 8][0:96, t % 8 * BLK:(t % 8 + 1) * BLK],
                                      KS2[t // 8][0:96, chunk(m)], start=True, stop=True)
                        last.then_inc(t2_made, 1)
                    stage_end(pe, b, pe_at)
                    pe.wait_ge(bad_summed, b * 4 + (pr + 1))
                    mm(PS[0:1, 7, 0:1], BADSUM, k("mean")[:, 0:1], start=True, stop=True).then_inc(bad_total, 1)
                    stage_end(pe, b, pe_at)
                    for t in range(17):
                        if t < 16:
                            pe.wait_ge(m2_ready, b * (16 * 4) + (16 * pr + t + 1))
                            if t >= 2:
                                pe.wait_ge(x2_free_act, b * (16 * 4) + (16 * pr + t - 1))
                                pe.wait_ge(x2_free_dve, b * (16 * 4) + (16 * pr + t - 1))
                            for j in range(8):
                                last = nc.tensor.transpose(PS[:, 2 * (t % 2) + j // 4, (j % 4) * BLK:(j % 4 + 1) * BLK],
                                                           SROW[:, t, j * BLK:(j + 1) * BLK], k("ident"))
                            last.then_inc(x2_made, 1)
                        if t >= 1:
                            u = t - 1
                            i, r = u // 8, u % 8
                            pe.wait_ge(x2_free_act, b * (16 * 4) + (16 * pr + u + 1))
                            pe.wait_ge(x2_free_dve, b * (16 * 4) + (16 * pr + u + 1))
                            for j in range(8):
                                last = mm(PS[0:64, 4 + 2 * i + r // 4, (r % 4) * BLK:(r % 4 + 1) * BLK],
                                          VT2[:, j, 2 * pr + i, :], PT2[:, u % 2, j * BLK:(j + 1) * BLK],
                                          start=(j == 0), stop=(j == 7))
                            last.then_inc(pv2_done, 1)
                    stage_end(pe, b, pe_at)
                    stage_end(pe, b, pe_at)

                def group_sums(g, tiles, name):
                    pe.wait_ge(gn_stats, b * 5 + (g + 1))
                    for o in range(tiles):
                        n = tiles if name == "g12" else 1
                        for i in range(n):
                            gi = i if n > 1 else o
                            m = k(name)[:, gi * 384 + o * 128:gi * 384 + (o + 1) * 128] if n > 1 else k(name)
                            last = mm(PS[:, 7, 2 * o:2 * o + 2], m, EX[:, gi, :], start=(i == 0), stop=(i == n - 1))
                    last.then_inc(gn_sums, 1)

                pe.wait_ge(o2_divided, b + 1)
                for t in range(2):
                    for g in range(2):
                        last = mm(PS[:, t, :], w("proj2")[:, g * C:(g + 1) * C], O2[:, g, chunk(t)],
                                  start=(g == 0), stop=(g == 1))
                    last.then_inc(o2_made, 1)
                group_sums(0, 1, "g4")
                stage_end(pe, b, pe_at)
                for g in range(3):
                    for t in range(2):
                        for tap in range(9):
                            src = PAD[g].rearrange("p (y x) -> p y x", x=S2 + 2)[:, 16 * t + tap // 3:16 * t + tap // 3 + 16,
                                                                              tap % 3:tap % 3 + S2]
                            last = mm(PS[:, 2 * g + t, :].rearrange("p (y x) -> p y x", x=S2),
                                      DG[:, (9 * g + tap) * 128:(9 * g + tap + 1) * 128], src,
                                      start=(tap == 0), stop=(tap == 8))
                        last.then_inc(dw2_made, 1)
                group_sums(1, 3, "g12")
                stage_end(pe, b, pe_at)
                for o in range(3):
                    for t in range(2):
                        for g in range(3):
                            last = mm(PS[:, 2 * o + t, :], w("he_pw")[:, g * 384 + o * 128:g * 384 + (o + 1) * 128],
                                      Y1[g][:, chunk(t)], start=(g == 0), stop=(g == 2))
                        last.then_inc(pw2_made, 1)
                group_sums(2, 3, "g12")
                stage_end(pe, b, pe_at)
                for j in range(2 * NCH):
                    if j >= 4:
                        pe.wait_ge(u1_copied, b * (2 * NCH) + (j - 3))
                    mm(PS[:, j % 4, :], w("f1")[:, j // NCH * 128:(j // NCH + 1) * 128], X[:, chunk(j % NCH)],
                       start=True, stop=True).then_inc(u1_made, 1)
                group_sums(3, 2, "g8")
                for t in range(NCH):
                    pe.wait_ge(u2_ready, b * (2 * NCH) + (2 * t + 2))
                    if t >= 2:
                        pe.wait_ge(u2_copied, b * NCH + (t - 1))
                    for i in range(2):
                        last = mm(PS[:, 4 + t % 2, :], w("f2")[:, i * 128:(i + 1) * 128], F1[:, i, chunk(t)],
                                  start=(i == 0), stop=(i == 1))
                    last.then_inc(u2_made, 1)
                group_sums(4, 1, "g4")
                stage_end(pe, b, pe_at)
                mm(PS[:, 6, 0:128], k("msel", 40), w("filt", 40), start=True, stop=True).then_inc(fl_made, 1)
                for g in range(NCH + 2):
                    if g < NCH:
                        if g >= 2:
                            pe.wait_ge(h3_copied, b * NCH + (g - 1))
                        pe.wait_ge(xp_made, b * NCH + (g + 1))
                        for q in range(4):
                            o = PS[:, g % 2, q * 128:(q + 1) * 128]
                            mm(o, XP[:, g % 2, q * 128:(q + 1) * 128], w("w_in"), start=True, stop=False)
                            last = mm(o, ONE[:, 0:128], w("b_in", 1), start=False, stop=True)
                        last.then_inc(h3_made, 1)
                    if 1 <= g <= NCH:
                        i = g - 1
                        pe.wait_ge(h3_copied, b * NCH + (i + 1))
                        if i >= 2:
                            pe.wait_ge(c3_scaled, b * NCH + (i - 1))
                        mm(PS[:, 2 + i % 2, :], k("dft"), HT[:, i % 2, :], start=True, stop=True).then_inc(c3_made, 1)
                    if g >= 2:
                        i = g - 2
                        pe.wait_ge(c3_scaled, b * NCH + (i + 1))
                        if i >= 2:
                            pe.wait_ge(i3_placed, b * NCH + (i - 1))
                        for q in range(4):
                            last = mm(PS[:, 4 + i % 2, q * 128:(q + 1) * 128], GC[:, i % 2, q * 128:(q + 1) * 128],
                                      k("idft"), start=True, stop=True)
                        last.then_inc(i3_made, 1)
                stage_end(pe, b, pe_at)
                for g in range(NCH + 1):
                    if g < NCH:
                        if g >= 2:
                            pe.wait_ge(d3_gated, b * NCH + (g - 1))
                        for tap in range(9):
                            last = mm(PS[:, 6 + g % 2, :].rearrange("p (y x) -> p y x", x=SIDE),
                                      DG[:, (27 + tap) * 128:(28 + tap) * 128],
                                      HP[:, 8 * g + tap // 3:8 * g + tap // 3 + 8, tap % 3:tap % 3 + SIDE],
                                      start=(tap == 0), stop=(tap == 8))
                        last.then_inc(d3_made, 1)
                    if g >= 1:
                        i = g - 1
                        pe.wait_ge(d3_gated, b * NCH + (i + 1))
                        if i >= 2:
                            pe.wait_ge(o3_free, b * NCH + (i - 1))
                        mm(PS[:, i % 2, :], w("w_out", 64), G2[0:64, i % 2, :], start=True, stop=True).then_inc(o3_made, 1)
                stage_end(pe, b, pe_at)
            assert pe_at[0] == STAGES

        @block.scalar
        def _(act):
            go = nc.scalar.activation
            act.sem_inc(L0.p_ready, 2)
            act.sem_inc(L1.p_ready, 2)
            act.sem_inc(L0.o_free, L0.o_buffers)
            act.sem_inc(L1.o_free, L1.o_buffers)
            act.sem_inc(act_counted, 2)
            act.wait_ge(loaded, 32)
            act.wait_ge(setup_done, 2)

            def exps(L, u, scale, take=None):
                for s in range(STEPS):
                    act.wait_ge(L.scored, u * STEPS + (s + 1))
                    act.wait_ge(L.p_used, u * STEPS + (s + 1))
                    go(P[:, s % 2, :].rearrange("p (i n) -> p i n", i=2), PS[:, 2 + 2 * (s % 2):4 + 2 * (s % 2), :],
                       ACT.Exp, scale=scale).then_inc(L.p_ready, 1)
                    if s == 0 and take is not None:
                        take()

            def l0_take(u, c):
                act.wait_ge(L0.p_used, u * STEPS + (STEPS + 2))
                act.sem_inc(wait_passed, 1)
                for i in range(2):
                    for rows, to in ((0, Y0), (64, Z0)):
                        last = go(to[64 * i:64 * i + 64, bass.ds(c, 1), :].rearrange("p a n -> p (a n)"),
                                  PS[rows:rows + 64, 6 + i, :], ACT.Copy)
                last.then_inc(L0.o_free, 1)

            def l1_take(u, pair, col):
                act.wait_ge(L1.p_used, u * STEPS + (STEPS + 2))
                act.sem_inc(wait_passed, 1)
                for i in range(2):
                    h = 2 * pair + i
                    for rows, to in ((0, O1), (32, Z1)):
                        last = go(to[32 * h:32 * h + 32, bass.ds(col, CH)],
                                  PS[64 * i + rows:64 * i + rows + 32, 6 + pair, :], ACT.Copy)
                last.then_inc(L1.o_free, 1)

            act_at = [0]
            with act.Fori(0, nb) as b:
                for t in range(NCH):
                    act.wait_ge(p0_made, b * (2 * NCH) + (2 * t + 1))
                    go(QA[:, chunk(t)], PS[:, 2 * t % 4, :], ACT.Identity, bias=w("bt2")).then_inc(p0_head, 1)
                    act.wait_ge(p0_made, b * (2 * NCH) + (2 * t + 2))
                    go(KB[0:64, chunk(t)], PS[0:64, (2 * t + 1) % 4, :], ACT.Identity, bias=w("bp2", 64))
                    go(KA[:, chunk(t)], PS[:, (2 * t + 1) % 4, :], ACT.Identity, bias=w("bp2")).then_inc(p0_head, 1)
                stage_end(act, b, act_at)
                u0 = b * (NCH // 2)
                exps(L0, u0, 1.0)
                with act.Fori(1, NCH // 2) as q:
                    exps(L0, u0 + q, 1.0, lambda: l0_take(u0 + q - 1, q - 1))
                l0_take(u0 + (NCH // 2 - 1), NCH // 2 - 1)
                stage_end(act, b, act_at)
                stage_end(act, b, act_at)

                def layernorm(n):
                    base = b * (2 * NCH) + n * NCH
                    for t in range(NCH + 1):
                        if t < NCH:
                            act.wait_ge(ln_xc, base + (t + 1))
                            if t >= 2:
                                act.wait_ge(ln_var, base + (t - 1))
                            go(SQ[:, t % 2, :], XC[:, t % 2, :], ACT.Square).then_inc(ln_sq, 1)
                        if t >= 1:
                            act.wait_ge(ln_var, base + t)
                            if t >= 3:
                                act.wait_ge(ln_rs, base + (t - 2))
                            go(SD[:, (t - 1) % 2, :], PS[:, 2 + (t - 1) % 2, :], ACT.Sqrt, bias=EPS5).then_inc(ln_sd, 1)

                layernorm(0)
                stage_end(act, b, act_at)
                for j in range(2 * H1 * NCH):
                    h, t = j // 2 % H1, j // (2 * H1)
                    act.wait_ge(p1_made, b * (2 * H1 * NCH) + (j + 1))
                    go((QS if j % 2 == 0 else KS)[h][0:96, chunk(t)], PS[0:96, j % 4, :], ACT.Copy).then_inc(p1_head, 1)
                stage_end(act, b, act_at)
                u1, scale = b * (2 * NCH), float(D1) ** -0.5
                exps(L1, u1, scale)
                exps(L1, u1 + 1, scale, lambda: l1_take(u1, 0, 0))
                with act.Fori(1, NCH) as q:
                    exps(L1, u1 + q * 2, scale, lambda: l1_take(u1 + q * 2 - 1, 1, q * CH - CH))
                    exps(L1, u1 + q * 2 + 1, scale, lambda: l1_take(u1 + q * 2, 0, q * CH))
                l1_take(u1 + (2 * NCH - 1), 1, N - CH)
                stage_end(act, b, act_at)
                stage_end(act, b, act_at)
                layernorm(1)
                stage_end(act, b, act_at)
                for t in range(NCH):
                    for i in range(2):
                        act.wait_ge(f1_made, b * (2 * NCH) + (2 * t + i + 1))
                        if t >= 2:
                            act.wait_ge(f2_made, b * NCH + (t - 1))
                        go(HID[:, t % 2, i, :], PS[:, 2 * (t % 2) + i, :], ACT.Gelu,
                           bias=w("fc1b")[:, i:i + 1]).then_inc(f1_done, 1)
                stage_end(act, b, act_at)
                go(XH2, X[:, :], ACT.Copy, scale=0.5).then_inc(xh_made, 1)
                stage_end(act, b, act_at)
                for j in range(4):
                    act.wait_ge(n2_made, b * 4 + (j + 1))
                    go(SQ2[:, chunk(j)], PS[:, j, :], ACT.Square).then_inc(n2_sq, 1)
                for j in range(4):
                    act.wait_ge(n2_sum, b * 4 + (j + 1))
                    go(SD2[:, chunk(j)], PS[:, 4 + j % 2, :], ACT.Sqrt).then_inc(n2_sd, 1)
                stage_end(act, b, act_at)
                for pr in range(H2 // 2):
                    for j in range(8):
                        i, z, t = j // 4, j // 2 % 2, j % 2
                        act.wait_ge(s2_made, b * (8 * 4) + (8 * pr + j + 1))
                        go((QS2, KS2)[z][i][0:96, chunk(t)], PS[0:96, j % 4, :], ACT.Copy).then_inc(s2_head, 1)
                    stage_end(act, b, act_at)
                    for t in range(0, 16, 2):
                        act.wait_ge(t2_made, b * (16 * 4) + (16 * pr + t + 1))
                        go(SROW[:, t, :].rearrange("p (m n) -> p m n", m=2), PS[:, 4:6, :], ACT.Copy,
                           scale=float(D2) ** -0.5, accum_out=CNT[:, t:t + 1]).then_inc(t2_free_act, 1)
                    stage_end(act, b, act_at)
                    counted = b * (4 * (8 * EVALS + 16)) + pr * (8 * EVALS + 16)
                    with act.Fori(0, EVALS) as n:
                        act.wait_ge(mid_ready, b * (4 * (EVALS + 1)) + n + (pr * (EVALS + 1) + 1))
                        for t in range(8):
                            act.wait_ge(act_counted, counted + n * 8 + (t + 1))
                            go(JUNK[2 + t % 2], SROW[:, 8 + t, :], ACT.Sign, bias=MID[:, 8 + t:9 + t], scale=-1.0,
                               accum_out=CNT[:, 8 + t:9 + t]).then_inc(act_counted, 1)
                    for t in range(16):
                        act.wait_ge(found, b * 64 + (16 * pr + t + 1))
                        act.wait_ge(act_counted, counted + (8 * EVALS + t + 1))
                        go(JUNK[2 + t % 2], SROW[:, t, :], ACT.Sign, bias=THR[:, t:t + 1], scale=-1.0,
                           accum_out=SEEN[:, t:t + 1]).then_inc(act_counted, 1)
                    stage_end(act, b, act_at)
                    for t in range(17):
                        if t < 16:
                            if t >= 2:
                                act.wait_ge(m2_ready, b * (16 * 4) + (16 * pr + t - 1))
                            go(E2[:, t % 2, :], SROW[:, t, :], ACT.Exp).then_inc(e2_ready, 1)
                        if t >= 1:
                            u = t - 1
                            act.wait_ge(x2_made, b * (16 * 4) + (16 * pr + u + 1))
                            if u >= 2:
                                act.wait_ge(pv2_done, b * (16 * 4) + (16 * pr + u - 1))
                            go(PT2[:, u % 2, 0:CH], PS[:, 2 * (u % 2), :], ACT.Copy).then_inc(x2_free_act, 1)
                    stage_end(act, b, act_at)
                    for i in range(2):
                        h = 2 * pr + i
                        go(O2[32 * (h % 4):32 * (h % 4) + 32, h // 4, :].rearrange("p (t n) -> p t n", t=2),
                           PS[0:32, 4 + 2 * i:6 + 2 * i, :], ACT.Copy)
                    stage_end(act, b, act_at)

                def group_sd(g, tiles):
                    act.wait_ge(gn_var, b * 5 + (g + 1))
                    go(SDG[:, 0:tiles], VAR[:, 0:tiles], ACT.Sqrt, bias=EPS6).then_inc(gn_sd, 1)

                group_sd(0, 1)
                act.wait_ge(gn_ready, b * 5 + 1)
                go(AO.rearrange("p (t n) -> p t n", t=2), PS[:, 0:2, :], ACT.Identity,
                   bias=SH(0)[:, 0:1], scale=SC(0)[:, 0:1]).then_inc(ao_done, 1)
                go(XHB, X[:, :], ACT.Copy, scale=0.5).then_inc(xh2_made, 1)
                stage_end(act, b, act_at)
                group_sd(1, 3)
                act.wait_ge(gn_ready, b * 5 + 2)
                for g in range(3):
                    go(Y1[g].rearrange("p (t n) -> p t n", t=2), PS[:, 2 * g:2 * g + 2, :], ACT.Silu,
                       bias=SH(1)[:, g:g + 1], scale=SC(1)[:, g:g + 1])
                stage_end(act, b, act_at)
                group_sd(2, 3)
                act.wait_ge(gn_ready, b * 5 + 3)
                for g in range(3):
                    go(HO[g].rearrange("p (t n) -> p t n", t=2), PS[:, 2 * g:2 * g + 2, :], ACT.Identity,
                       bias=SH(2)[:, g:g + 1], scale=SC(2)[:, g:g + 1]).then_inc(ho_made, 1)
                stage_end(act, b, act_at)
                for j in range(2 * NCH):
                    act.wait_ge(u1_made, b * (2 * NCH) + (j + 1))
                    go(F1[:, j // NCH, chunk(j % NCH)], PS[:, j % 4, :], ACT.Copy).then_inc(u1_copied, 1)
                group_sd(3, 2)
                act.wait_ge(gn_ready, b * 5 + 4)
                for t in range(NCH):
                    for i in range(2):
                        go(F1[:, i, chunk(t)], F1[:, i, chunk(t)], ACT.Gelu, bias=SH(3)[:, i:i + 1],
                           scale=SC(3)[:, i:i + 1]).then_inc(u2_ready, 1)
                for t in range(NCH):
                    act.wait_ge(u2_made, b * NCH + (t + 1))
                    go(F2[:, chunk(t)], PS[:, 4 + t % 2, :], ACT.Copy).then_inc(u2_copied, 1)
                group_sd(4, 1)
                act.wait_ge(gn_ready, b * 5 + 5)
                for t in range(NCH):
                    go(F2[:, chunk(t)], F2[:, chunk(t)], ACT.Identity, bias=SH(4)[:, 0:1],
                       scale=SC(4)[:, 0:1]).then_inc(u3_ready, 1)
                stage_end(act, b, act_at)
                for g in range(NCH + 1):
                    if g < NCH:
                        act.wait_ge(h3_made, b * NCH + (g + 1))
                        if g >= 2:
                            act.wait_ge(c3_made, b * NCH + (g - 1))
                        go(HT[:, g % 2, :], PS[:, g % 2, :], ACT.Copy).then_inc(h3_copied, 1)
                    if g >= 1:
                        i = g - 1
                        act.wait_ge(i3_made, b * NCH + (i + 1))
                        go(HP[:, 8 * i + 1:8 * i + 9, 1:SIDE + 1].rearrange("p r (q c) -> p r q c", q=4),
                           PS[:, 4 + i % 2, :].rearrange("p (q r c) -> p r q c", q=4, r=8), ACT.Copy).then_inc(i3_placed, 1)
                stage_end(act, b, act_at)
                for g in range(NCH):
                    act.wait_ge(d3_made, b * NCH + (g + 1))
                    if g >= 2:
                        act.wait_ge(d3_gated, b * NCH + (g - 1))
                    go(G1[0:64, g % 2, :], PS[0:64, 6 + g % 2, :], ACT.Gelu, bias=w("b_dw", 64)).then_inc(d3_gelu, 1)
                stage_end(act, b, act_at)
            assert act_at[0] == STAGES

        @block.gpsimd
        def _(pool):
            pool.sem_inc(xin_free, 1)
            pool.wait_ge(loaded, 32)
            for i in range(36):
                col = w("he_dw")[:, i:i + 1] if i < 27 else w("w_dw")[:, i - 27:i - 26]
                nc.gpsimd.tensor_scalar(DG[:, i * 128:(i + 1) * 128], k("ident"), col, None, ALU.mult)
            pool.drain().then_inc(setup_done, 1)
            pool_at = [0]
            with pool.Fori(0, nb) as b:
                stage_end(pool, b, pool_at)
                stage_end(pool, b, pool_at)
                stage_end(pool, b, pool_at)
                for n in range(4, 10):
                    if n in (4, 8):
                        base = b * (2 * NCH) + (n == 8) * NCH
                        for t in range(NCH):
                            pool.wait_ge(ln_xh, base + (t + 1))
                            pool.sem_inc(wait_passed, 1)
                            nc.gpsimd.tensor_scalar(XLN[:, chunk(t)], XH[:, t % 2, :], w("ln1w" if n == 4 else "ln2w"),
                                                    w("ln1b" if n == 4 else "ln2b"), ALU.mult, ALU.add).then_inc(ln_out, 1)
                    stage_end(pool, b, pool_at)
                for n in range(10, STAGES + 1):
                    if n == STAGES - 1:
                        for g in range(NCH):
                            if g >= 2:
                                pool.wait_ge(h3_made, b * NCH + (g - 1))
                                pool.sem_inc(wait_passed, 1)
                            nc.gpsimd.tensor_copy(
                                XP[:, g % 2, :].rearrange("p (q r c) -> p r q c", q=4, r=8),
                                X[:, chunk(g)].rearrange("p (r q c) -> p r q c", r=8, q=4)).then_inc(xp_made, 1)
                    stage_end(pool, b, pool_at)
            assert pool_at[0] == STAGES

        @block.vector
        def _(dve):
            v = nc.vector
            dve.sem_inc(L0.tile_free, 2)
            dve.sem_inc(L1.tile_free, 2)
            dve.sem_inc(dve_counted, 2)
            v.memset(EPS5, 1e-5)
            v.memset(EPS6, 1e-6)
            v.memset(ONE, 1.0)
            for i in range(8):
                v.memset(IOTA8[:, i:i + 1], float(i))
            dve.drain().then_inc(setup_done, 1)
            dve.wait_ge(loaded, 32)

            def maxima(L, u, at, rows_to):
                for t in range(64):
                    dve.wait_ge(L.tile_scored, u * TILES + (t + 1))
                    v.tensor_reduce(MX[:, t // 8, t % 8:t % 8 + 1], PS[:, t % 2, :], AX.X, ALU.max).then_inc(L.tile_free, 1)
                dve.wait_ge(L.tile_free, u * TILES + 66)
                v.tensor_reduce(NEG, MX, AX.X, ALU.max, negate=True).then_inc(L.shift_step, 1)
                dve.wait_ge(L.shift_step, u * 3 + 1)
                v.tensor_copy(N16, NEG).then_inc(L.shift_step, 1)
                dve.wait_ge(L.shift_step, u * 3 + 2)
                v.tensor_copy(NHL[:, :, 0], N16).then_inc(L.shift_step, 1)
                dve.wait_ge(L.shift_step, u * 3 + 3)
                v.tensor_tensor(NHL[:, :, 1], NEG, NHL[:, :, 0], ALU.subtract).then_inc(L.shift_split, 1)
                for i in range(2):
                    dve.wait_ge(L.tile_scored, u * TILES + (65 + i))
                    v.tensor_copy(rows_to(i), PS[at:at + 2, i, :]).then_inc(L.tile_free, 1)

            def l0_maxima(u, col):
                maxima(L0, u, 64, lambda i: QB[64:66, bass.ds(col + i * CH, CH)])

            def l1_maxima(u, pair, col):
                maxima(L1, u, 96, lambda i: QS[2 * pair + i][96:98, bass.ds(col, CH)])

            def divide(L, t, base, sums, totals):
                if t >= 2:
                    dve.wait_ge(L.divided, base + (t - 1))
                v.reciprocal(RCP[:, t % 2, :], totals).then_inc(L.inverted, 1)
                dve.wait_ge(L.inverted, base + (t + 1))
                v.tensor_tensor(sums, sums, RCP[:, t % 2, :], ALU.mult).then_inc(L.divided, 1)

            dve_at = [0]
            with dve.Fori(0, nb) as b:
                for t in range(NCH):
                    for i in range(2):
                        j = 2 * t + i
                        dve.wait_ge(p0_head, b * (2 * NCH) + (j + 1))
                        if i == 0:
                            v.scalar_tensor_tensor(QB[0:64, chunk(t)], PS[0:64, j % 4, :], w("bt2", 64), QA[0:64, chunk(t)],
                                                   ALU.add, ALU.subtract).then_inc(p0_free, 1)
                        else:
                            v.scalar_tensor_tensor(KA[64:128, chunk(t)], PS[64:128, j % 4, :], w("bp2")[64:128, :],
                                                   KA[64:128, chunk(t)], ALU.add, ALU.subtract).then_inc(p0_free, 1)
                v.memset(GT[:, :, IC:128], 1.0)
                v.memset(QB[64:66, :], 0.0)
                v.memset(KB[64:66, :], 1.0)
                for j in range(4):
                    dve.wait_ge(g0_made, b * 4 + (j + 1))
                    v.tensor_copy(GT[:, 8 * j:8 * j + 8, 0:IC], PS[:, 4 + j, :].rearrange("p (j o) -> p j o", o=IC))
                stage_end(dve, b, dve_at)
                u0 = b * (NCH // 2)
                l0_maxima(u0, 0)
                with dve.Fori(0, NCH // 2 - 1) as q:
                    l0_maxima(u0 + q + 1, q * (2 * CH) + 2 * CH)
                stage_end(dve, b, dve_at)
                dve.wait_ge(out_stored, b * 16 + 16)
                for c in range(NCH // 2):
                    divide(L0, c, b * (NCH // 2), Y0[:, c, :], Z0[:, c, :])
                for t in range(NCH):
                    dve.wait_ge(y0_made, b * NCH + (t + 1))
                    v.scalar_tensor_tensor(X[:, chunk(t)], PS[:, t % 2, :], w("bw"), XIN[:, chunk(t)],
                                           ALU.add, ALU.add).then_inc(y0_free, 1)
                stage_end(dve, b, dve_at)

                def layernorm(n):
                    base = b * (2 * NCH) + n * NCH
                    for t in range(NCH + 1):
                        if t < NCH:
                            dve.wait_ge(ln_mean, base + (t + 1))
                            if t >= 2:
                                dve.wait_ge(ln_xh, base + (t - 1))
                            v.tensor_tensor(XC[:, t % 2, :], X[:, chunk(t)], PS[:, t % 2, :], ALU.subtract).then_inc(ln_xc, 1)
                        if t >= 1:
                            i = (t - 1) % 2
                            dve.wait_ge(ln_sd, base + t)
                            v.reciprocal(RS[:, i, :], SD[:, i, :]).then_inc(ln_rs, 1)
                            dve.wait_ge(ln_rs, base + t)
                            if t >= 3:
                                dve.wait_ge(ln_out, base + (t - 2))
                            v.tensor_tensor(XH[:, i, :], XC[:, i, :], RS[:, i, :], ALU.mult).then_inc(ln_xh, 1)

                layernorm(0)
                stage_end(dve, b, dve_at)
                for j in range(2 * H1 * NCH):
                    h, t = j // 2 % H1, j // (2 * H1)
                    at, to = (64, QS) if j % 2 == 0 else (32, KS)
                    dve.wait_ge(p1_head, b * (2 * H1 * NCH) + (j + 1))
                    low = to[h][at:at + 32, chunk(t)]
                    v.tensor_tensor(low, PS[at:at + 32, j % 4, :], low, ALU.subtract).then_inc(p1_free, 1)
                for h in range(H1):
                    v.memset(QS[h][96:98, :], 0.0)
                    v.memset(KS[h][96:98, :], 1.0)
                v.memset(VT[:, :, :, 32:64], 1.0)
                for j in range(NBLK // 4):
                    dve.wait_ge(v1_made, b * (NBLK // 4) + (j + 1))
                    for i in range(4):
                        last = v.tensor_copy(VT[:, 4 * j + i, :, 0:32],
                                             PS[:, 4 + j % 4, i * C:(i + 1) * C].rearrange("p (h o) -> p h o", h=H1))
                    last.then_inc(v1_free, 1)
                stage_end(dve, b, dve_at)
                u1 = b * (2 * NCH)
                l1_maxima(u1, 0, 0)
                with dve.Fori(0, NCH - 1) as q:
                    l1_maxima(u1 + q * 2 + 1, 1, q * CH)
                    l1_maxima(u1 + q * 2 + 2, 0, q * CH + CH)
                l1_maxima(u1 + (2 * NCH - 1), 1, N - CH)
                stage_end(dve, b, dve_at)
                for t in range(NCH + 1):
                    if t < NCH:
                        divide(L1, t, b * NCH, O1[:, chunk(t)], Z1[:, chunk(t)])
                    if t == 0:
                        continue
                    t -= 1
                    dve.wait_ge(pr_made, b * NCH + (t + 1))
                    v.scalar_tensor_tensor(X[:, chunk(t)], PS[:, t % 2, :], w("projb"), X[:, chunk(t)],
                                           ALU.add, ALU.add).then_inc(pr_free, 1)
                stage_end(dve, b, dve_at)
                layernorm(1)
                stage_end(dve, b, dve_at)
                for t in range(NCH):
                    dve.wait_ge(f2_made, b * NCH + (t + 1))
                    v.scalar_tensor_tensor(X[:, chunk(t)], PS[:, 4 + t % 2, :], w("fc2b"), X[:, chunk(t)],
                                           ALU.add, ALU.add).then_inc(f2_free, 1)
                stage_end(dve, b, dve_at)
                dve.wait_ge(xh_made, b + 1)
                tt = v.tensor_tensor
                tt(half(E2[:, 0, :]), quarter(XH2, 0, 0), quarter(XH2, 1, 0), ALU.add)
                tt(half(E2[:, 1, :]), quarter(XH2, 0, 1), quarter(XH2, 1, 1), ALU.add)
                dve.drain()
                tt(LL, E2[:, 0, :], E2[:, 1, :], ALU.add)
                stage_end(dve, b, dve_at)
                v.memset(VT2[:, :, :, D2:SLOT], 0.0)
                v.memset(VT2[:, :, :, SLOT:64], 1.0)
                dve.wait_ge(v2_made, b + 1)
                for j in range(8):
                    v.tensor_copy(VT2[:, j, :, 0:D2],
                                  PS[:, 6 + j // 4, (j % 4) * C:(j % 4 + 1) * C].rearrange("p (h o) -> p h o", h=H2))
                for j in range(4):
                    dve.wait_ge(n2_sd, b * 4 + (j + 1))
                    v.tensor_scalar_max(SD2[:, chunk(j)], SD2[:, chunk(j)], 1e-12)
                    dve.drain()
                    v.reciprocal(SQ2[:, chunk(j)], SD2[:, chunk(j)])
                    dve.drain()
                    tt(QKN[:, chunk(j)], PS[:, j, :], SQ2[:, chunk(j)], ALU.mult)
                stage_end(dve, b, dve_at)
                for pr in range(H2 // 2):
                    for j in range(8):
                        i, z, t = j // 4, j // 2 % 2, j % 2
                        at = (64, 32)[z]
                        dve.wait_ge(s2_head, b * (8 * 4) + (8 * pr + j + 1))
                        low = (QS2, KS2)[z][i][at:at + 32, chunk(t)]
                        tt(low, PS[at:at + 32, j % 4, :], low, ALU.subtract).then_inc(s2_free, 1)
                    stage_end(dve, b, dve_at)
                    for t in range(1, 16, 2):
                        dve.wait_ge(t2_made, b * (16 * 4) + (16 * pr + t + 1))
                        v.tensor_scalar(SROW[:, t, :].rearrange("p (m n) -> p m n", m=2), PS[:, 6:8, :],
                                        float(D2) ** -0.5, None, ALU.mult, ALU.add,
                                        accum_out=CNT[:, t:t + 1]).then_inc(t2_free_dve, 1)
                    v.memset(LOW, LOWEST)
                    v.memset(HIGH, -LOWEST)
                    v.memset(DLOW, N2 - KEEP + AIM)
                    v.memset(DHIGH, AIM - KEEP)
                    stage_end(dve, b, dve_at)
                    v.tensor_scalar(MID, CNT, 1.0 / N2, None, ALU.mult).then_inc(mid_ready, 1)
                    dve.drain()
                    counted = b * (4 * 8 * EVALS) + pr * (8 * EVALS)

                    def count(n):
                        for t in range(8):
                            dve.wait_ge(dve_counted, counted + n * 8 + (t + 1))
                            v.tensor_scalar(JUNK[t % 2], SROW[:, t, :], MID[:, t:t + 1], None, ALU.is_ge, ALU.add,
                                            accum_out=CNT[:, t:t + 1]).then_inc(dve_counted, 1)
                        dve.drain()
                        dve.wait_ge(act_counted, b * (4 * (8 * EVALS + 16)) + n * 8 + (pr * (8 * EVALS + 16) + 10))
                        v.tensor_scalar(DEV[:, 0:8], CNT[:, 0:8], AIM - KEEP, None, ALU.add)
                        v.tensor_scalar(DEV[:, 8:16], CNT[:, 8:16], -0.5, AIM, ALU.mult, ALU.add)
                        dve.drain()

                    def bracket():
                        v.tensor_scalar(POS, DEV, 0.0, None, ALU.is_ge)
                        v.tensor_scalar(NEGA, DEV, 0.0, None, ALU.is_lt)
                        tt(OUTW, DEV, DEV, ALU.mult)
                        dve.drain()
                        v.tensor_scalar(OUTW, OUTW, 3.6 ** 2, None, ALU.is_gt)
                        for mask, end, dev in ((POS, LOW, DLOW), (NEGA, HIGH, DHIGH)):
                            v.copy_predicated(end, mask.bitcast(mybir.dt.int32), MID)
                            v.copy_predicated(dev, mask.bitcast(mybir.dt.int32), DEV)
                        dve.drain()

                    count(0)
                    bracket()
                    v.tensor_scalar(SPAN, POS, 6.0, -3.0, ALU.mult, ALU.add)
                    dve.drain()
                    tt(SPAN, SPAN, DEV, ALU.add)
                    dve.drain()
                    v.scalar_tensor_tensor(NEXT, SPAN, SLOPE, MID, ALU.mult, ALU.add)
                    dve.drain()
                    v.copy_predicated(MID, OUTW.bitcast(mybir.dt.int32), NEXT).then_inc(mid_ready, 1)
                    dve.drain()
                    with dve.Fori(1, EVALS) as n:
                        count(n)
                        bracket()
                        tt(RDEV, DLOW, DHIGH, ALU.subtract)
                        tt(SPAN, HIGH, LOW, ALU.subtract)
                        dve.drain()
                        v.reciprocal(RDEV, RDEV)
                        tt(SPAN, SPAN, DLOW, ALU.mult)
                        v.tensor_scalar(IDX, DEV, -1.0, 3.5 - 0.25, ALU.mult, ALU.add)
                        dve.drain()
                        tt(SPAN, SPAN, RDEV, ALU.mult)
                        v.tensor_scalar(IDX, IDX, 1.5 * 2.0 ** 23, -1.5 * 2.0 ** 23, ALU.add, ALU.add)
                        dve.drain()
                        tt(NEXT, SPAN, LOW, ALU.add)
                        dve.drain()
                        v.tensor_copy(NEGA, MID)
                        dve.drain()
                        v.copy_predicated(MID, OUTW.bitcast(mybir.dt.int32), NEXT).then_inc(mid_ready, 1)
                        dve.drain()
                    for t in range(18):
                        if t < 16:
                            if t >= 2:
                                dve.wait_ge(best_made, b * 64 + (16 * pr + t - 1))
                            v.scalar_tensor_tensor(MK[t % 2], SROW[:, t, :], NEGA[:, t:t + 1], SROW[:, t, :],
                                                   ALU.is_ge, ALU.subtract, reverse1=True).then_inc(masked, 1)
                        if 1 <= t < 17:
                            dve.wait_ge(masked, b * 64 + (16 * pr + t))
                            dve.sem_inc(wait_passed, 1)
                            v.max(BEST[:, t - 1, :], MK[(t - 1) % 2]).then_inc(best_made, 1)
                        if t >= 2:
                            dve.wait_ge(best_made, b * 64 + (16 * pr + t - 1))
                            v.scalar_tensor_tensor(M8J[:, (t - 2) % 16, :], IOTA8, IDX[:, t - 2:t - 1], BEST[:, t - 2, :],
                                                   ALU.is_equal, ALU.mult, accum_out=THR[:, t - 2:t - 1]).then_inc(found, 1)
                    dve.wait_ge(act_counted, b * (4 * (8 * EVALS + 16)) + ((pr + 1) * (8 * EVALS + 16) + 2))
                    v.tensor_scalar(SEEN, SEEN, 1.0, None, ALU.subtract)
                    v.tensor_scalar(IDX, IDX, 3.5, None, ALU.subtract)
                    dve.drain()
                    tt(SEEN, SEEN, SEEN, ALU.mult)
                    tt(IDX, IDX, IDX, ALU.mult)
                    dve.drain()
                    v.tensor_scalar(SEEN, SEEN, 1.5, None, ALU.is_gt)
                    v.tensor_scalar(IDX, IDX, 3.6 ** 2, None, ALU.is_gt)
                    dve.drain()
                    tt(BAD, SEEN, IDX, ALU.add)
                    dve.drain()
                    v.tensor_reduce(BADSUM, BAD, AX.X, ALU.add).then_inc(bad_summed, 1)
                    dve.wait_ge(bad_total, b * 4 + (pr + 1))
                    v.tensor_scalar(FLAG, PS[0:1, 7, 0:1], 0.0, None, ALU.is_gt)
                    dve.drain()
                    again = dve.value_load(FLAG, min_val=0, max_val=1)
                    with dve.If(again > 0):
                        v.memset(LOW, LOWEST)
                        v.memset(STEP, RANGE / 2)
                        v.memset(MID, LOWEST + RANGE / 2)
                        with dve.Fori(0, BISECTIONS) as n:
                            for t in range(16):
                                dve.drain()
                                v.tensor_scalar(JUNKF, SROW[:, t, :], MID[:, t:t + 1], None, ALU.is_ge, ALU.add,
                                                accum_out=CNT[:, t:t + 1])
                            dve.drain()
                            v.tensor_scalar(CNT, CNT, KEEP - 0.5, None, ALU.is_ge)
                            dve.drain()
                            tt(CNT, CNT, STEP, ALU.mult)
                            dve.drain()
                            tt(LOW, LOW, CNT, ALU.add)
                            v.tensor_scalar(STEP, STEP, 0.5, None, ALU.mult)
                            dve.drain()
                            tt(MID, LOW, STEP, ALU.add)
                            dve.drain()
                        v.tensor_copy(THR, LOW)
                        dve.drain()
                    stage_end(dve, b, dve_at)
                    for t in range(17):
                        if t < 16:
                            dve.wait_ge(e2_ready, b * (16 * 4) + (16 * pr + t + 1))
                            v.scalar_tensor_tensor(SROW[:, t, :], SROW[:, t, :], THR[:, t:t + 1], E2[:, t % 2, :],
                                                   ALU.is_ge, ALU.mult).then_inc(m2_ready, 1)
                        if t >= 1:
                            u = t - 1
                            dve.wait_ge(x2_made, b * (16 * 4) + (16 * pr + u + 1))
                            if u >= 2:
                                dve.wait_ge(pv2_done, b * (16 * 4) + (16 * pr + u - 1))
                            v.tensor_copy(PT2[:, u % 2, CH:2 * CH], PS[:, 2 * (u % 2) + 1, :]).then_inc(x2_free_dve, 1)
                    stage_end(dve, b, dve_at)
                    for i in range(2):
                        h = 2 * pr + i
                        v.tensor_copy(Z2[32 * (h % 4):32 * (h % 4) + 32, h // 4, :].rearrange("p (t n) -> p t n", t=2),
                                      PS[32:64, 4 + 2 * i:6 + 2 * i, :])
                    stage_end(dve, b, dve_at)

                def group_norm(g, tiles, stats, gamma, beta, factor=None):
                    dve.drain()
                    for i in range(tiles):
                        v.bn_aggr(MV[:, i, :], stats(i))
                    dve.drain()
                    v.tensor_copy(EX[:, 0:tiles, 0], MV[:, 0:tiles, 0])
                    tt(MSQ[:, 0:tiles], MV[:, 0:tiles, 0], MV[:, 0:tiles, 0], ALU.mult)
                    dve.drain()
                    tt(EX[:, 0:tiles, 1], MSQ[:, 0:tiles], MV[:, 0:tiles, 1], ALU.add).then_inc(gn_stats, 1)
                    dve.wait_ge(gn_sums, b * 5 + (g + 1))
                    v.tensor_copy(GM[:, 0:tiles, :], PS[:, 7, 0:2 * tiles].rearrange("p (t two) -> p t two", two=2))
                    dve.drain()
                    tt(MSQ[:, 0:tiles], GM[:, 0:tiles, 0], GM[:, 0:tiles, 0], ALU.mult)
                    dve.drain()
                    tt(VAR[:, 0:tiles], GM[:, 0:tiles, 1], MSQ[:, 0:tiles], ALU.subtract).then_inc(gn_var, 1)
                    dve.wait_ge(gn_sd, b * 5 + (g + 1))
                    v.reciprocal(RG[:, 0:tiles], SDG[:, 0:tiles])
                    dve.drain()
                    tt(SC(g)[:, 0:tiles], RG[:, 0:tiles], gamma, ALU.mult)
                    dve.drain()
                    tt(MSQ[:, 0:tiles], GM[:, 0:tiles, 0], SC(g)[:, 0:tiles], ALU.mult)
                    dve.drain()
                    tt(SH(g)[:, 0:tiles], beta, MSQ[:, 0:tiles], ALU.subtract)
                    dve.drain()
                    if factor is not None:
                        v.tensor_scalar(SC(g)[:, 0:tiles], SC(g)[:, 0:tiles], factor, None, ALU.mult)
                        v.tensor_scalar(SH(g)[:, 0:tiles], SH(g)[:, 0:tiles], factor, None, ALU.mult)
                    dve.drain().then_inc(gn_ready, 1)

                def stat(i, n):
                    return BST[:, i * 6 * n:(i + 1) * 6 * n].rearrange("p (c six) -> p c six", six=6)

                for g in range(2):
                    v.reciprocal(RC2[:, g, :], Z2[:, g, :])
                dve.drain()
                for g in range(2):
                    tt(O2[:, g, :], O2[:, g, :], RC2[:, g, :], ALU.mult)
                dve.drain().then_inc(o2_divided, 1)
                for t in range(2):
                    dve.wait_ge(o2_made, b * 2 + (t + 1))
                    v.bn_stats(BST[:, 6 * t:6 * t + 6], PS[:, t, :])
                dve.drain().then_inc(xin_free, 1)
                group_norm(0, 1, lambda i: stat(i, 2), w("agn_g"), w("agn_b"))
                dve.wait_ge(ao_done, b + 1)
                tt(LL, LL, AO, ALU.add)
                for g in range(3):
                    v.memset(PAD[g], 0.0)
                dve.drain()
                dve.wait_ge(xh2_made, b + 1)
                q00, q10, q01, q11 = quarter(XHB, 0, 0), quarter(XHB, 1, 0), quarter(XHB, 0, 1), quarter(XHB, 1, 1)
                tt(half(TMPB[0]), q00, q10, ALU.add)
                tt(half(TMPB[1]), q01, q11, ALU.add)
                tt(half(TMPB[2]), q10, q00, ALU.subtract)
                tt(half(TMPB[3]), q11, q01, ALU.subtract)
                dve.drain()
                tt(inner(0), half(TMPB[1]), half(TMPB[0]), ALU.subtract)
                tt(inner(1), half(TMPB[2]), half(TMPB[3]), ALU.add)
                tt(inner(2), half(TMPB[3]), half(TMPB[2]), ALU.subtract)
                stage_end(dve, b, dve_at)
                for j in range(6):
                    dve.wait_ge(dw2_made, b * 6 + (j + 1))
                    v.bn_stats(BST[:, 6 * j:6 * j + 6], PS[:, j, :])
                group_norm(1, 3, lambda i: stat(i, 2), w("he1_g"), w("he1_b"))
                stage_end(dve, b, dve_at)
                for j in range(6):
                    dve.wait_ge(pw2_made, b * 6 + (j + 1))
                    v.bn_stats(BST[:, 6 * j:6 * j + 6], PS[:, j, :])
                group_norm(2, 3, lambda i: stat(i, 2), w("he2_g"), w("he2_b"), w("alpha"))
                for g in range(3):
                    dve.wait_ge(ho_made, b * 3 + (g + 1))
                    tt(half(HO[g]), half(HO[g]), inner(g), ALU.add)
                dve.drain()
                tt(TMP[0], LL, HO[2], ALU.add)
                tt(TMP[1], LL, HO[2], ALU.subtract)
                tt(TMP[2], HO[0], HO[1], ALU.add)
                tt(TMP[3], HO[0], HO[1], ALU.subtract)
                dve.drain()
                q = [area(56 + 4 * i, 4) for i in range(4)]
                tt(q[0], TMP[0], TMP[2], ALU.subtract)
                tt(q[1], TMP[1], TMP[3], ALU.subtract)
                tt(q[2], TMP[1], TMP[3], ALU.add)
                tt(q[3], TMP[0], TMP[2], ALU.add)
                dve.drain()
                for i, (r, c) in enumerate(((0, 0), (1, 0), (0, 1), (1, 1))):
                    v.scalar_tensor_tensor(quarter(X, r, c), half(q[i]), 0.1, quarter(X, r, c), ALU.mult, ALU.add)
                stage_end(dve, b, dve_at)
                for j in range(2 * NCH):
                    dve.wait_ge(u1_copied, b * (2 * NCH) + (j + 1))
                    v.bn_stats(BST[:, 6 * j:6 * j + 6], F1[:, j // NCH, chunk(j % NCH)])
                group_norm(3, 2, lambda i: stat(i, 8), w("f1_g"), w("f1_b"))
                for t in range(NCH):
                    dve.wait_ge(u2_copied, b * NCH + (t + 1))
                    v.bn_stats(BST[:, 6 * t:6 * t + 6], F2[:, chunk(t)])
                group_norm(4, 1, lambda i: stat(i, 8), w("f2_g"), w("f2_b"), 0.1)
                for t in range(NCH):
                    dve.wait_ge(u3_ready, b * NCH + (t + 1))
                    tt(X[:, chunk(t)], X[:, chunk(t)], F2[:, chunk(t)], ALU.add)
                stage_end(dve, b, dve_at)
                v.memset(HP, 0.0)
                dve.wait_ge(fl_made, b + 1)
                v.tensor_copy(FILT, PS[:, 6, 0:128]).then_inc(dve_link, 1)
                dve.wait_ge(dve_link, b + 1)
                for g in range(NCH):
                    dve.wait_ge(c3_made, b * NCH + (g + 1))
                    if g >= 2:
                        dve.wait_ge(i3_made, b * NCH + (g - 1))
                    tt(GC[:, g % 2, :].rearrange("p (q c) -> p q c", q=4), PS[:, 2 + g % 2, :].rearrange("p (q c) -> p q c", q=4),
                       FILT.rearrange("p (one c) -> p one c", one=1).to_broadcast([128, 4, 128]), ALU.mult).then_inc(c3_scaled, 1)
                stage_end(dve, b, dve_at)
                for g in range(NCH + 1):
                    if g < NCH:
                        dve.wait_ge(d3_gelu, b * NCH + (g + 1))
                        if g >= 2:
                            dve.wait_ge(o3_made, b * NCH + (g - 1))
                        v.scalar_tensor_tensor(G2[0:64, g % 2, :], PS[64:128, 6 + g % 2, :], w("b_dw2", 64),
                                               G1[0:64, g % 2, :], ALU.add, ALU.mult).then_inc(d3_gated, 1)
                    if g >= 1:
                        i = g - 1
                        dve.wait_ge(o3_made, b * NCH + (i + 1))
                        v.scalar_tensor_tensor(X[:, chunk(i)], PS[:, i % 2, :], w("b_out"), X[:, chunk(i)],
                                               ALU.add, ALU.add).then_inc(o3_free, 1)
                stage_end(dve, b, dve_at)
            assert dve_at[0] == STAGES


def _packed_constants():
    K = np.zeros((128, C_TOTAL), np.float32)

    def put(name, a):
        at, n = CCOLS[name]
        K[0:a.shape[0], at:at + n] = a
    i = np.arange(128)
    put("ident", np.eye(128))
    put("mean", np.full((128, 128), 1 / 128))
    ch = np.arange(384)
    g12 = (ch[:, None] // 12 == ch[None, :] // 12) / 12.0
    put("g12", g12.reshape(3, 128, 384).transpose(1, 0, 2).reshape(128, 9 * 128))
    put("g8", (i[:, None] // 8 == i[None, :] // 8) / 8.0)
    put("g4", (i[:, None] // 4 == i[None, :] // 4) / 4.0)
    put("bd16", (i[:, None] // D2 == i[None, :] // D2) * 1.0)
    sel = np.zeros((128, H2, 96))
    for h in range(H2):
        for d in range(D2):
            for s in range(3):
                sel[h * D2 + d, h, s * SLOT + d] = 1
    put("sel", sel.reshape(128, H2 * 96))
    r, c = np.meshgrid(np.arange(8), np.arange(8), indexing="ij")
    basis, scales = [], []
    for v in range(5):
        for u in range(8):
            if v in (0, 4) and u > 4:
                continue
            a = 2 * np.pi * (u * r + v * c) / 8
            f = np.zeros((8, 5))
            if v in (0, 4):
                f[u, v] += 0.5
                f[(8 - u) % 8, v] += 0.5
            else:
                f[u, v] = 1
            if v in (0, 4) and u in (0, 4):
                basis.append(np.cos(a) / 8)
                scales.append(f)
            else:
                basis += [np.cos(a) * np.sqrt(2) / 8, np.sin(a) * np.sqrt(2) / 8]
                scales += [f, f]
    dft = np.zeros((8, 2, 8, 2, 64))
    for p in range(2):
        dft[:, p, :, p, :] = np.stack(basis, -1)
    dft = dft.reshape(128, 128)
    put("dft", dft)
    put("idft", dft.T)
    put("msel", np.tile(np.stack(scales).reshape(64, 40).T, (1, 2)))
    return K


def kernel(**inputs):
    import concourse.bacc as bacc
    from concourse.bass_utils import run_bass_kernel_spmd

    a = {n: np.ascontiguousarray(v) for n, v in inputs.items()}
    Wp = np.zeros((128, W_TOTAL), np.float32)

    def put(name, v):
        at, n = WCOLS[name]
        v = v.reshape(-1, n)
        Wp[0:v.shape[0], at:at + n] = v

    def tiles(v):
        return v.reshape(-1, 128, v.shape[1]).transpose(1, 0, 2).reshape(128, -1)

    def cols(v):
        return v.reshape(-1, 128).T

    put("wt2", np.tile(a["L0_conv_Wt"].T, (1, 2)))
    put("wp2", np.tile(a["L0_conv_Wp"].T, (1, 2)))
    put("wg", a["L0_conv_Wg"].T)
    put("ww", np.tile(a["L0_conv_Ww"].T, (2, 1)))
    put("bt2", np.tile(a["L0_conv_bt"], 2)[:, None])
    put("bp2", np.tile(a["L0_conv_bp"], 2)[:, None])
    put("bg", a["L0_conv_bg"][None])
    put("bw", a["L0_conv_bw"][:, None])
    put("ln1w", a["L1_conv_ln1_w"][:, None])
    put("ln1b", a["L1_conv_ln1_b"][:, None])
    qkv = a["L1_conv_qkv_w"].reshape(3, H1, D1, C)
    for name, m in (("wq", 0), ("wk", 1)):
        put(name, np.tile(qkv[m].transpose(2, 0, 1)[:, :, None, :], (1, 1, 3, 1)).reshape(C, H1 * 96))
    put("wv", qkv[2].reshape(C, C).T)
    put("proj", a["L1_conv_proj_w"].T)
    put("projb", a["L1_conv_proj_b"][:, None])
    put("ln2w", a["L1_conv_ln2_w"][:, None])
    put("ln2b", a["L1_conv_ln2_b"][:, None])
    put("fc1", a["L1_conv_fc1_w"].T)
    put("fc1b", cols(a["L1_conv_fc1_b"]))
    put("fc2", tiles(a["L1_conv_fc2_w"].T))
    put("fc2b", a["L1_conv_fc2_b"][:, None])
    put("q2", a["L2_conv_qkv_w"].T)
    p2 = np.zeros((2, 4, SLOT, C), np.float32)
    p2[:, :, 0:D2, :] = a["L2_conv_proj_w"].T.reshape(2, 4, D2, C)
    put("proj2", tiles(p2.reshape(256, C)))
    put("agn_g", a["L2_conv_attn_gn_g"][:, None])
    put("agn_b", a["L2_conv_attn_gn_b"][:, None])
    put("he_dw", a["L2_conv_he_dw_w"].reshape(3, 128, 9).transpose(1, 0, 2).reshape(128, 27))
    for n, v in (("he1", "he_gn1"), ("he2", "he_gn2"), ("f1", "ffn_gn1"), ("f2", "ffn_gn2")):
        put(n + "_g", cols(a[f"L2_conv_{v}_g"]))
        put(n + "_b", cols(a[f"L2_conv_{v}_b"]))
    put("he_pw", tiles(a["L2_conv_he_pw_w"].T))
    put("alpha", np.broadcast_to(a["L2_conv_alpha"], (128, 1)))
    put("f1", a["L2_conv_ffn_w1"].T)
    put("f2", tiles(a["L2_conv_ffn_w2"].T))
    put("w_in", a["L3_conv_w_in"].T)
    put("b_in", a["L3_conv_b_in"][None])
    put("w_dw", a["L3_conv_w_dw"].reshape(128, 9))
    put("b_dw", a["L3_conv_b_dw"][:, None])
    put("b_dw2", a["L3_conv_b_dw"][64:, None])
    put("filt", a["L3_conv_fft_filter"].reshape(128, 40).T)
    put("w_out", a["L3_conv_w_out"].T)
    put("b_out", a["L3_conv_b_out"][:, None])

    nc = bacc.Bacc("TRN2", target_bir_lowering=False, num_devices=1)
    arrays = {"x_dram": a["x"].reshape(B, C, N), "weights_dram": Wp, "consts_dram": _packed_constants()}
    aps = [nc.dram_tensor(n, v.shape, FP32, kind="ExternalInput").ap() for n, v in arrays.items()]
    out = nc.dram_tensor("out_dram", (B, C, N), FP32, kind="ExternalOutput").ap()
    build(nc, *aps, out)
    r = run_bass_kernel_spmd(nc, [arrays], core_ids=[0])
    return r.results[0]["out_dram"].reshape(B, C, SIDE, SIDE)
```

```python
import concourse.bass as bass
from concourse import mybir
from contextlib import ExitStack
import numpy as np

FP32 = mybir.dt.float32
FP16 = mybir.dt.float16
ALU = mybir.AluOpType
ACT = mybir.ActivationFunctionType
AX = mybir.AxisListType

B, C, SIDE = 4, 128, 64
N = SIDE * SIDE
CH = 512
NCH = N // CH
BLK = 128
NBLK = N // BLK
IC = 64
H1, D1 = 4, 32
H2, D2 = 8, 16
N2 = 1024
S2 = 32
KEEP = N2 // 2
SLOT = 32

WCOLS, CCOLS = {}, {}


def _columns(table, spec):
    at = 0
    for name, n in spec:
        table[name] = (at, n)
        at += n
    return at


W_TOTAL = _columns(WCOLS, [
    ("wt2", 128), ("wp2", 128), ("wg", IC), ("ww", C), ("bt2", 1), ("bp2", 1), ("bg", IC), ("bw", 1),
    ("ln1w", 1), ("ln1b", 1), ("wq", H1 * 96), ("wk", H1 * 96), ("wv", C), ("proj", C), ("projb", 1),
    ("ln2w", 1), ("ln2b", 1), ("fc1", 256), ("fc1b", 2), ("fc2", 256), ("fc2b", 1),
    ("q2", 3 * C), ("proj2", 256), ("agn_g", 1), ("agn_b", 1), ("he_dw", 27), ("he1_g", 3), ("he1_b", 3),
    ("he_pw", 3 * 384), ("he2_g", 3), ("he2_b", 3), ("alpha", 1), ("f1", 256), ("f1_g", 2), ("f1_b", 2),
    ("f2", 256), ("f2_g", 1), ("f2_b", 1),
    ("w_in", C), ("b_in", C), ("w_dw", 9), ("b_dw", 1), ("b_dw2", 1), ("filt", C), ("w_out", C), ("b_out", 1),
])
C_TOTAL = _columns(CCOLS, [
    ("ident", 128), ("mean", 128), ("g12", 9 * 128), ("g8", 128), ("g4", 128), ("bd16", 128),
    ("sel", H2 * 96), ("dft", 128), ("idft", 128), ("msel", 128),
])


class Layer:

    def __init__(self, sem, name, units, o_buffers):
        self.units, self.o_buffers = units, o_buffers
        self.tile_scored = sem(name + "_tile_scored")
        self.tile_free = sem(name + "_tile_free")
        self.shift_split = sem(name + "_shift_split")
        self.shift_step = sem(name + "_shift_step")
        self.scored = sem(name + "_scored")
        self.p_ready = sem(name + "_p_ready")
        self.p_used = sem(name + "_p_used")
        self.o_free = sem(name + "_o_free")
        self.inverted = sem(name + "_inverted")
        self.divided = sem(name + "_divided")


TILES = 66
STEPS = NBLK
TILE_PLAN = [3] * 10 + [2] * 17 + [0] * 5
assert sum(TILE_PLAN) == 64 and len(TILE_PLAN) == STEPS


def build(nc, x, weights, consts, out, nb=B):
    nc.disable_value_cache = True
    ctx = ExitStack()
    with ctx:
        def sb(name, shape, dt=FP32):
            return ctx.enter_context(nc.sbuf_tensor(name, shape, dt))

        def sem(name):
            return ctx.enter_context(nc.semaphore(name))

        W = sb("W", [128, W_TOTAL])
        K = sb("K", [128, C_TOTAL])
        DG = sb("DG", [128, 27 * 128])
        XIN = sb("XIN", [128, N])
        X = sb("X", [128, N])
        SM = sb("SM", [128, 512])
        ARENA = sb("ARENA", [128, 31 * 1024])
        PS = ctx.enter_context(nc.psum_tensor("PS", [128, 8, CH], FP32))

        def w(name, p=128):
            a, n = WCOLS[name]
            return W[0:p, a:a + n]

        def k(name, p=128):
            a, n = CCOLS[name]
            return K[0:p, a:a + n]

        def area(kb, n_kb, dt=FP32):
            v = ARENA[:, kb * 256:(kb + n_kb) * 256]
            return v if dt == FP32 else v.bitcast(dt)

        def chunk(t):
            return slice(t * CH, (t + 1) * CH)

        QA, QB, KA, KB = (area(8 * i, 8, FP16) for i in range(4))
        GT = area(32, 16).rearrange("p (j o) -> p j o", j=NBLK)
        Y0, Z0 = (area(48 + 8 * i, 8).rearrange("p (c n) -> p c n", c=NCH // 2) for i in range(2))
        QS = [area(8 * h, 8, FP16) for h in range(H1)]
        KS = [area(32 + 8 * h, 8, FP16) for h in range(H1)]
        VT = area(64, 32).rearrange("p (j h o) -> p j h o", j=NBLK, h=H1)
        XLN = area(96, 16)
        O1 = XLN
        SQ, SD, RS, XH = (area(4 * i, 4).rearrange("p (s n) -> p s n", s=2) for i in range(4))
        XC = area(20, 16)
        HID = area(0, 8).rearrange("p (s h n) -> p s h n", s=2, h=2)
        P = area(112, 8).rearrange("p (s n) -> p s n", s=2)
        RCP = area(120, 2)
        Z1 = XIN
        MX = SM[:, 0:64].rearrange("p (r m) -> p r m", r=8)
        NEG, N16 = SM[:, 64:72], SM[:, 72:76].bitcast(FP16)
        NHL = SM[:, 80:96].rearrange("p (r two) -> p r two", two=2)
        EPS5, EPS6 = SM[:, 96:97], SM[:, 97:98]
        ONES = SM[:, 128:256]

        XH2 = area(0, 16)
        SROW = area(0, 64).rearrange("p (t n) -> p t n", t=16)
        QS2 = [area(64 + 2 * i, 2, FP16) for i in range(2)]
        KS2 = [area(68 + 2 * i, 2, FP16) for i in range(2)]
        QKN = area(72, 8)
        VT2 = area(80, 16).rearrange("p (j h o) -> p j h o", j=8, h=H2)
        LL = area(96, 4)
        O2 = area(100, 8).rearrange("p (g n) -> p g n", g=2)
        Z2 = XIN[:, 0:2 * N2].rearrange("p (g n) -> p g n", g=2)
        E2 = area(108, 8).rearrange("p (s n) -> p s n", s=2)
        PT2 = area(116, 8).rearrange("p (s n) -> p s n", s=2)
        SQ2, SD2 = area(100, 8), area(108, 8)
        JUNK = [area(108 + 2 * i, 2, FP16) for i in range(4)]
        RC2 = area(116, 8).rearrange("p (g n) -> p g n", g=2)
        PADN = (S2 + 2) * (S2 + 2)
        PAD = [ARENA[:, g * PADN:(g + 1) * PADN] for g in range(3)]
        Y1 = [area(16 + 4 * g, 4) for g in range(3)]
        HO = [area(28 + 4 * g, 4) for g in range(3)]
        TMP = [area(40 + 4 * g, 4) for g in range(4)]
        CONV = TMP[1]
        XHB = area(56, 16)
        TMPB = [area(72 + 4 * g, 4) for g in range(4)]
        F1 = area(0, 32).rearrange("p (h n) -> p h n", h=2)
        F2 = area(32, 16)
        AO = area(40, 4)
        BST = SM[:, 256:352]
        MV, EX, GM = (SM[:, 352 + 6 * i:358 + 6 * i].rearrange("p (t two) -> p t two", two=2) for i in range(3))
        MSQ, VAR, SDG, RG = (SM[:, 370 + 3 * i:373 + 3 * i] for i in range(4))

        def SC(g):
            return SM[:, 384 + 6 * g:387 + 6 * g]

        def SH(g):
            return SM[:, 387 + 6 * g:390 + 6 * g]
        THR = SM[:, 416:432]
        BAD, BADSUM, FLAG = SM[:, 432:448], SM[:, 448:449], SM[0:1, 449:450].bitcast(mybir.dt.int32)
        IOTA8 = SM[:, 456:464]
        (LOW, HIGH, DLOW, DHIGH, MID, CNT, DEV, POS, BELOW, OUTW, NEXT, SPAN, RDEV, SEEN, IDX, STEP) = (
            ARENA[:, 120 * 256 + 16 * i:120 * 256 + 16 * i + 16] for i in range(16))
        BEST = ARENA[:, 121 * 256:121 * 256 + 128].rearrange("p (t e) -> p t e", e=8)
        M8J = ARENA[:, 122 * 256:122 * 256 + 128].rearrange("p (t e) -> p t e", e=8)
        JUNKF = area(116, 2, FP16)
        MK = [area(116, 4), area(108, 4)]
        HP = ARENA[:, 0:66 * 66].rearrange("p (r c) -> p r c", c=66)
        FILT = ARENA[:, 19 * 256:19 * 256 + 128]
        HT, GC, G1, G2, XP = (area(20 + 4 * i, 4).rearrange("p (s n) -> p s n", s=2) for i in range(5))

        def quarter(v, r, c):
            return v.rearrange("p (y a x b) -> p y a x b", y=S2, a=2, b=2)[:, :, r, :, c]

        def half(v):
            return v.rearrange("p (y x) -> p y x", x=S2)

        def inner(g):
            return PAD[g].rearrange("p (y x) -> p y x", x=S2 + 2)[:, 1:S2 + 1, 1:S2 + 1]

        loaded = sem("loaded")
        x_loaded = sem("x_loaded")
        xin_free = sem("xin_free")
        out_stored = sem("out_stored")
        setup_done = sem("setup_done")
        stage_done = sem("stage_done")
        wait_passed = sem("wait_passed")
        filt_placed = sem("filt_placed")
        L0 = Layer(sem, "L0", NCH // 2, 1)
        L1 = Layer(sem, "L1", 2 * NCH, 2)

        def events(*names):
            return [sem(n) for n in names]

        p0_made, p0_head, p0_free, g0_made = events("p0_made", "p0_head", "p0_free", "g0_made")
        y0_made, y0_free = events("y0_made", "y0_free")
        ln_mean, ln_xc, ln_sq, ln_var, ln_sd, ln_rs, ln_spread, ln_xh, ln_out = events(
            "ln_mean", "ln_xc", "ln_sq", "ln_var", "ln_sd", "ln_rs", "ln_spread", "ln_xh", "ln_out")
        p1_made, p1_head, p1_free, v1_made, v1_free = events("p1_made", "p1_head", "p1_free", "v1_made", "v1_free")
        pr_made, pr_free = events("pr_made", "pr_free")
        f1_made, f1_done, f2_made, f2_free = events("f1_made", "f1_done", "f2_made", "f2_free")
        xh_made, xh2_made = events("xh_made", "xh2_made")
        n2_made, n2_sq, n2_sum, n2_sd, v2_made = events(
            "n2_made", "n2_sq", "n2_sum", "n2_sd", "v2_made")
        s2_made, s2_head, s2_free = events("s2_made", "s2_head", "s2_free")
        t2_made, t2_free_act, t2_free_dve = events("t2_made", "t2_free_act", "t2_free_dve")
        mid_ready, act_counted, dve_counted, found = events("mid_ready", "act_counted", "dve_counted", "found")
        masked, best_made, bad_summed, bad_total = events("masked", "best_made", "bad_summed", "bad_total")
        e2_ready, m2_ready, x2_made, x2_free_act, x2_free_dve, pv2_done = events(
            "e2_ready", "m2_ready", "x2_made", "x2_free_act", "x2_free_dve", "pv2_done")
        gn_stats, gn_sums, gn_var, gn_sd, gn_ready = events("gn_stats", "gn_sums", "gn_var", "gn_sd", "gn_ready")
        o2_taken, o2_divided, o2_made, ao_done = events("o2_taken", "o2_divided", "o2_made", "ao_done")
        dw2_made, pw2_made, ho_made = events("dw2_made", "pw2_made", "ho_made")
        u1_made, u1_copied, u2_ready, u2_made, u2_copied, u3_ready = events(
            "u1_made", "u1_copied", "u2_ready", "u2_made", "u2_copied", "u3_ready")
        (xp_made,) = events("xp_made")
        fl_made, h3_made, h3_copied, c3_made, c3_scaled, i3_made, i3_placed = events(
            "fl_made", "h3_made", "h3_copied", "c3_made", "c3_scaled", "i3_made", "i3_placed")
        d3_made, d3_gelu, d3_gated, o3_made, o3_free = events("d3_made", "d3_gelu", "d3_gated", "o3_made", "o3_free")
        EVALS = 7
        BY_DVE = 7
        AIM = 4.5
        BY_ACT = 16 - BY_DVE
        ACT_PASSES = (EVALS - 1) * BY_ACT + 16 + 16
        SLOPE = 0.0625 * 2.5066 / N2
        BISECTIONS = 26
        LOWEST, RANGE = -0.25 - 2.0 ** -12, 0.5 + 2.0 ** -11

        block = ctx.enter_context(nc.Block())
        STAGES = 26

        def stage_end(eng, b, at):
            at[0] += 1
            eng.drain().then_inc(stage_done, 1)
            eng.wait_ge(stage_done, b * (4 * STAGES) + 4 * at[0])
            eng.sem_inc(wait_passed, 1)

        @block.sync
        def _(sp):
            sp.sem_inc(out_stored, 16)
            sp.dma_start(W[:, :], weights).then_inc(loaded, 16)
            sp.dma_start(K[:, :], consts).then_inc(loaded, 16)
            with sp.Fori(0, nb) as b:
                sp.wait_ge(xin_free, b + 1)
                sp.sem_inc(wait_passed, 1)
                sp.dma_start(XIN[:, :], x[bass.ds(b, 1), :, :].rearrange("a p n -> (a p) n")).then_inc(x_loaded, 16)
                sp.wait_ge(stage_done, b * (4 * STAGES) + 4 * STAGES)
                sp.dma_start(out[bass.ds(b, 1), :, :].rearrange("a p n -> (a p) n"), X[:, :]).then_inc(out_stored, 16)
            sp.wait_ge(out_stored, 16 * nb + 16)

        @block.tensor
        def _(pe):
            mm = nc.tensor.matmul
            pe.sem_inc(L0.p_used, 2)
            pe.sem_inc(L1.p_used, 2)
            pe.wait_ge(loaded, 32)
            pe.wait_ge(setup_done, 1)

            def l0_tile(t, col):
                r, m = t // NCH, t % NCH
                rows = bass.ds(col + r * BLK, BLK)
                mm(PS[:, t % 2, :], QA[:, rows], KA[:, chunk(m)], start=True, stop=False)
                return mm(PS[:, t % 2, :], QB[0:66, rows], KB[0:66, chunk(m)], start=False, stop=True)

            def l0_scores(s, col):
                for i in range(2):
                    cols = bass.ds(col + i * CH, CH)
                    o = PS[:, 2 + 2 * (s % 2) + i, :]
                    mm(o, KA[:, s * BLK:(s + 1) * BLK], QA[:, cols], start=True, stop=False)
                    last = mm(o, KB[0:66, s * BLK:(s + 1) * BLK], QB[0:66, cols], start=False, stop=True)
                return last

            def l0_sums(s):
                for i in range(2):
                    last = mm(PS[:, 6 + i, :], GT[:, s, :], P[:, s % 2, chunk(i)],
                              start=(s == 0), stop=(s == STEPS - 1))
                return last

            def l1_tile(pair):
                def tile(t, col):
                    h, r, m = 2 * pair + t // 32, t // NCH % 4, t % NCH
                    return mm(PS[:, t % 2, :], QS[h][0:96, bass.ds(col + r * BLK, BLK)], KS[h][0:96, chunk(m)],
                              start=True, stop=True)
                return tile

            def l1_scores(pair):
                def scores(s, col):
                    for i in range(2):
                        h = 2 * pair + i
                        last = mm(PS[:, 2 + 2 * (s % 2) + i, :], KS[h][0:98, s * BLK:(s + 1) * BLK],
                                  QS[h][0:98, bass.ds(col, CH)], start=True, stop=True)
                    return last
                return scores

            def l1_sums(pair):
                def sums(s):
                    for i in range(2):
                        last = mm(PS[64 * i:64 * i + 64, 6 + pair, :], VT[:, s, 2 * pair + i, :],
                                  P[:, s % 2, chunk(i)], start=(s == 0), stop=(s == STEPS - 1))
                    return last
                return sums

            def unit(L, at, ua=None, a_tile=None, a_col=None, a_scores=None, ub=None, b_scores=None, b_col=None,
                     b_sums=None):
                t = 0
                for s in range(STEPS):
                    if ua is not None:
                        for _ in range(TILE_PLAN[s]):
                            pe.wait_ge(L.tile_free, ua * TILES + (t + 1))
                            a_tile(t, a_col).then_inc(L.tile_scored, 1)
                            t += 1
                        if s == STEPS - 2:
                            pe.wait_ge(L.shift_split, ua + 1)
                            for i in range(2):
                                pe.wait_ge(L.tile_free, ua * TILES + (65 + i))
                                for r in range(4):
                                    last = mm(PS[at:at + 2, i, r * BLK:(r + 1) * BLK], NHL[:, 4 * i + r, :], k("ident"),
                                              start=True, stop=True)
                                last.then_inc(L.tile_scored, 1)
                        if s == STEPS - 1:
                            pe.wait_ge(L.tile_free, ua * TILES + (TILES + 2))
                            pe.wait_ge(L.p_ready, ua * STEPS + 1)
                            a_scores(0, a_col).then_inc(L.scored, 1)
                    if ub is not None:
                        if s + 1 < STEPS:
                            pe.wait_ge(L.p_ready, ub * STEPS + (s + 2))
                            b_scores(s + 1, b_col).then_inc(L.scored, 1)
                        pe.wait_ge(L.p_ready, ub * STEPS + (s + 3))
                        if s == 0:
                            pe.wait_ge(L.o_free, ub + 1)
                        b_sums(s).then_inc(L.p_used, 1)

            pe_at = [0]
            with pe.Fori(0, nb) as b:
                pe.wait_ge(x_loaded, b * 16 + 16)
                for j in range(2 * NCH):
                    if j >= 4:
                        pe.wait_ge(p0_free, b * (2 * NCH) + (j - 3))
                    mm(PS[:, j % 4, :], w("wt2") if j % 2 == 0 else w("wp2"), XIN[:, chunk(j // 2)],
                       start=True, stop=True).then_inc(p0_made, 1)
                for j in range(NBLK):
                    o = PS[:, 4 + j // 8, (j % 8) * IC:(j % 8 + 1) * IC]
                    mm(o, XIN[:, j * BLK:(j + 1) * BLK], w("wg"), start=True, stop=False)
                    last = mm(o, ONES[0:1, 0:BLK], w("bg", 1), start=False, stop=True)
                    if j % 8 == 7:
                        last.then_inc(g0_made, 1)
                stage_end(pe, b, pe_at)
                a = dict(a_tile=l0_tile, a_scores=l0_scores)
                bb = dict(b_scores=l0_scores, b_sums=l0_sums)
                u0 = b * (NCH // 2)
                unit(L0, 64, ua=u0, a_col=0, **a)
                with pe.Fori(0, NCH // 2 - 1) as q:
                    unit(L0, 64, ua=u0 + q + 1, a_col=q * (2 * CH) + 2 * CH, ub=u0 + q, b_col=q * (2 * CH), **a, **bb)
                unit(L0, 64, ub=u0 + (NCH // 2 - 1), b_col=N - 2 * CH, **bb)
                stage_end(pe, b, pe_at)
                for t in range(NCH):
                    if t >= 2:
                        pe.wait_ge(y0_free, b * NCH + (t - 1))
                    pe.wait_ge(L0.divided, b * (NCH // 2) + (t // 2 + 1))
                    at = IC * (t % 2)
                    mm(PS[:, t % 2, :], w("ww")[at:at + IC, :], Y0[at:at + IC, t // 2, :],
                       start=True, stop=True).then_inc(y0_made, 1)
                stage_end(pe, b, pe_at)

                def layernorm(n):
                    base = b * (2 * NCH) + n * NCH
                    for t in range(NCH + 1):
                        if t < NCH:
                            if t >= 2:
                                pe.wait_ge(ln_xc, base + (t - 1))
                            mm(PS[:, t % 2, :], k("mean"), X[:, chunk(t)], start=True, stop=True).then_inc(ln_mean, 1)
                        if t >= 1:
                            u, at = t - 1, 32 * ((t - 1) % 4)
                            pe.wait_ge(ln_sq, base + (u + 1))
                            mm(PS[at:at + 32, 2 + u // 4, :], k("mean")[:, 0:32], SQ[:, u % 2, :],
                               start=True, stop=True).then_inc(ln_var, 1)
                    for t in range(NCH):
                        at = 32 * (t % 4)
                        if t % 4 == 0:
                            pe.wait_ge(ln_rs, b * 4 + (2 * n + t // 4 + 1))
                        if t >= 4:
                            pe.wait_ge(ln_xh, base + (t - 3))
                        mm(PS[:, 4 + t % 4, :], ONES[at:at + 1, :], RS[at:at + 1, t // 4, :],
                           start=True, stop=True).then_inc(ln_spread, 1)

                layernorm(0)
                stage_end(pe, b, pe_at)
                for j in range(2 * H1 * NCH):
                    h, t = j // 2 % H1, j // (2 * H1)
                    if j >= 4:
                        pe.wait_ge(p1_free, b * (2 * H1 * NCH) + (j - 3))
                    mm(PS[0:96, j % 4, :], w("wq" if j % 2 == 0 else "wk")[:, h * 96:(h + 1) * 96],
                       XLN[:, chunk(t)], start=True, stop=True).then_inc(p1_made, 1)
                for j in range(NBLK):
                    if j % 4 == 0 and j >= 16:
                        pe.wait_ge(v1_free, b * (NBLK // 4) + (j // 4 - 3))
                    last = mm(PS[:, 4 + j // 4 % 4, (j % 4) * C:(j % 4 + 1) * C], XLN[:, j * BLK:(j + 1) * BLK],
                              w("wv"), start=True, stop=True)
                    if j % 4 == 3:
                        last.then_inc(v1_made, 1)
                stage_end(pe, b, pe_at)
                u1 = b * (2 * NCH)

                def a1(p):
                    return dict(a_tile=l1_tile(p), a_scores=l1_scores(p))

                def b1(p):
                    return dict(b_scores=l1_scores(p), b_sums=l1_sums(p))

                unit(L1, 96, ua=u1, a_col=0, **a1(0))
                with pe.Fori(0, NCH - 1) as q:
                    unit(L1, 96, ua=u1 + q * 2 + 1, a_col=q * CH, **a1(1), ub=u1 + q * 2, b_col=q * CH, **b1(0))
                    unit(L1, 96, ua=u1 + q * 2 + 2, a_col=q * CH + CH, **a1(0), ub=u1 + q * 2 + 1, b_col=q * CH, **b1(1))
                unit(L1, 96, ua=u1 + (2 * NCH - 1), a_col=N - CH, **a1(1), ub=u1 + (2 * NCH - 2), b_col=N - CH, **b1(0))
                unit(L1, 96, ub=u1 + (2 * NCH - 1), b_col=N - CH, **b1(1))
                stage_end(pe, b, pe_at)
                for t in range(NCH):
                    if t >= 2:
                        pe.wait_ge(pr_free, b * NCH + (t - 1))
                    pe.wait_ge(L1.divided, b * NCH + (t + 1))
                    mm(PS[:, t % 2, :], w("proj"), O1[:, chunk(t)], start=True, stop=True).then_inc(pr_made, 1)
                stage_end(pe, b, pe_at)
                layernorm(1)
                stage_end(pe, b, pe_at)
                for t in range(NCH + 1):
                    if t < NCH:
                        for i in range(2):
                            if t >= 2:
                                pe.wait_ge(f1_done, b * (2 * NCH) + (2 * (t - 2) + i + 1))
                            mm(PS[:, 2 * (t % 2) + i, :], w("fc1")[:, i * 128:(i + 1) * 128], XLN[:, chunk(t)],
                               start=True, stop=True).then_inc(f1_made, 1)
                    if t >= 1:
                        pe.wait_ge(f1_done, b * (2 * NCH) + 2 * t)
                        if t >= 3:
                            pe.wait_ge(f2_free, b * NCH + (t - 2))
                        for i in range(2):
                            last = mm(PS[:, 4 + (t - 1) % 2, :], w("fc2")[:, i * 128:(i + 1) * 128],
                                      HID[:, (t - 1) % 2, i, :], start=(i == 0), stop=(i == 1))
                        last.then_inc(f2_made, 1)
                stage_end(pe, b, pe_at)
                stage_end(pe, b, pe_at)
                for j in range(4):
                    mm(PS[:, j, :], w("q2")[:, j // 2 * C:(j // 2 + 1) * C], LL[:, chunk(j % 2)],
                       start=True, stop=True).then_inc(n2_made, 1)
                for j in range(8):
                    last = mm(PS[:, 6 + j // 4, (j % 4) * C:(j % 4 + 1) * C], LL[:, j * BLK:(j + 1) * BLK],
                              w("q2")[:, 2 * C:3 * C], start=True, stop=True)
                last.then_inc(v2_made, 1)
                for j in range(4):
                    pe.wait_ge(n2_sq, b * 4 + (j + 1))
                    if j >= 2:
                        pe.wait_ge(n2_sd, b * 4 + (j - 1))
                    mm(PS[:, 4 + j % 2, :], k("bd16"), SQ2[:, chunk(j)], start=True, stop=True).then_inc(n2_sum, 1)
                stage_end(pe, b, pe_at)
                for pr in range(H2 // 2):
                    for j in range(8):
                        i, z, t = j // 4, j // 2 % 2, j % 2
                        if j >= 4:
                            pe.wait_ge(s2_free, b * (8 * 4) + (8 * pr + j - 3))
                        mm(PS[0:96, j % 4, :], k("sel")[:, (2 * pr + i) * 96:(2 * pr + i + 1) * 96],
                           QKN[:, z * N2 + t * CH:z * N2 + (t + 1) * CH], start=True, stop=True).then_inc(s2_made, 1)
                    if pr > 0:
                        pe.wait_ge(o2_taken, b * 8 + 2 * pr)
                    for t in range(16):
                        if t % 8 == 0:
                            pe.wait_ge(s2_free, b * (8 * 4) + (8 * pr + t // 2 + 4))
                        if t >= 2:
                            pe.wait_ge(t2_free_act if t % 2 == 0 else t2_free_dve, b * (8 * 4) + (8 * pr + (t - 2) // 2 + 1))
                        for m in range(2):
                            last = mm(PS[:, 4 + 2 * (t % 2) + m, :], QS2[t // 8][0:96, t % 8 * BLK:(t % 8 + 1) * BLK],
                                      KS2[t // 8][0:96, chunk(m)], start=True, stop=True)
                        last.then_inc(t2_made, 1)
                    stage_end(pe, b, pe_at)
                    pe.wait_ge(bad_summed, b * 4 + (pr + 1))
                    mm(PS[0:1, 7, 0:1], BADSUM, k("mean")[:, 0:1], start=True, stop=True).then_inc(bad_total, 1)
                    stage_end(pe, b, pe_at)
                    for t in range(17):
                        if t < 16:
                            pe.wait_ge(m2_ready, b * (16 * 4) + (16 * pr + t + 1))
                            if t >= 2:
                                pe.wait_ge(x2_free_act, b * (16 * 4) + (16 * pr + t - 1))
                                pe.wait_ge(x2_free_dve, b * (16 * 4) + (16 * pr + t - 1))
                            for j in range(8):
                                last = nc.tensor.transpose(PS[:, 2 * (t % 2) + j // 4, (j % 4) * BLK:(j % 4 + 1) * BLK],
                                                           SROW[:, t, j * BLK:(j + 1) * BLK], k("ident"))
                            last.then_inc(x2_made, 1)
                        if t >= 1:
                            u = t - 1
                            i, r = u // 8, u % 8
                            pe.wait_ge(x2_free_act, b * (16 * 4) + (16 * pr + u + 1))
                            pe.wait_ge(x2_free_dve, b * (16 * 4) + (16 * pr + u + 1))
                            for j in range(8):
                                last = mm(PS[0:64, 4 + 2 * i + r // 4, (r % 4) * BLK:(r % 4 + 1) * BLK],
                                          VT2[:, j, 2 * pr + i, :], PT2[:, u % 2, j * BLK:(j + 1) * BLK],
                                          start=(j == 0), stop=(j == 7))
                            last.then_inc(pv2_done, 1)
                stage_end(pe, b, pe_at)

                def group_sums(g, tiles, name):
                    pe.wait_ge(gn_stats, b * 5 + (g + 1))
                    for o in range(tiles):
                        n = tiles if name == "g12" else 1
                        for i in range(n):
                            gi = i if n > 1 else o
                            m = k(name)[:, gi * 384 + o * 128:gi * 384 + (o + 1) * 128] if n > 1 else k(name)
                            last = mm(PS[:, 7, 2 * o:2 * o + 2], m, EX[:, gi, :], start=(i == 0), stop=(i == n - 1))
                    last.then_inc(gn_sums, 1)

                pe.wait_ge(o2_divided, b + 1)
                for t in range(2):
                    for g in range(2):
                        last = mm(PS[:, t, :], w("proj2")[:, g * C:(g + 1) * C], O2[:, g, chunk(t)],
                                  start=(g == 0), stop=(g == 1))
                    last.then_inc(o2_made, 1)
                group_sums(0, 1, "g4")
                stage_end(pe, b, pe_at)
                for g in range(2):
                    for t in range(2):
                        for tap in range(9):
                            src = PAD[g].rearrange("p (y x) -> p y x", x=S2 + 2)[:, 16 * t + tap // 3:16 * t + tap // 3 + 16,
                                                                              tap % 3:tap % 3 + S2]
                            last = mm(PS[:, 2 * g + t, :].rearrange("p (y x) -> p y x", x=S2),
                                      DG[:, (9 * g + tap) * 128:(9 * g + tap + 1) * 128], src,
                                      start=(tap == 0), stop=(tap == 8))
                        last.then_inc(dw2_made, 1)
                group_sums(1, 3, "g12")
                stage_end(pe, b, pe_at)
                for o in range(3):
                    for t in range(2):
                        for g in range(3):
                            last = mm(PS[:, 2 * o + t, :], w("he_pw")[:, g * 384 + o * 128:g * 384 + (o + 1) * 128],
                                      Y1[g][:, chunk(t)], start=(g == 0), stop=(g == 2))
                        last.then_inc(pw2_made, 1)
                group_sums(2, 3, "g12")
                stage_end(pe, b, pe_at)
                for j in range(2 * NCH):
                    if j >= 4:
                        pe.wait_ge(u1_copied, b * (2 * NCH) + (j - 3))
                    mm(PS[:, j % 4, :], w("f1")[:, j // NCH * 128:(j // NCH + 1) * 128], X[:, chunk(j % NCH)],
                       start=True, stop=True).then_inc(u1_made, 1)
                group_sums(3, 2, "g8")
                for t in range(NCH):
                    pe.wait_ge(u2_ready, b * (2 * NCH) + (2 * t + 2))
                    if t >= 2:
                        pe.wait_ge(u2_copied, b * NCH + (t - 1))
                    for i in range(2):
                        last = mm(PS[:, 4 + t % 2, :], w("f2")[:, i * 128:(i + 1) * 128], F1[:, i, chunk(t)],
                                  start=(i == 0), stop=(i == 1))
                    last.then_inc(u2_made, 1)
                group_sums(4, 1, "g4")
                stage_end(pe, b, pe_at)
                mm(PS[:, 6, 0:128], k("msel", 40), w("filt", 40), start=True, stop=True).then_inc(fl_made, 1)
                for g in range(NCH + 2):
                    if g < NCH:
                        if g >= 2:
                            pe.wait_ge(h3_copied, b * NCH + (g - 1))
                        pe.wait_ge(xp_made, b * NCH + (g + 1))
                        for q in range(4):
                            o = PS[:, g % 2, q * 128:(q + 1) * 128]
                            mm(o, XP[:, g % 2, q * 128:(q + 1) * 128], w("w_in"), start=True, stop=False)
                            last = mm(o, ONES[0:1, :], w("b_in", 1), start=False, stop=True)
                        last.then_inc(h3_made, 1)
                    if 1 <= g <= NCH:
                        i = g - 1
                        pe.wait_ge(h3_copied, b * NCH + (i + 1))
                        if i >= 2:
                            pe.wait_ge(c3_scaled, b * NCH + (i - 1))
                        mm(PS[:, 2 + i % 2, :], k("dft"), HT[:, i % 2, :], start=True, stop=True).then_inc(c3_made, 1)
                    if g >= 2:
                        i = g - 2
                        pe.wait_ge(c3_scaled, b * NCH + (i + 1))
                        if i >= 2:
                            pe.wait_ge(i3_placed, b * NCH + (i - 1))
                        for q in range(4):
                            last = mm(PS[:, 4 + i % 2, q * 128:(q + 1) * 128], GC[:, i % 2, q * 128:(q + 1) * 128],
                                      k("idft"), start=True, stop=True)
                        last.then_inc(i3_made, 1)
                stage_end(pe, b, pe_at)
                for g in range(NCH + 1):
                    if g < NCH:
                        if g >= 2:
                            pe.wait_ge(d3_gated, b * NCH + (g - 1))
                        for tap in range(9):
                            last = mm(PS[:, 6 + g % 2, :].rearrange("p (y x) -> p y x", x=SIDE),
                                      DG[:, (18 + tap) * 128:(19 + tap) * 128],
                                      HP[:, 8 * g + tap // 3:8 * g + tap // 3 + 8, tap % 3:tap % 3 + SIDE],
                                      start=(tap == 0), stop=(tap == 8))
                        last.then_inc(d3_made, 1)
                    if g >= 1:
                        i = g - 1
                        pe.wait_ge(d3_gated, b * NCH + (i + 1))
                        if i >= 2:
                            pe.wait_ge(o3_free, b * NCH + (i - 1))
                        mm(PS[:, i % 2, :], w("w_out", 64), G2[0:64, i % 2, :], start=True, stop=True).then_inc(o3_made, 1)
                stage_end(pe, b, pe_at)
            assert pe_at[0] == STAGES

        @block.scalar
        def _(act):
            go = nc.scalar.activation
            act.sem_inc(L0.p_ready, 2)
            act.sem_inc(L1.p_ready, 2)
            act.sem_inc(L0.o_free, L0.o_buffers)
            act.sem_inc(L1.o_free, L1.o_buffers)
            act.sem_inc(act_counted, 2)
            act.wait_ge(loaded, 32)
            act.wait_ge(setup_done, 1)

            def exps(L, u, scale, take=None):
                for s in range(STEPS):
                    act.wait_ge(L.scored, u * STEPS + (s + 1))
                    act.wait_ge(L.p_used, u * STEPS + (s + 1))
                    go(P[:, s % 2, :].rearrange("p (i n) -> p i n", i=2), PS[:, 2 + 2 * (s % 2):4 + 2 * (s % 2), :],
                       ACT.Exp, scale=scale).then_inc(L.p_ready, 1)
                    if s == 0 and take is not None:
                        take()

            def l0_take(u, c):
                act.wait_ge(L0.p_used, u * STEPS + (STEPS + 2))
                act.sem_inc(wait_passed, 1)
                for i in range(2):
                    for rows, to in ((0, Y0), (64, Z0)):
                        last = go(to[64 * i:64 * i + 64, bass.ds(c, 1), :].rearrange("p a n -> p (a n)"),
                                  PS[rows:rows + 64, 6 + i, :], ACT.Copy)
                last.then_inc(L0.o_free, 1)

            def l1_take(u, pair, col):
                act.wait_ge(L1.p_used, u * STEPS + (STEPS + 2))
                act.sem_inc(wait_passed, 1)
                for i in range(2):
                    h = 2 * pair + i
                    for rows, to in ((0, O1), (32, Z1)):
                        last = go(to[32 * h:32 * h + 32, bass.ds(col, CH)],
                                  PS[64 * i + rows:64 * i + rows + 32, 6 + pair, :], ACT.Copy)
                last.then_inc(L1.o_free, 1)

            act_at = [0]
            with act.Fori(0, nb) as b:
                for t in range(NCH):
                    act.wait_ge(p0_made, b * (2 * NCH) + (2 * t + 1))
                    go(QA[:, chunk(t)], PS[:, 2 * t % 4, :], ACT.Identity, bias=w("bt2")).then_inc(p0_head, 1)
                    act.wait_ge(p0_made, b * (2 * NCH) + (2 * t + 2))
                    go(KB[0:64, chunk(t)], PS[0:64, (2 * t + 1) % 4, :], ACT.Identity, bias=w("bp2", 64))
                    go(KA[:, chunk(t)], PS[:, (2 * t + 1) % 4, :], ACT.Identity, bias=w("bp2")).then_inc(p0_head, 1)
                stage_end(act, b, act_at)
                u0 = b * (NCH // 2)
                exps(L0, u0, 1.0)
                with act.Fori(1, NCH // 2) as q:
                    exps(L0, u0 + q, 1.0, lambda: l0_take(u0 + q - 1, q - 1))
                l0_take(u0 + (NCH // 2 - 1), NCH // 2 - 1)
                stage_end(act, b, act_at)
                stage_end(act, b, act_at)

                def layernorm(n):
                    base = b * (2 * NCH) + n * NCH
                    for t in range(NCH):
                        act.wait_ge(ln_xc, base + (t + 1))
                        if t >= 2:
                            act.wait_ge(ln_var, base + (t - 1))
                        go(SQ[:, t % 2, :], XC[:, chunk(t)], ACT.Square).then_inc(ln_sq, 1)
                    for g in range(2):
                        act.wait_ge(ln_var, base + 4 * (g + 1))
                        go(SD[:, g, :], PS[:, 2 + g, :], ACT.Sqrt, bias=EPS5).then_inc(ln_sd, 1)

                layernorm(0)
                stage_end(act, b, act_at)
                for j in range(2 * H1 * NCH):
                    h, t = j // 2 % H1, j // (2 * H1)
                    act.wait_ge(p1_made, b * (2 * H1 * NCH) + (j + 1))
                    go((QS if j % 2 == 0 else KS)[h][0:96, chunk(t)], PS[0:96, j % 4, :], ACT.Copy).then_inc(p1_head, 1)
                stage_end(act, b, act_at)
                u1, scale = b * (2 * NCH), float(D1) ** -0.5
                exps(L1, u1, scale)
                exps(L1, u1 + 1, scale, lambda: l1_take(u1, 0, 0))
                with act.Fori(1, NCH) as q:
                    exps(L1, u1 + q * 2, scale, lambda: l1_take(u1 + q * 2 - 1, 1, q * CH - CH))
                    exps(L1, u1 + q * 2 + 1, scale, lambda: l1_take(u1 + q * 2, 0, q * CH))
                l1_take(u1 + (2 * NCH - 1), 1, N - CH)
                stage_end(act, b, act_at)
                stage_end(act, b, act_at)
                layernorm(1)
                stage_end(act, b, act_at)
                for t in range(NCH):
                    for i in range(2):
                        act.wait_ge(f1_made, b * (2 * NCH) + (2 * t + i + 1))
                        if t >= 2:
                            act.wait_ge(f2_made, b * NCH + (t - 1))
                        go(HID[:, t % 2, i, :], PS[:, 2 * (t % 2) + i, :], ACT.Gelu,
                           bias=w("fc1b")[:, i:i + 1]).then_inc(f1_done, 1)
                stage_end(act, b, act_at)
                go(XH2, X[:, :], ACT.Copy, scale=0.5).then_inc(xh_made, 1)
                stage_end(act, b, act_at)
                for j in range(4):
                    act.wait_ge(n2_made, b * 4 + (j + 1))
                    go(SQ2[:, chunk(j)], PS[:, j, :], ACT.Square).then_inc(n2_sq, 1)
                for j in range(4):
                    act.wait_ge(n2_sum, b * 4 + (j + 1))
                    go(SD2[:, chunk(j)], PS[:, 4 + j % 2, :], ACT.Sqrt).then_inc(n2_sd, 1)
                stage_end(act, b, act_at)
                for pr in range(H2 // 2):
                    for j in range(8):
                        i, z, t = j // 4, j // 2 % 2, j % 2
                        act.wait_ge(s2_made, b * (8 * 4) + (8 * pr + j + 1))
                        go((QS2, KS2)[z][i][0:96, chunk(t)], PS[0:96, j % 4, :], ACT.Copy).then_inc(s2_head, 1)
                    for t in range(0, 16, 2):
                        act.wait_ge(t2_made, b * (16 * 4) + (16 * pr + t + 1))
                        go(SROW[:, t, :].rearrange("p (m n) -> p m n", m=2), PS[:, 4:6, :], ACT.Copy,
                           scale=float(D2) ** -0.5, accum_out=CNT[:, t:t + 1]).then_inc(t2_free_act, 1)
                    stage_end(act, b, act_at)
                    counted = b * (4 * ACT_PASSES) + pr * ACT_PASSES

                    def signs(t, before, point, sums):
                        act.wait_ge(act_counted, counted + before + 1)
                        go(JUNK[2 + t % 2], SROW[:, t, :], ACT.Sign, bias=point[:, t:t + 1], scale=-1.0,
                           accum_out=sums[:, t:t + 1]).then_inc(act_counted, 1)

                    with act.Fori(0, EVALS - 1) as n:
                        act.wait_ge(mid_ready, b * (4 * EVALS) + n + (pr * EVALS + 1))
                        for i in range(BY_ACT):
                            t = BY_DVE + i
                            act.wait_ge(act_counted, counted + n * BY_ACT + (i + 1))
                            go(JUNK[2 + i % 2], SROW[:, t, :], ACT.Sign, bias=MID[:, t:t + 1], scale=-1.0,
                               accum_out=CNT[:, t:t + 1]).then_inc(act_counted, 1)
                    act.wait_ge(mid_ready, b * (4 * EVALS) + (pr + 1) * EVALS)
                    for t in range(16):
                        signs(t, BY_ACT * (EVALS - 1) + t, MID, CNT)
                    for t in range(16):
                        act.wait_ge(found, b * 64 + (16 * pr + t + 1))
                        signs(t, BY_ACT * (EVALS - 1) + 16 + t, THR, SEEN)
                    stage_end(act, b, act_at)
                    for t in range(17):
                        if t < 16:
                            if t >= 2:
                                act.wait_ge(m2_ready, b * (16 * 4) + (16 * pr + t - 1))
                            go(E2[:, t % 2, :], SROW[:, t, :], ACT.Exp).then_inc(e2_ready, 1)
                        if t >= 1:
                            u = t - 1
                            act.wait_ge(x2_made, b * (16 * 4) + (16 * pr + u + 1))
                            if u >= 2:
                                act.wait_ge(pv2_done, b * (16 * 4) + (16 * pr + u - 1))
                            go(PT2[:, u % 2, 0:CH], PS[:, 2 * (u % 2), :], ACT.Copy).then_inc(x2_free_act, 1)
                    act.wait_ge(pv2_done, b * (16 * 4) + (16 * pr + 16))
                    for i in range(2):
                        h = 2 * pr + i
                        last = go(O2[32 * (h % 4):32 * (h % 4) + 32, h // 4, :].rearrange("p (t n) -> p t n", t=2),
                           PS[0:32, 4 + 2 * i:6 + 2 * i, :], ACT.Copy)
                    last.then_inc(o2_taken, 1)
                stage_end(act, b, act_at)

                def group_sd(g, tiles):
                    act.wait_ge(gn_var, b * 5 + (g + 1))
                    go(SDG[:, 0:tiles], VAR[:, 0:tiles], ACT.Sqrt, bias=EPS6).then_inc(gn_sd, 1)

                group_sd(0, 1)
                act.wait_ge(gn_ready, b * 5 + 1)
                go(AO.rearrange("p (t n) -> p t n", t=2), PS[:, 0:2, :], ACT.Identity,
                   bias=SH(0)[:, 0:1], scale=SC(0)[:, 0:1]).then_inc(ao_done, 1)
                go(XHB, X[:, :], ACT.Copy, scale=0.5).then_inc(xh2_made, 1)
                stage_end(act, b, act_at)
                group_sd(1, 3)
                act.wait_ge(gn_ready, b * 5 + 2)
                for g in range(3):
                    conv = PS[:, 2 * g:2 * g + 2, :] if g < 2 else CONV.rearrange("p (t n) -> p t n", t=2)
                    go(Y1[g].rearrange("p (t n) -> p t n", t=2), conv, ACT.Silu,
                       bias=SH(1)[:, g:g + 1], scale=SC(1)[:, g:g + 1])
                stage_end(act, b, act_at)
                group_sd(2, 3)
                act.wait_ge(gn_ready, b * 5 + 3)
                for g in range(3):
                    go(HO[g].rearrange("p (t n) -> p t n", t=2), PS[:, 2 * g:2 * g + 2, :], ACT.Identity,
                       bias=SH(2)[:, g:g + 1], scale=SC(2)[:, g:g + 1]).then_inc(ho_made, 1)
                stage_end(act, b, act_at)
                for j in range(2 * NCH):
                    act.wait_ge(u1_made, b * (2 * NCH) + (j + 1))
                    go(F1[:, j // NCH, chunk(j % NCH)], PS[:, j % 4, :], ACT.Copy).then_inc(u1_copied, 1)
                group_sd(3, 2)
                act.wait_ge(gn_ready, b * 5 + 4)
                for t in range(NCH):
                    for i in range(2):
                        go(F1[:, i, chunk(t)], F1[:, i, chunk(t)], ACT.Gelu, bias=SH(3)[:, i:i + 1],
                           scale=SC(3)[:, i:i + 1]).then_inc(u2_ready, 1)
                for t in range(NCH):
                    act.wait_ge(u2_made, b * NCH + (t + 1))
                    go(F2[:, chunk(t)], PS[:, 4 + t % 2, :], ACT.Copy).then_inc(u2_copied, 1)
                group_sd(4, 1)
                act.wait_ge(gn_ready, b * 5 + 5)
                for t in range(NCH):
                    go(F2[:, chunk(t)], F2[:, chunk(t)], ACT.Identity, bias=SH(4)[:, 0:1],
                       scale=SC(4)[:, 0:1]).then_inc(u3_ready, 1)
                stage_end(act, b, act_at)
                for g in range(NCH + 1):
                    if g < NCH:
                        act.wait_ge(h3_made, b * NCH + (g + 1))
                        if g >= 2:
                            act.wait_ge(c3_made, b * NCH + (g - 1))
                        go(HT[:, g % 2, :], PS[:, g % 2, :], ACT.Copy).then_inc(h3_copied, 1)
                    if g >= 1:
                        i = g - 1
                        act.wait_ge(i3_made, b * NCH + (i + 1))
                        go(HP[:, 8 * i + 1:8 * i + 9, 1:SIDE + 1].rearrange("p r (q c) -> p r q c", q=4),
                           PS[:, 4 + i % 2, :].rearrange("p (q r c) -> p r q c", q=4, r=8), ACT.Copy).then_inc(i3_placed, 1)
                stage_end(act, b, act_at)
                for g in range(NCH):
                    act.wait_ge(d3_made, b * NCH + (g + 1))
                    if g >= 2:
                        act.wait_ge(d3_gated, b * NCH + (g - 1))
                    go(G1[0:64, g % 2, :], PS[0:64, 6 + g % 2, :], ACT.Gelu, bias=w("b_dw", 64)).then_inc(d3_gelu, 1)
                stage_end(act, b, act_at)
            assert act_at[0] == STAGES

        @block.gpsimd
        def _(pool):
            pool.sem_inc(xin_free, 1)
            pool.wait_ge(loaded, 32)
            for i in range(27):
                col = w("he_dw")[:, i:i + 1] if i < 18 else w("w_dw")[:, i - 18:i - 17]
                nc.gpsimd.tensor_scalar(DG[:, i * 128:(i + 1) * 128], k("ident"), col, None, ALU.mult)
            pool.drain()
            pool_at = [0]
            with pool.Fori(0, nb) as b:
                stage_end(pool, b, pool_at)
                stage_end(pool, b, pool_at)
                stage_end(pool, b, pool_at)
                for n in range(4, 10):
                    if n in (4, 8):
                        base = b * (2 * NCH) + (n == 8) * NCH
                        for t in range(NCH):
                            pool.wait_ge(ln_xh, base + (t + 1))
                            pool.sem_inc(wait_passed, 1)
                            nc.gpsimd.tensor_scalar(XLN[:, chunk(t)], XH[:, t % 2, :], w("ln1w" if n == 4 else "ln2w"),
                                                    w("ln1b" if n == 4 else "ln2b"), ALU.mult, ALU.add).then_inc(ln_out, 1)
                    stage_end(pool, b, pool_at)
                for n in range(10, STAGES + 1):
                    if n == STAGES - 1:
                        for g in range(NCH):
                            if g >= 2:
                                pool.wait_ge(h3_made, b * NCH + (g - 1))
                                pool.sem_inc(wait_passed, 1)
                            nc.gpsimd.tensor_copy(
                                XP[:, g % 2, :].rearrange("p (q r c) -> p r q c", q=4, r=8),
                                X[:, chunk(g)].rearrange("p (r q c) -> p r q c", r=8, q=4)).then_inc(xp_made, 1)
                    stage_end(pool, b, pool_at)
            assert pool_at[0] == STAGES

        @block.vector
        def _(dve):
            v = nc.vector
            dve.sem_inc(L0.tile_free, 2)
            dve.sem_inc(L1.tile_free, 2)
            dve.sem_inc(dve_counted, 2)
            v.memset(EPS5, 1e-5)
            v.memset(EPS6, 1e-6)
            v.memset(ONES, 1.0)
            for i in range(8):
                v.memset(IOTA8[:, i:i + 1], float(i))
            dve.drain().then_inc(setup_done, 1)
            dve.wait_ge(loaded, 32)

            def maxima(L, u, at, rows_to, meanwhile=None):
                for t in range(64):
                    dve.wait_ge(L.tile_scored, u * TILES + (t + 1))
                    v.tensor_reduce(MX[:, t // 8, t % 8:t % 8 + 1], PS[:, t % 2, :], AX.X, ALU.max).then_inc(L.tile_free, 1)
                dve.wait_ge(L.tile_free, u * TILES + 66)
                v.tensor_reduce(NEG, MX, AX.X, ALU.max, negate=True).then_inc(L.shift_step, 1)
                dve.wait_ge(L.shift_step, u * 3 + 1)
                v.tensor_copy(N16, NEG).then_inc(L.shift_step, 1)
                dve.wait_ge(L.shift_step, u * 3 + 2)
                v.tensor_copy(NHL[:, :, 0], N16).then_inc(L.shift_step, 1)
                dve.wait_ge(L.shift_step, u * 3 + 3)
                v.tensor_tensor(NHL[:, :, 1], NEG, NHL[:, :, 0], ALU.subtract).then_inc(L.shift_split, 1)
                if meanwhile is not None:
                    meanwhile()
                for i in range(2):
                    dve.wait_ge(L.tile_scored, u * TILES + (65 + i))
                    v.tensor_copy(rows_to(i), PS[at:at + 2, i, :]).then_inc(L.tile_free, 1)

            def l0_maxima(u, col, meanwhile=None):
                maxima(L0, u, 64, lambda i: QB[64:66, bass.ds(col + i * CH, CH)], meanwhile)

            def l1_maxima(u, pair, col, meanwhile=None):
                maxima(L1, u, 96, lambda i: QS[2 * pair + i][96:98, bass.ds(col, CH)], meanwhile)

            def divide(L, taken, divided, sums, totals):
                dve.wait_ge(L.o_free, taken)
                dve.sem_inc(wait_passed, 1)
                v.reciprocal(RCP, totals).then_inc(L.inverted, 1)
                dve.wait_ge(L.inverted, divided + 1)
                dve.sem_inc(wait_passed, 1)
                v.tensor_tensor(sums, sums, RCP, ALU.mult).then_inc(L.divided, 1)
                dve.wait_ge(L.divided, divided + 1)
                dve.sem_inc(wait_passed, 1)

            def l0_divide(c):
                y, z = (m[:, bass.ds(c, 1), :].rearrange("p a n -> p (a n)") for m in (Y0, Z0))
                divide(L0, b * (NCH // 2) + (c + 2), b * (NCH // 2) + c, y, z)

            def l1_divide(t):
                o, z = O1[:, bass.ds(t * CH, CH)], Z1[:, bass.ds(t * CH, CH)]
                divide(L1, b * (2 * NCH) + (t * 2 + 4), b * NCH + t, o, z)

            dve_at = [0]
            with dve.Fori(0, nb) as b:
                for t in range(NCH):
                    for i in range(2):
                        j = 2 * t + i
                        dve.wait_ge(p0_head, b * (2 * NCH) + (j + 1))
                        if i == 0:
                            v.scalar_tensor_tensor(QB[0:64, chunk(t)], PS[0:64, j % 4, :], w("bt2", 64), QA[0:64, chunk(t)],
                                                   ALU.add, ALU.subtract).then_inc(p0_free, 1)
                        else:
                            v.scalar_tensor_tensor(KA[64:128, chunk(t)], PS[64:128, j % 4, :], w("bp2")[64:128, :],
                                                   KA[64:128, chunk(t)], ALU.add, ALU.subtract).then_inc(p0_free, 1)
                v.memset(GT[:, :, IC:128], 1.0)
                v.memset(QB[64:66, :], 0.0)
                v.memset(KB[64:66, :], 1.0)
                for j in range(4):
                    dve.wait_ge(g0_made, b * 4 + (j + 1))
                    v.tensor_copy(GT[:, 8 * j:8 * j + 8, 0:IC], PS[:, 4 + j, :].rearrange("p (j o) -> p j o", o=IC))
                stage_end(dve, b, dve_at)
                u0 = b * (NCH // 2)
                l0_maxima(u0, 0)
                l0_maxima(u0 + 1, 2 * CH)
                with dve.Fori(1, NCH // 2 - 1) as q:
                    l0_maxima(u0 + q + 1, q * (2 * CH) + 2 * CH, lambda: l0_divide(q - 1))
                l0_divide(NCH // 2 - 2)
                stage_end(dve, b, dve_at)
                dve.wait_ge(out_stored, b * 16 + 16)
                l0_divide(NCH // 2 - 1)
                for t in range(NCH):
                    dve.wait_ge(y0_made, b * NCH + (t + 1))
                    v.scalar_tensor_tensor(X[:, chunk(t)], PS[:, t % 2, :], w("bw"), XIN[:, chunk(t)],
                                           ALU.add, ALU.add).then_inc(y0_free, 1)
                stage_end(dve, b, dve_at)

                def layernorm(n):
                    base = b * (2 * NCH) + n * NCH
                    for t in range(NCH):
                        dve.wait_ge(ln_mean, base + (t + 1))
                        v.tensor_tensor(XC[:, chunk(t)], X[:, chunk(t)], PS[:, t % 2, :], ALU.subtract).then_inc(ln_xc, 1)
                    for t in range(-1, NCH):
                        if t in (-1, 3):
                            g = (t + 1) // 4
                            dve.wait_ge(ln_sd, b * 4 + (2 * n + g + 1))
                            v.reciprocal(RS[:, g, :], SD[:, g, :]).then_inc(ln_rs, 1)
                        if t >= 0:
                            dve.wait_ge(ln_spread, base + (t + 1))
                            if t >= 2:
                                dve.wait_ge(ln_out, base + (t - 1))
                            v.tensor_tensor(XH[:, t % 2, :], XC[:, chunk(t)], PS[:, 4 + t % 4, :], ALU.mult).then_inc(ln_xh, 1)

                layernorm(0)
                stage_end(dve, b, dve_at)
                for j in range(2 * H1 * NCH):
                    h, t = j // 2 % H1, j // (2 * H1)
                    at, to = (64, QS) if j % 2 == 0 else (32, KS)
                    dve.wait_ge(p1_head, b * (2 * H1 * NCH) + (j + 1))
                    low = to[h][at:at + 32, chunk(t)]
                    v.tensor_tensor(low, PS[at:at + 32, j % 4, :], low, ALU.subtract).then_inc(p1_free, 1)
                for h in range(H1):
                    v.memset(QS[h][96:98, :], 0.0)
                    v.memset(KS[h][96:98, :], 1.0)
                v.memset(VT[:, :, :, 32:64], 1.0)
                for j in range(NBLK // 4):
                    dve.wait_ge(v1_made, b * (NBLK // 4) + (j + 1))
                    for i in range(4):
                        last = v.tensor_copy(VT[:, 4 * j + i, :, 0:32],
                                             PS[:, 4 + j % 4, i * C:(i + 1) * C].rearrange("p (h o) -> p h o", h=H1))
                    last.then_inc(v1_free, 1)
                stage_end(dve, b, dve_at)
                u1 = b * (2 * NCH)
                l1_maxima(u1, 0, 0)
                l1_maxima(u1 + 1, 1, 0)
                l1_maxima(u1 + 2, 0, CH)
                with dve.Fori(1, NCH - 1) as q:
                    l1_maxima(u1 + q * 2 + 1, 1, q * CH)
                    l1_maxima(u1 + q * 2 + 2, 0, q * CH + CH, lambda: l1_divide(q - 1))
                l1_maxima(u1 + (2 * NCH - 1), 1, N - CH, lambda: l1_divide(NCH - 2))
                stage_end(dve, b, dve_at)
                l1_divide(NCH - 1)
                for t in range(NCH):
                    dve.wait_ge(pr_made, b * NCH + (t + 1))
                    v.scalar_tensor_tensor(X[:, chunk(t)], PS[:, t % 2, :], w("projb"), X[:, chunk(t)],
                                           ALU.add, ALU.add).then_inc(pr_free, 1)
                stage_end(dve, b, dve_at)
                layernorm(1)
                stage_end(dve, b, dve_at)
                for t in range(NCH):
                    dve.wait_ge(f2_made, b * NCH + (t + 1))
                    v.scalar_tensor_tensor(X[:, chunk(t)], PS[:, 4 + t % 2, :], w("fc2b"), X[:, chunk(t)],
                                           ALU.add, ALU.add).then_inc(f2_free, 1)
                stage_end(dve, b, dve_at)
                dve.wait_ge(xh_made, b + 1)
                tt = v.tensor_tensor
                tt(half(E2[:, 0, :]), quarter(XH2, 0, 0), quarter(XH2, 1, 0), ALU.add)
                tt(half(E2[:, 1, :]), quarter(XH2, 0, 1), quarter(XH2, 1, 1), ALU.add)
                dve.drain()
                tt(LL, E2[:, 0, :], E2[:, 1, :], ALU.add)
                stage_end(dve, b, dve_at)
                v.memset(VT2[:, :, :, D2:SLOT], 0.0)
                v.memset(VT2[:, :, :, SLOT:64], 1.0)
                dve.wait_ge(v2_made, b + 1)
                for j in range(8):
                    v.tensor_copy(VT2[:, j, :, 0:D2],
                                  PS[:, 6 + j // 4, (j % 4) * C:(j % 4 + 1) * C].rearrange("p (h o) -> p h o", h=H2))
                for j in range(4):
                    dve.wait_ge(n2_sd, b * 4 + (j + 1))
                    v.tensor_scalar_max(SD2[:, chunk(j)], SD2[:, chunk(j)], 1e-12)
                    dve.drain()
                    v.reciprocal(SQ2[:, chunk(j)], SD2[:, chunk(j)])
                    dve.drain()
                    tt(QKN[:, chunk(j)], PS[:, j, :], SQ2[:, chunk(j)], ALU.mult)
                stage_end(dve, b, dve_at)
                for pr in range(H2 // 2):
                    for j in range(8):
                        i, z, t = j // 4, j // 2 % 2, j % 2
                        at = (64, 32)[z]
                        dve.wait_ge(s2_head, b * (8 * 4) + (8 * pr + j + 1))
                        low = (QS2, KS2)[z][i][at:at + 32, chunk(t)]
                        tt(low, PS[at:at + 32, j % 4, :], low, ALU.subtract).then_inc(s2_free, 1)
                    for t in range(1, 16, 2):
                        dve.wait_ge(t2_made, b * (16 * 4) + (16 * pr + t + 1))
                        v.tensor_scalar(SROW[:, t, :].rearrange("p (m n) -> p m n", m=2), PS[:, 6:8, :],
                                        float(D2) ** -0.5, None, ALU.mult, ALU.add,
                                        accum_out=CNT[:, t:t + 1]).then_inc(t2_free_dve, 1)
                    v.memset(LOW, LOWEST)
                    v.memset(HIGH, -LOWEST)
                    v.memset(DLOW, N2 - KEEP + AIM)
                    v.memset(DHIGH, AIM - KEEP)
                    stage_end(dve, b, dve_at)
                    v.tensor_scalar(MID, CNT, 1.0 / N2, None, ALU.mult).then_inc(mid_ready, 1)
                    dve.drain()
                    counted = b * (4 * BY_DVE * (EVALS - 1)) + pr * (BY_DVE * (EVALS - 1))

                    def count(n):
                        for t in range(BY_DVE):
                            dve.wait_ge(dve_counted, counted + n * BY_DVE + (t + 1))
                            v.tensor_scalar(JUNK[t % 2], SROW[:, t, :], MID[:, t:t + 1], None, ALU.is_ge, ALU.add,
                                            accum_out=CNT[:, t:t + 1]).then_inc(dve_counted, 1)
                        dve.drain()
                        v.tensor_scalar(DEV[:, 0:BY_DVE], CNT[:, 0:BY_DVE], AIM - KEEP, None, ALU.add)
                        dve.wait_ge(act_counted, b * (4 * ACT_PASSES) + n * BY_ACT + (pr * ACT_PASSES + BY_ACT + 2))
                        v.tensor_scalar(DEV[:, BY_DVE:16], CNT[:, BY_DVE:16], -0.5, AIM, ALU.mult, ALU.add)
                        dve.drain()

                    def bracket():
                        v.tensor_scalar(POS, DEV, 0.0, None, ALU.is_ge)
                        v.tensor_scalar(BELOW, DEV, 0.0, None, ALU.is_lt)
                        tt(OUTW, DEV, DEV, ALU.mult)
                        dve.drain()
                        v.tensor_scalar(OUTW, OUTW, 3.6 ** 2, None, ALU.is_gt)
                        for mask, end, dev in ((POS, LOW, DLOW), (BELOW, HIGH, DHIGH)):
                            v.copy_predicated(end, mask.bitcast(mybir.dt.int32), MID)
                            v.copy_predicated(dev, mask.bitcast(mybir.dt.int32), DEV)
                        dve.drain()

                    count(0)
                    bracket()
                    v.tensor_scalar(SPAN, POS, 6.0, -3.0, ALU.mult, ALU.add)
                    dve.drain()
                    tt(SPAN, SPAN, DEV, ALU.add)
                    dve.drain()
                    v.scalar_tensor_tensor(NEXT, SPAN, SLOPE, MID, ALU.mult, ALU.add)
                    dve.drain()
                    v.copy_predicated(MID, OUTW.bitcast(mybir.dt.int32), NEXT).then_inc(mid_ready, 1)
                    dve.drain()
                    with dve.Fori(1, EVALS - 1) as n:
                        count(n)
                        bracket()
                        tt(RDEV, DLOW, DHIGH, ALU.subtract)
                        tt(SPAN, HIGH, LOW, ALU.subtract)
                        dve.drain()
                        v.reciprocal(RDEV, RDEV)
                        tt(SPAN, SPAN, DLOW, ALU.mult)
                        dve.drain()
                        tt(SPAN, SPAN, RDEV, ALU.mult)
                        dve.drain()
                        tt(NEXT, SPAN, LOW, ALU.add)
                        dve.drain()
                        v.copy_predicated(MID, OUTW.bitcast(mybir.dt.int32), NEXT).then_inc(mid_ready, 1)
                        dve.drain()

                    def pick(t):
                        dve.wait_ge(best_made, b * 64 + (16 * pr + t + 1))
                        v.scalar_tensor_tensor(M8J[:, t, :], IOTA8, IDX[:, t:t + 1], BEST[:, t, :],
                                               ALU.is_equal, ALU.mult, accum_out=THR[:, t:t + 1]).then_inc(found, 1)

                    for t in range(17):
                        if t < 16:
                            if t >= 2:
                                dve.wait_ge(best_made, b * 64 + (16 * pr + t - 1))
                            v.scalar_tensor_tensor(MK[t % 2], SROW[:, t, :], MID[:, t:t + 1], SROW[:, t, :],
                                                   ALU.is_ge, ALU.subtract, reverse1=True).then_inc(masked, 1)
                        if t >= 1:
                            dve.wait_ge(masked, b * 64 + (16 * pr + t))
                            dve.sem_inc(wait_passed, 1)
                            v.max(BEST[:, t - 1, :], MK[(t - 1) % 2]).then_inc(best_made, 1)
                        if t == 8:
                            dve.wait_ge(act_counted, b * (4 * ACT_PASSES) + ((pr + 1) * ACT_PASSES - 16 + 2))
                            v.tensor_scalar(DEV, CNT, -0.5, AIM, ALU.mult, ALU.add)
                            dve.drain()
                            v.tensor_scalar(IDX, DEV, -1.0, 3.5 - 0.25, ALU.mult, ALU.add)
                            dve.drain()
                            v.tensor_scalar(IDX, IDX, 1.5 * 2.0 ** 23, -1.5 * 2.0 ** 23, ALU.add, ALU.add)
                            dve.drain()
                            for u in range(7):
                                pick(u)
                        if t > 8:
                            pick(t - 2)
                    pick(15)
                    dve.wait_ge(act_counted, b * (4 * ACT_PASSES) + ((pr + 1) * ACT_PASSES + 2))
                    v.tensor_scalar(SEEN, SEEN, 1.0, None, ALU.subtract)
                    v.tensor_scalar(IDX, IDX, 3.5, None, ALU.subtract)
                    dve.drain()
                    tt(SEEN, SEEN, SEEN, ALU.mult)
                    tt(IDX, IDX, IDX, ALU.mult)
                    dve.drain()
                    v.tensor_scalar(SEEN, SEEN, 1.5, None, ALU.is_gt)
                    v.tensor_scalar(IDX, IDX, 3.6 ** 2, None, ALU.is_gt)
                    dve.drain()
                    tt(BAD, SEEN, IDX, ALU.add)
                    dve.drain()
                    v.tensor_reduce(BADSUM, BAD, AX.X, ALU.add).then_inc(bad_summed, 1)
                    dve.wait_ge(bad_total, b * 4 + (pr + 1))
                    v.tensor_scalar(FLAG, PS[0:1, 7, 0:1], 0.0, None, ALU.is_gt)
                    dve.drain()
                    again = dve.value_load(FLAG, min_val=0, max_val=1)
                    with dve.If(again > 0):
                        v.memset(LOW, LOWEST)
                        v.memset(STEP, RANGE / 2)
                        v.memset(MID, LOWEST + RANGE / 2)
                        with dve.Fori(0, BISECTIONS) as n:
                            for t in range(16):
                                dve.drain()
                                v.tensor_scalar(JUNKF, SROW[:, t, :], MID[:, t:t + 1], None, ALU.is_ge, ALU.add,
                                                accum_out=CNT[:, t:t + 1])
                            dve.drain()
                            v.tensor_scalar(CNT, CNT, KEEP - 0.5, None, ALU.is_ge)
                            dve.drain()
                            tt(CNT, CNT, STEP, ALU.mult)
                            dve.drain()
                            tt(LOW, LOW, CNT, ALU.add)
                            v.tensor_scalar(STEP, STEP, 0.5, None, ALU.mult)
                            dve.drain()
                            tt(MID, LOW, STEP, ALU.add)
                            dve.drain()
                        v.tensor_copy(THR, LOW)
                        dve.drain()
                    stage_end(dve, b, dve_at)
                    for t in range(17):
                        if t < 16:
                            dve.wait_ge(e2_ready, b * (16 * 4) + (16 * pr + t + 1))
                            v.scalar_tensor_tensor(SROW[:, t, :], SROW[:, t, :], THR[:, t:t + 1], E2[:, t % 2, :],
                                                   ALU.is_ge, ALU.mult).then_inc(m2_ready, 1)
                        if t >= 1:
                            u = t - 1
                            dve.wait_ge(x2_made, b * (16 * 4) + (16 * pr + u + 1))
                            if u >= 2:
                                dve.wait_ge(pv2_done, b * (16 * 4) + (16 * pr + u - 1))
                            v.tensor_copy(PT2[:, u % 2, CH:2 * CH], PS[:, 2 * (u % 2) + 1, :]).then_inc(x2_free_dve, 1)
                    dve.wait_ge(pv2_done, b * (16 * 4) + (16 * pr + 16))
                    for i in range(2):
                        h = 2 * pr + i
                        last = v.tensor_copy(Z2[32 * (h % 4):32 * (h % 4) + 32, h // 4, :].rearrange("p (t n) -> p t n", t=2),
                                             PS[32:64, 4 + 2 * i:6 + 2 * i, :])
                    last.then_inc(o2_taken, 1)
                stage_end(dve, b, dve_at)

                def group_norm(g, tiles, stats, gamma, beta, factor=None):
                    dve.drain()
                    for i in range(tiles):
                        v.bn_aggr(MV[:, i, :], stats(i))
                    dve.drain()
                    v.tensor_copy(EX[:, 0:tiles, 0], MV[:, 0:tiles, 0])
                    tt(MSQ[:, 0:tiles], MV[:, 0:tiles, 0], MV[:, 0:tiles, 0], ALU.mult)
                    dve.drain()
                    tt(EX[:, 0:tiles, 1], MSQ[:, 0:tiles], MV[:, 0:tiles, 1], ALU.add).then_inc(gn_stats, 1)
                    dve.wait_ge(gn_sums, b * 5 + (g + 1))
                    v.tensor_copy(GM[:, 0:tiles, :], PS[:, 7, 0:2 * tiles].rearrange("p (t two) -> p t two", two=2))
                    dve.drain()
                    tt(MSQ[:, 0:tiles], GM[:, 0:tiles, 0], GM[:, 0:tiles, 0], ALU.mult)
                    dve.drain()
                    tt(VAR[:, 0:tiles], GM[:, 0:tiles, 1], MSQ[:, 0:tiles], ALU.subtract).then_inc(gn_var, 1)
                    dve.wait_ge(gn_sd, b * 5 + (g + 1))
                    v.reciprocal(RG[:, 0:tiles], SDG[:, 0:tiles])
                    dve.drain()
                    tt(SC(g)[:, 0:tiles], RG[:, 0:tiles], gamma, ALU.mult)
                    dve.drain()
                    tt(MSQ[:, 0:tiles], GM[:, 0:tiles, 0], SC(g)[:, 0:tiles], ALU.mult)
                    dve.drain()
                    tt(SH(g)[:, 0:tiles], beta, MSQ[:, 0:tiles], ALU.subtract)
                    dve.drain()
                    if factor is not None:
                        v.tensor_scalar(SC(g)[:, 0:tiles], SC(g)[:, 0:tiles], factor, None, ALU.mult)
                        v.tensor_scalar(SH(g)[:, 0:tiles], SH(g)[:, 0:tiles], factor, None, ALU.mult)
                    dve.drain().then_inc(gn_ready, 1)

                def stat(i, n):
                    return BST[:, i * 6 * n:(i + 1) * 6 * n].rearrange("p (c six) -> p c six", six=6)

                for g in range(2):
                    v.reciprocal(RC2[:, g, :], Z2[:, g, :])
                dve.drain()
                for g in range(2):
                    tt(O2[:, g, :], O2[:, g, :], RC2[:, g, :], ALU.mult)
                dve.drain().then_inc(o2_divided, 1)
                for t in range(2):
                    dve.wait_ge(o2_made, b * 2 + (t + 1))
                    v.bn_stats(BST[:, 6 * t:6 * t + 6], PS[:, t, :])
                dve.drain().then_inc(xin_free, 1)
                group_norm(0, 1, lambda i: stat(i, 2), w("agn_g"), w("agn_b"))
                dve.wait_ge(ao_done, b + 1)
                tt(LL, LL, AO, ALU.add)
                for g in range(3):
                    v.memset(PAD[g], 0.0)
                dve.drain()
                dve.wait_ge(xh2_made, b + 1)
                q00, q10, q01, q11 = quarter(XHB, 0, 0), quarter(XHB, 1, 0), quarter(XHB, 0, 1), quarter(XHB, 1, 1)
                tt(half(TMPB[0]), q00, q10, ALU.add)
                tt(half(TMPB[1]), q01, q11, ALU.add)
                tt(half(TMPB[2]), q10, q00, ALU.subtract)
                tt(half(TMPB[3]), q11, q01, ALU.subtract)
                dve.drain()
                tt(inner(0), half(TMPB[1]), half(TMPB[0]), ALU.subtract)
                tt(inner(1), half(TMPB[2]), half(TMPB[3]), ALU.add)
                tt(inner(2), half(TMPB[3]), half(TMPB[2]), ALU.subtract)
                stage_end(dve, b, dve_at)
                for tap in range(9):
                    src = PAD[2].rearrange("p (y x) -> p y x", x=S2 + 2)[:, tap // 3:tap // 3 + S2, tap % 3:tap % 3 + S2]
                    weight = w("he_dw")[:, 18 + tap:19 + tap]
                    if tap == 0:
                        v.tensor_scalar(half(CONV), src, weight, None, ALU.mult)
                    else:
                        v.scalar_tensor_tensor(half(CONV), src, weight, half(CONV), ALU.mult, ALU.add)
                    dve.drain()
                for t in range(2):
                    v.bn_stats(BST[:, 6 * (4 + t):6 * (4 + t) + 6], CONV[:, chunk(t)])
                for j in range(4):
                    dve.wait_ge(dw2_made, b * 4 + (j + 1))
                    v.bn_stats(BST[:, 6 * j:6 * j + 6], PS[:, j, :])
                group_norm(1, 3, lambda i: stat(i, 2), w("he1_g"), w("he1_b"))
                stage_end(dve, b, dve_at)
                for j in range(6):
                    dve.wait_ge(pw2_made, b * 6 + (j + 1))
                    v.bn_stats(BST[:, 6 * j:6 * j + 6], PS[:, j, :])
                group_norm(2, 3, lambda i: stat(i, 2), w("he2_g"), w("he2_b"), w("alpha"))
                for g in range(3):
                    dve.wait_ge(ho_made, b * 3 + (g + 1))
                    tt(half(HO[g]), half(HO[g]), inner(g), ALU.add)
                dve.drain()
                tt(TMP[0], LL, HO[2], ALU.add)
                tt(TMP[1], LL, HO[2], ALU.subtract)
                tt(TMP[2], HO[0], HO[1], ALU.add)
                tt(TMP[3], HO[0], HO[1], ALU.subtract)
                dve.drain()
                q = [area(56 + 4 * i, 4) for i in range(4)]
                tt(q[0], TMP[0], TMP[2], ALU.subtract)
                tt(q[1], TMP[1], TMP[3], ALU.subtract)
                tt(q[2], TMP[1], TMP[3], ALU.add)
                tt(q[3], TMP[0], TMP[2], ALU.add)
                dve.drain()
                for i, (r, c) in enumerate(((0, 0), (1, 0), (0, 1), (1, 1))):
                    v.scalar_tensor_tensor(quarter(X, r, c), half(q[i]), 0.1, quarter(X, r, c), ALU.mult, ALU.add)
                stage_end(dve, b, dve_at)
                for j in range(2 * NCH):
                    dve.wait_ge(u1_copied, b * (2 * NCH) + (j + 1))
                    v.bn_stats(BST[:, 6 * j:6 * j + 6], F1[:, j // NCH, chunk(j % NCH)])
                group_norm(3, 2, lambda i: stat(i, 8), w("f1_g"), w("f1_b"))
                for t in range(NCH):
                    dve.wait_ge(u2_copied, b * NCH + (t + 1))
                    v.bn_stats(BST[:, 6 * t:6 * t + 6], F2[:, chunk(t)])
                group_norm(4, 1, lambda i: stat(i, 8), w("f2_g"), w("f2_b"), 0.1)
                for t in range(NCH):
                    dve.wait_ge(u3_ready, b * NCH + (t + 1))
                    tt(X[:, chunk(t)], X[:, chunk(t)], F2[:, chunk(t)], ALU.add)
                stage_end(dve, b, dve_at)
                v.memset(HP, 0.0)
                dve.wait_ge(fl_made, b + 1)
                v.tensor_copy(FILT, PS[:, 6, 0:128]).then_inc(filt_placed, 1)
                dve.wait_ge(filt_placed, b + 1)
                for g in range(NCH):
                    dve.wait_ge(c3_made, b * NCH + (g + 1))
                    if g >= 2:
                        dve.wait_ge(i3_made, b * NCH + (g - 1))
                    tt(GC[:, g % 2, :].rearrange("p (q c) -> p q c", q=4), PS[:, 2 + g % 2, :].rearrange("p (q c) -> p q c", q=4),
                       FILT.rearrange("p (one c) -> p one c", one=1).to_broadcast([128, 4, 128]), ALU.mult).then_inc(c3_scaled, 1)
                stage_end(dve, b, dve_at)
                for g in range(NCH + 1):
                    if g < NCH:
                        dve.wait_ge(d3_gelu, b * NCH + (g + 1))
                        if g >= 2:
                            dve.wait_ge(o3_made, b * NCH + (g - 1))
                        v.scalar_tensor_tensor(G2[0:64, g % 2, :], PS[64:128, 6 + g % 2, :], w("b_dw2", 64),
                                               G1[0:64, g % 2, :], ALU.add, ALU.mult).then_inc(d3_gated, 1)
                    if g >= 1:
                        i = g - 1
                        dve.wait_ge(o3_made, b * NCH + (i + 1))
                        v.scalar_tensor_tensor(X[:, chunk(i)], PS[:, i % 2, :], w("b_out"), X[:, chunk(i)],
                                               ALU.add, ALU.add).then_inc(o3_free, 1)
                stage_end(dve, b, dve_at)
            assert dve_at[0] == STAGES


def _packed_constants():
    K = np.zeros((128, C_TOTAL), np.float32)

    def put(name, a):
        at, n = CCOLS[name]
        K[0:a.shape[0], at:at + n] = a
    i = np.arange(128)
    put("ident", np.eye(128))
    put("mean", np.full((128, 128), 1 / 128))
    ch = np.arange(384)
    g12 = (ch[:, None] // 12 == ch[None, :] // 12) / 12.0
    put("g12", g12.reshape(3, 128, 384).transpose(1, 0, 2).reshape(128, 9 * 128))
    put("g8", (i[:, None] // 8 == i[None, :] // 8) / 8.0)
    put("g4", (i[:, None] // 4 == i[None, :] // 4) / 4.0)
    put("bd16", (i[:, None] // D2 == i[None, :] // D2) * 1.0)
    sel = np.zeros((128, H2, 96))
    for h in range(H2):
        for d in range(D2):
            for s in range(3):
                sel[h * D2 + d, h, s * SLOT + d] = 1
    put("sel", sel.reshape(128, H2 * 96))
    r, c = np.meshgrid(np.arange(8), np.arange(8), indexing="ij")
    basis, scales = [], []
    for v in range(5):
        for u in range(8):
            if v in (0, 4) and u > 4:
                continue
            a = 2 * np.pi * (u * r + v * c) / 8
            f = np.zeros((8, 5))
            if v in (0, 4):
                f[u, v] += 0.5
                f[(8 - u) % 8, v] += 0.5
            else:
                f[u, v] = 1
            if v in (0, 4) and u in (0, 4):
                basis.append(np.cos(a) / 8)
                scales.append(f)
            else:
                basis += [np.cos(a) * np.sqrt(2) / 8, np.sin(a) * np.sqrt(2) / 8]
                scales += [f, f]
    dft = np.zeros((8, 2, 8, 2, 64))
    for p in range(2):
        dft[:, p, :, p, :] = np.stack(basis, -1)
    dft = dft.reshape(128, 128)
    put("dft", dft)
    put("idft", dft.T)
    put("msel", np.tile(np.stack(scales).reshape(64, 40).T, (1, 2)))
    return K


def kernel(**inputs):
    import concourse.bacc as bacc
    from concourse.bass_utils import run_bass_kernel_spmd

    a = {n: np.ascontiguousarray(v) for n, v in inputs.items()}
    Wp = np.zeros((128, W_TOTAL), np.float32)

    def put(name, v):
        at, n = WCOLS[name]
        v = v.reshape(-1, n)
        Wp[0:v.shape[0], at:at + n] = v

    def tiles(v):
        return v.reshape(-1, 128, v.shape[1]).transpose(1, 0, 2).reshape(128, -1)

    def cols(v):
        return v.reshape(-1, 128).T

    put("wt2", np.tile(a["L0_conv_Wt"].T, (1, 2)))
    put("wp2", np.tile(a["L0_conv_Wp"].T, (1, 2)))
    put("wg", a["L0_conv_Wg"].T)
    put("ww", np.tile(a["L0_conv_Ww"].T, (2, 1)))
    put("bt2", np.tile(a["L0_conv_bt"], 2)[:, None])
    put("bp2", np.tile(a["L0_conv_bp"], 2)[:, None])
    put("bg", a["L0_conv_bg"][None])
    put("bw", a["L0_conv_bw"][:, None])
    put("ln1w", a["L1_conv_ln1_w"][:, None])
    put("ln1b", a["L1_conv_ln1_b"][:, None])
    qkv = a["L1_conv_qkv_w"].reshape(3, H1, D1, C)
    for name, m in (("wq", 0), ("wk", 1)):
        put(name, np.tile(qkv[m].transpose(2, 0, 1)[:, :, None, :], (1, 1, 3, 1)).reshape(C, H1 * 96))
    put("wv", qkv[2].reshape(C, C).T)
    put("proj", a["L1_conv_proj_w"].T)
    put("projb", a["L1_conv_proj_b"][:, None])
    put("ln2w", a["L1_conv_ln2_w"][:, None])
    put("ln2b", a["L1_conv_ln2_b"][:, None])
    put("fc1", a["L1_conv_fc1_w"].T)
    put("fc1b", cols(a["L1_conv_fc1_b"]))
    put("fc2", tiles(a["L1_conv_fc2_w"].T))
    put("fc2b", a["L1_conv_fc2_b"][:, None])
    put("q2", a["L2_conv_qkv_w"].T)
    p2 = np.zeros((2, 4, SLOT, C), np.float32)
    p2[:, :, 0:D2, :] = a["L2_conv_proj_w"].T.reshape(2, 4, D2, C)
    put("proj2", tiles(p2.reshape(256, C)))
    put("agn_g", a["L2_conv_attn_gn_g"][:, None])
    put("agn_b", a["L2_conv_attn_gn_b"][:, None])
    put("he_dw", a["L2_conv_he_dw_w"].reshape(3, 128, 9).transpose(1, 0, 2).reshape(128, 27))
    for n, v in (("he1", "he_gn1"), ("he2", "he_gn2"), ("f1", "ffn_gn1"), ("f2", "ffn_gn2")):
        put(n + "_g", cols(a[f"L2_conv_{v}_g"]))
        put(n + "_b", cols(a[f"L2_conv_{v}_b"]))
    put("he_pw", tiles(a["L2_conv_he_pw_w"].T))
    put("alpha", np.broadcast_to(a["L2_conv_alpha"], (128, 1)))
    put("f1", a["L2_conv_ffn_w1"].T)
    put("f2", tiles(a["L2_conv_ffn_w2"].T))
    put("w_in", a["L3_conv_w_in"].T)
    put("b_in", a["L3_conv_b_in"][None])
    put("w_dw", a["L3_conv_w_dw"].reshape(128, 9))
    put("b_dw", a["L3_conv_b_dw"][:, None])
    put("b_dw2", a["L3_conv_b_dw"][64:, None])
    put("filt", a["L3_conv_fft_filter"].reshape(128, 40).T)
    put("w_out", a["L3_conv_w_out"].T)
    put("b_out", a["L3_conv_b_out"][:, None])

    nc = bacc.Bacc("TRN2", target_bir_lowering=False, num_devices=1)
    arrays = {"x_dram": a["x"].reshape(B, C, N), "weights_dram": Wp, "consts_dram": _packed_constants()}
    aps = [nc.dram_tensor(n, v.shape, FP32, kind="ExternalInput").ap() for n, v in arrays.items()]
    out = nc.dram_tensor("out_dram", (B, C, N), FP32, kind="ExternalOutput").ap()
    build(nc, *aps, out)
    r = run_bass_kernel_spmd(nc, [arrays], core_ids=[0])
    return r.results[0]["out_dram"].reshape(B, C, SIDE, SIDE)
```
